# Optimizing a Trainium2 kernel written in Bass

```python
import numpy as np
import jax
import jax.numpy as jnp

def _softmax(x, axis=-1):
    return jax.nn.softmax(x, axis=axis)

def _gelu(x):
    return jax.nn.gelu(x, approximate=True)

def _silu(x):
    return jax.nn.silu(x)

def _sigmoid(x):
    return jax.nn.sigmoid(x)

def _layernorm(x, axis=-1, eps=1e-05):
    m = jnp.mean(x, axis=axis, keepdims=True)
    v = jnp.var(x, axis=axis, keepdims=True)
    return (x - m) / jnp.sqrt(v + eps)

def _scatter_add(tgt, idx, src, axis=0):
    return tgt.at[idx].add(src)

def _segment_sum(src, seg, n):
    return jax.ops.segment_sum(src, seg, n)
kernel_name = 'mk_recurrent_d2_jaxref_r8_0e0e1d'

def setup_inputs(seed: int=0):
    np.random.seed(seed)
    _w = jnp.asarray

    def _L0_attn_setup():
        import jax, jax.numpy as jnp
        import numpy as np
        B, S, D_IN = (4, 256, 128)
        D_Q = D_K = D_V = 128
        key = jax.random.key(seed)
        ks = jax.random.split(key, 6)
        s = lambda d: 1.0 / np.sqrt(d)
        return {'x': jax.random.normal(ks[0], (B, S, D_IN), dtype=jnp.float32), 'Wk': jax.random.normal(ks[1], (D_K, D_IN), dtype=jnp.float32) * s(D_IN), 'Wq': jax.random.normal(ks[2], (D_Q, D_IN), dtype=jnp.float32) * s(D_IN), 'Wv': jax.random.normal(ks[3], (D_V, D_IN), dtype=jnp.float32) * s(D_IN), 'Wa': jax.random.normal(ks[4], (D_Q, D_K), dtype=jnp.float32) * s(D_K), 'Wb': jax.random.normal(ks[5], (D_V, D_V), dtype=jnp.float32) * s(D_V)}
    _L0_attn_in = _L0_attn_setup()

    def _L0_ffn_setup():
        import jax, jax.numpy as jnp
        import numpy as np
        D_IN, D_HID = (128, 512)

        def _ternary(key, shape):
            return jax.random.randint(key, shape, -1, 2).astype(jnp.float32)

        def _tlin(x, w, s):
            return jnp.einsum('bsi,oi->bso', x, w) * s
        key = jax.random.key(seed)
        ks = jax.random.split(key, 12)
        inv = lambda fan: 1.0 / np.sqrt(fan).astype(np.float32)
        return {'x': jax.random.normal(ks[0], (4, 256, D_IN), dtype=jnp.float32), 'w1_w': _ternary(ks[1], (D_HID, D_IN)), 'w1_s': jax.random.uniform(ks[2], (D_HID,), dtype=jnp.float32) * inv(D_IN), 'w2_w': _ternary(ks[3], (D_HID, D_IN)), 'w2_s': jax.random.uniform(ks[4], (D_HID,), dtype=jnp.float32) * inv(D_IN), 'h1_w': _ternary(ks[5], (D_HID, D_HID)), 'h1_s': jax.random.uniform(ks[6], (D_HID,), dtype=jnp.float32) * inv(D_HID), 'h2_w': _ternary(ks[7], (D_HID, D_HID)), 'h2_s': jax.random.uniform(ks[8], (D_HID,), dtype=jnp.float32) * inv(D_HID), 'w3_w': _ternary(ks[9], (D_IN, D_HID)), 'w3_s': jax.random.uniform(ks[10], (D_IN,), dtype=jnp.float32) * inv(D_HID)}
    _L0_ffn_in = _L0_ffn_setup()

    def _L1_attn_setup():
        import jax, jax.numpy as jnp
        import numpy as np
        HIDDEN, HEADS, HDIM = (128, 8, 64)
        B, S = (4, 1024)
        LN_EPS = 1e-06
        key = jax.random.key(seed)
        ks = jax.random.split(key, 12)
        inner = HEADS * HDIM
        sd = HIDDEN ** (-0.5)
        return {'x': jax.random.normal(ks[0], (B, S, HIDDEN), jnp.float32), 'Wq': jax.random.normal(ks[1], (HIDDEN, inner), jnp.float32) * sd, 'bq': jnp.zeros((inner,), jnp.float32), 'Wk': jax.random.normal(ks[2], (HIDDEN, inner), jnp.float32) * sd, 'bk': jnp.zeros((inner,), jnp.float32), 'Wv': jax.random.normal(ks[3], (HIDDEN, inner), jnp.float32) * sd, 'bv': jnp.zeros((inner,), jnp.float32), 'Wo': jax.random.normal(ks[4], (inner, HIDDEN), jnp.float32) * inner ** (-0.5), 'bo': jnp.zeros((HIDDEN,), jnp.float32), 'alpha': jnp.ones((HEADS, HDIM), jnp.float32), 'aug_param': jax.random.normal(ks[5], (1, HEADS, HDIM), jnp.float32), 'ln_scale': jnp.ones((HIDDEN,), jnp.float32), 'ln_bias': jnp.zeros((HIDDEN,), jnp.float32)}
    _L1_attn_in = _L1_attn_setup()

    def _L1_ffn_setup():
        import jax, jax.numpy as jnp
        import numpy as np
        NUM_HEADS = 16
        TOP_K = 2
        key = jax.random.key(seed)
        ks = jax.random.split(key, 5)
        B, S, D, E = (4, 256, 128, 8)
        scale = 0.02
        return {'x': jax.random.normal(ks[0], (B, S, D), dtype=jnp.float32), 'W_qkv': jax.random.normal(ks[1], (D, 3 * D), dtype=jnp.float32) * scale, 'b_qkv': jnp.zeros((3 * D,), dtype=jnp.float32), 'W_gate': jax.random.normal(ks[2], (D, E), dtype=jnp.float32) * scale, 'b_gate': jnp.zeros((E,), dtype=jnp.float32), 'W_experts': jax.random.normal(ks[3], (E, D, D), dtype=jnp.float32) * scale, 'b_experts': jnp.zeros((E, D), dtype=jnp.float32)}
    _L1_ffn_in = _L1_ffn_setup()
    _d = {'L0_attn_x': _L0_attn_in['x'], 'L0_attn_Wk': _L0_attn_in['Wk'], 'L0_attn_Wq': _L0_attn_in['Wq'], 'L0_attn_Wv': _L0_attn_in['Wv'], 'L0_attn_Wa': _L0_attn_in['Wa'], 'L0_attn_Wb': _L0_attn_in['Wb'], 'L0_ffn_w1_w': _L0_ffn_in['w1_w'], 'L0_ffn_w1_s': _L0_ffn_in['w1_s'], 'L0_ffn_w2_w': _L0_ffn_in['w2_w'], 'L0_ffn_w2_s': _L0_ffn_in['w2_s'], 'L0_ffn_h1_w': _L0_ffn_in['h1_w'], 'L0_ffn_h1_s': _L0_ffn_in['h1_s'], 'L0_ffn_h2_w': _L0_ffn_in['h2_w'], 'L0_ffn_h2_s': _L0_ffn_in['h2_s'], 'L0_ffn_w3_w': _L0_ffn_in['w3_w'], 'L0_ffn_w3_s': _L0_ffn_in['w3_s'], 'L1_attn_Wq': _L1_attn_in['Wq'], 'L1_attn_bq': _L1_attn_in['bq'], 'L1_attn_Wk': _L1_attn_in['Wk'], 'L1_attn_bk': _L1_attn_in['bk'], 'L1_attn_Wv': _L1_attn_in['Wv'], 'L1_attn_bv': _L1_attn_in['bv'], 'L1_attn_Wo': _L1_attn_in['Wo'], 'L1_attn_bo': _L1_attn_in['bo'], 'L1_attn_alpha': _L1_attn_in['alpha'], 'L1_attn_aug_param': _L1_attn_in['aug_param'], 'L1_attn_ln_scale': _L1_attn_in['ln_scale'], 'L1_attn_ln_bias': _L1_attn_in['ln_bias'], 'L1_ffn_W_qkv': _L1_ffn_in['W_qkv'], 'L1_ffn_b_qkv': _L1_ffn_in['b_qkv'], 'L1_ffn_W_gate': _L1_ffn_in['W_gate'], 'L1_ffn_b_gate': _L1_ffn_in['b_gate'], 'L1_ffn_W_experts': _L1_ffn_in['W_experts'], 'L1_ffn_b_experts': _L1_ffn_in['b_experts']}
    _x0 = _d['L0_attn_x']
    _d['L0_attn_x'] = jax.random.normal(jax.random.fold_in(jax.random.key(seed), 1), (4, 1024, 128), dtype=_x0.dtype)
    del _x0
    return _d

def reference(L0_attn_x, L0_attn_Wk, L0_attn_Wq, L0_attn_Wv, L0_attn_Wa, L0_attn_Wb, L0_ffn_w1_w, L0_ffn_w1_s, L0_ffn_w2_w, L0_ffn_w2_s, L0_ffn_h1_w, L0_ffn_h1_s, L0_ffn_h2_w, L0_ffn_h2_s, L0_ffn_w3_w, L0_ffn_w3_s, L1_attn_Wq, L1_attn_bq, L1_attn_Wk, L1_attn_bk, L1_attn_Wv, L1_attn_bv, L1_attn_Wo, L1_attn_bo, L1_attn_alpha, L1_attn_aug_param, L1_attn_ln_scale, L1_attn_ln_bias, L1_ffn_W_qkv, L1_ffn_b_qkv, L1_ffn_W_gate, L1_ffn_b_gate, L1_ffn_W_experts, L1_ffn_b_experts):

    def _L0_attn_ref(x, Wk, Wq, Wv, Wa, Wb):
        import jax, jax.numpy as jnp
        import numpy as np
        B, S, D_IN = (4, 256, 128)
        D_Q = D_K = D_V = 128
        k = jnp.einsum('bsd,kd->bsk', x, Wk)
        q = jnp.einsum('bsd,qd->bsq', x, Wq)
        v = jnp.einsum('bsd,vd->bsv', x, Wv)
        ak = jnp.einsum('bsk,qk->bsq', k, Wa)
        e = jnp.einsum('biq,bjq->bij', q, ak)
        alpha = jax.nn.softmax(e, axis=-1)
        u = jnp.einsum('bsv,wv->bsw', v, Wb)
        out = jnp.einsum('bij,bjv->biv', alpha, u)
        return out

    def _L0_ffn_ref(x, w1_w, w1_s, w2_w, w2_s, h1_w, h1_s, h2_w, h2_s, w3_w, w3_s):
        import jax, jax.numpy as jnp
        import numpy as np
        D_IN, D_HID = (128, 512)

        def _ternary(key, shape):
            return jax.random.randint(key, shape, -1, 2).astype(jnp.float32)

        def _tlin(x, w, s):
            return jnp.einsum('bsi,oi->bso', x, w) * s
        h = jax.nn.silu(_tlin(x, w1_w, w1_s)) * _tlin(x, w2_w, w2_s)
        h = jax.nn.gelu(_tlin(h, h1_w, h1_s), approximate=False)
        h = jax.nn.gelu(_tlin(h, h2_w, h2_s), approximate=False)
        return _tlin(h, w3_w, w3_s)

    def _L1_attn_ref(x, Wq, bq, Wk, bk, Wv, bv, Wo, bo, alpha, aug_param, ln_scale, ln_bias):
        import jax, jax.numpy as jnp
        import numpy as np
        HIDDEN, HEADS, HDIM = (128, 8, 64)
        B, S = (4, 1024)
        LN_EPS = 1e-06
        b, s, _ = x.shape
        h, d = alpha.shape
        scale = d ** (-0.5)
        q = (x @ Wq + bq).reshape(b, s, h, d)
        k = (x @ Wk + bk).reshape(b, s, h, d)
        v = (x @ Wv + bv).reshape(b, s, h, d)
        decay = jax.nn.sigmoid(alpha)

        def step(state, qkv):
            q_t, k_t, v_t = qkv
            attn = jax.nn.softmax(jnp.einsum('bhd,bhd->bh', q_t, k_t) * scale, axis=-1)
            new_state = decay * state + (1.0 - decay) * attn[..., None] * v_t
            return (new_state, new_state)
        qs = jnp.moveaxis(q, 1, 0)
        ks_ = jnp.moveaxis(k, 1, 0)
        vs = jnp.moveaxis(v, 1, 0)
        init = jnp.zeros((b, h, d), x.dtype)
        _, states = jax.lax.scan(step, init, (qs, ks_, vs))
        states = jnp.moveaxis(states, 0, 1)
        aug = jax.nn.sigmoid(q * aug_param)
        out = (q * states + aug).reshape(b, s, h * d)
        out = out @ Wo + bo
        mean = jnp.mean(out, axis=-1, keepdims=True)
        var = jnp.var(out, axis=-1, keepdims=True)
        return (out - mean) * jax.lax.rsqrt(var + LN_EPS) * ln_scale + ln_bias

    def _L1_ffn_ref(x, W_qkv, b_qkv, W_gate, b_gate, W_experts, b_experts):
        import jax, jax.numpy as jnp
        import numpy as np
        NUM_HEADS = 16
        TOP_K = 2
        B, S, D = x.shape
        H = NUM_HEADS
        hd = D // H
        E = W_gate.shape[-1]
        qkv = (x @ W_qkv + b_qkv).reshape(B, S, 3, H, hd)
        q, k, v = (qkv[:, :, 0], qkv[:, :, 1], qkv[:, :, 2])
        attn = jnp.einsum('bqhd,bkhd->bhqk', q, k) / jnp.sqrt(jnp.asarray(hd, x.dtype))
        attn = jax.nn.softmax(attn, axis=-1)
        attn_out = jnp.einsum('bhqk,bkhd->bqhd', attn, v).reshape(B, S, D)
        gate = jax.nn.softmax(x @ W_gate + b_gate, axis=-1)
        top_g, top_i = jax.lax.top_k(gate, TOP_K)
        combine = jnp.sum(jax.nn.one_hot(top_i, E, dtype=x.dtype) * top_g[..., None], axis=2)
        expert_out = jnp.einsum('bsd,edf->bsef', x, W_experts) + b_experts
        moe_out = jnp.einsum('bsef,bse->bsf', expert_out, combine)
        return attn_out + moe_out
    x = L0_attn_x
    xn = _layernorm(x, axis=-1)
    s = _L0_attn_ref(xn, L0_attn_Wk, L0_attn_Wq, L0_attn_Wv, L0_attn_Wa, L0_attn_Wb)
    g = _silu(_L0_ffn_ref(xn, L0_ffn_w1_w, L0_ffn_w1_s, L0_ffn_w2_w, L0_ffn_w2_s, L0_ffn_h1_w, L0_ffn_h1_s, L0_ffn_h2_w, L0_ffn_h2_s, L0_ffn_w3_w, L0_ffn_w3_s))
    x = x + s * g
    xn = _layernorm(x, axis=-1)
    s = _L1_attn_ref(xn, L1_attn_Wq, L1_attn_bq, L1_attn_Wk, L1_attn_bk, L1_attn_Wv, L1_attn_bv, L1_attn_Wo, L1_attn_bo, L1_attn_alpha, L1_attn_aug_param, L1_attn_ln_scale, L1_attn_ln_bias)
    g = _silu(_L1_ffn_ref(xn, L1_ffn_W_qkv, L1_ffn_b_qkv, L1_ffn_W_gate, L1_ffn_b_gate, L1_ffn_W_experts, L1_ffn_b_experts))
    x = x + s * g
    return x

_drawn_inputs = setup_inputs


def setup_inputs(seed=0):
    import zlib

    import numpy as np

    out = dict(_drawn_inputs(seed))
    spreads = {'L1_attn_bq': (0.0, 0.1),
     'L1_attn_bk': (0.0, 0.1),
     'L1_attn_bv': (0.0, 0.1),
     'L1_attn_bo': (0.0, 0.1),
     'L1_attn_alpha': (1.0, 0.2),
     'L1_attn_ln_scale': (1.0, 0.2),
     'L1_attn_ln_bias': (0.0, 0.1),
     'L1_ffn_b_qkv': (0.0, 0.1),
     'L1_ffn_b_gate': (0.0, 0.1),
     'L1_ffn_b_experts': (0.0, 0.1)}
    factors = {}
    for name, (base, spread) in spreads.items():
        noise = np.random.default_rng([zlib.crc32(name.encode()), seed]).standard_normal(out[name].shape)
        drawn = base * np.exp(spread * noise) if base else spread * noise
        out[name] = jnp.asarray(drawn.astype(out[name].dtype))
    for name, factor in factors.items():
        out[name] = (out[name] * factor).astype(out[name].dtype)
    return out
```

```python
from contextlib import ExitStack

import concourse.bass as bass
from concourse import mybir

ALU = mybir.AluOpType
ACT = mybir.ActivationFunctionType
F32 = mybir.dt.float32
F32R = mybir.dt.float32r
I32 = mybir.dt.int32
AX = mybir.AxisListType

P = 128
B, S, D = 4, 1024, 128
NT = S // P
CH = 512
NCH = S // CH
TPC = CH // P
HID = 512
KM = HID // P
H1, HD1 = 8, 64
HM, HDM = 16, 8
GH = 4
NG = HM // GH
E = 8
QUAD = 32
LN_EPS, LN1_EPS = 1e-5, 1e-6
SAFE = 40.0
UNITS = NG * NT * GH

COL = {}
_at = 0
for _name, _n in (("w1s", KM), ("w2s", KM), ("h1s", KM), ("h2s", KM), ("w3s", 1), ("bq", KM), ("bk", KM),
                  ("bv", KM), ("aug", KM), ("alpha", KM), ("mbq", 1), ("mbk", 1), ("row24", 1)):
    COL[_name] = _at
    _at += _n
NCOL = _at
CI, CO, CHD, CBM, CSEL, CMASK = 0, 128, 256, 288, 304, 816
NCST = 816 + NT * E
FW1, FW2, FH1, FH2, FW3 = 0, HID, 2 * HID, 2 * HID + KM * HID, 2 * HID + 2 * KM * HID
NFW = FW3 + KM * D
LQ, LK, LV, LM, LE, LG = 0, HID, 2 * HID, 3 * HID, 3 * HID + 3 * D, 3 * HID + 3 * D + E * D
NLW = LG + E


class Signal:

    def __init__(self, ctx, nc, name, per):
        self.sem, self.per, self.name, self.given = ctx.enter_context(nc.semaphore(name)), per, name, 0

    def at(self, b, k):
        return b * self.per + k

    def check(self):
        assert self.given == self.per, (self.name, self.given, self.per)


def build_program(nc, x, fw, lw, aw, wo, cst, cols, rows, bexp, out):
    with ExitStack() as ctx:
        def sb(name, shape, dt=F32):
            return ctx.enter_context(nc.sbuf_tensor(name, shape, dt))

        def sem(name):
            return ctx.enter_context(nc.semaphore(name))

        def sig(name, per=1):
            return Signal(ctx, nc, name, per)

        fw_hi, fw_lo = sb("fw_hi", [P, NFW], F32R), sb("fw_lo", [P, NFW], F32R)
        lw_hi, lw_lo = sb("lw_hi", [P, NLW], F32R), sb("lw_lo", [P, NLW], F32R)
        gh_hi, gh_lo = sb("gh_hi", [P, 2 * D], F32R), sb("gh_lo", [P, 2 * D], F32R)
        wo_sb = sb("wo_sb", [P, KM * D])
        cst_sb = sb("cst_sb", [P, NCST])
        sel_r = sb("sel_r", [P, 4 * P], F32R)
        ones_r = sb("ones_r", [1, P], F32R)
        cols_sb = sb("cols_sb", [P, NCOL])
        rows_sb = sb("rows_sb", [P, 4 * D + E])
        bexp_sb = sb("bexp_sb", [NT * E, NT * D])
        decay = sb("decay", [P, 3 * KM])
        flags = sb("flags", [P, 8])
        iflag = sb("iflag", [P, 2], I32)
        ident, ones = cst_sb[:, CI:CI + P], cst_sb[:, CO:CO + P]

        xres = sb("xres", [P, NT, D])
        xn = sb("xn", [P, NT * D])
        xt_hi, xt_lo = sb("xt_hi", [P, S], F32R), sb("xt_lo", [P, S], F32R)
        spl = sb("spl", [P, 4, S], F32R)
        big = sb("big", [P, 2, 4, S])
        hid = sb("hid", [P, 2, 2, KM, CH], F32R)
        wk = sb("wk", [P, 4 * S])
        vaug = sb("vaug", [P, NT * HM * (HDM + 1) + QUAD])
        st = sb("st", [P, NT * 14])
        sm = sb("sm", [P, 12, NT * E])
        mx = sb("mx", [P, NT])
        negT = sb("negT", [NT, P], F32R)
        ct = sb("ct", [NT * E, P])
        bias_m = sb("bias_m", [P, HM])
        qk_max = sb("qk_max", [P, 4])
        mbuf = sb("mbuf", [P, P])
        mrow = sb("mrow", [P, 1])
        scrap = sb("scrap", [P, NT])

        bn = st[:, 0:NT * 6].rearrange("p (t k) -> p t k", k=6)
        lnw = st[:, NT * 6:NT * 10].rearrange("p (k t) -> p k t", k=4)
        mean, var, rstd = (st[:, NT * i:NT * (i + 1)] for i in (10, 11, 12))
        s_nat = wk[:, 0:S]
        act32 = [wk[:, S + i * CH:S + (i + 1) * CH] for i in range(3)]
        uaug = wk[:, S + 3 * CH:S + 3 * CH + NT * (D + 1)].rearrange("p (t n) -> p t n", n=D + 1)
        kz = spl
        negrow = spl[0:1, 2, :]
        vaug4 = vaug[:, 0:NT * HM * (HDM + 1)].rearrange("p (t h n) -> p t h n", t=NT, n=HDM + 1)
        q1, v1 = big[:, 0], big[:, 1]
        q_st, k_st = hid[:, 0].rearrange("p a k n -> p (a k n)").rearrange("p (g n) -> p g n", g=NG), \
            hid[:, 1].rearrange("p a k n -> p (a k n)").rearrange("p (g n) -> p g n", g=NG)
        prob = big
        gT = big[:, 0, 0, :]

        ps = ctx.enter_context(nc.psum_tensor("ps", [P, 8, CH], F32))

        loaded, bexp_in = sem("loaded"), sem("bexp_in")
        setup_v, setup_a, setup_p = sem("setup_v"), sem("setup_a"), sem("setup_p")

        trip_open, half_set = sem("trip_open"), sem("half_set")
        x_in = sig("x_in", 16)
        chain = sig("chain", 194)
        xT_mm, x_hi, x_lo = sig("xT_mm", 4), sig("x_hi", 4), sig("x_lo", 4)
        r_mm, r_hi, r_lo = sig("r_mm", 2), sig("r_hi", 2), sig("r_lo", 2)
        u_mm, u_ok = sig("u_mm", 2), sig("u_ok", 2)
        max_mm, row_max = sig("max_mm", NT), sig("row_max", NT)
        maxT, neg_ok, negrow_in = sig("maxT"), sig("neg_ok"), sig("negrow_in", 16)
        l1_mm, l1_act, hid_hi, hid_lo = sig("l1_mm", 16), sig("l1_act", 8), sig("hid_hi", 24), sig("hid_lo", 24)
        sc_mm, sc_exp = sig("sc_mm", 16), sig("sc_exp", 16)
        pv_mm, pv_norm = sig("pv_mm", NT), sig("pv_norm", NT)
        h_mm, h_act = sig("h_mm", 16), sig("h_act", 16)
        w3_mm, w3_act, gnat_mm, res_ok = sig("w3_mm", 2), sig("w3_act", 2), sig("gnat_mm", 2), sig("res_ok", 2)
        ln_ok, var_ok, rstd_ok = sig("ln_ok", 2), sig("var_ok", 3), sig("rstd_ok", 3)
        qk_mm, q_copy, prod_ok = sig("qk_mm", 16), sig("q_copy", 8), sig("prod_ok", 8)
        hs_mm, hs_sub, hs_exp, attn_ok = sig("hs_mm", 2), sig("hs_sub"), sig("hs_exp"), sig("attn_ok")
        v_mm, v_copy, bc_mm, u1_ok = sig("v_mm", 8), sig("v_copy", 8), sig("bc_mm", 8), sig("u1_ok", 8)
        aug_ok, z_ok, o_mm, s1_ok = sig("aug_ok", 8), sig("z_ok", 8), sig("o_mm", 2), sig("s1_ok")
        mq_mm, mq_hi, mq_lo = sig("mq_mm", 4), sig("mq_hi", 4), sig("mq_lo", 4)
        stk_mm, stk_ok = sig("stk_mm", 8), sig("stk_ok", 8)
        mv_mm, mv_ok, gate_mm = sig("mv_mm", 2), sig("mv_ok", 2), sig("gate_mm")
        g_sub, g_exp = sig("g_sub"), sig("g_exp")
        bnd_in, bnd_mm, bnd_ok = sig("bnd_in"), sig("bnd_mm"), sig("bnd_ok")
        kz_set, kz_ok = sig("kz_set"), sig("kz_ok", HM)
        kz_open = sig("kz_open")
        gen_mm, gen_mx, gen_T, gen_add = (sig("gen_mm", UNITS), sig("gen_mx", UNITS), sig("gen_T", NG * NT),
                                          sig("gen_add", NG * NT))
        ms_mm, ms_exp = sig("ms_mm", UNITS), sig("ms_exp", UNITS)
        mp_mm, oT_ok = sig("mp_mm", NG * NT * 2), sig("oT_ok", NG)
        oN_mm, att_ok = sig("oN_mm", NT), sig("att_ok", NT)
        comb_ok, cT_mm, cT_ok, eb_mm = sig("comb_ok"), sig("cT_mm"), sig("cT_ok"), sig("eb_mm")
        ex_mm, ex_ok, g2_ok, fin_ok = sig("ex_mm", NT), sig("ex_ok", NT), sig("g2_ok", 2), sig("fin_ok", 2)
        stored = sig("stored", 32)

        def col(name, k=0):
            return cols_sb[:, COL[name] + k:COL[name] + k + 1]

        def up(signal, ins, n=1):
            signal.given += n
            return ins.then_inc(signal.sem, n)

        block = ctx.enter_context(nc.Block())

        @block.sync
        def _(sp):
            sp.dma_start(cst_sb[:, :], cst).then_inc(loaded, 16)
            sp.dma_start(cols_sb[:, :], cols).then_inc(loaded, 16)
            sp.dma_start(xn[:, 0:5 * D], aw).then_inc(loaded, 16)
            bigf = big[:, :, :, :].rearrange("p a g n -> p (a g n)")
            sp.dma_start(bigf[:, 0:NFW], fw).then_inc(loaded, 16)
            sp.dma_start(wk[:, 0:NLW], lw).then_inc(loaded, 16)
            sp.dma_start(wo_sb[:, :], wo).then_inc(loaded, 16)
            sp.dma_start(rows_sb[:, :], rows).then_inc(loaded, 16)
            sp.wait_ge(setup_v, 1)
            for t in range(NT):
                sp.dma_start(bexp_sb[E * t:E * (t + 1), D * t:D * (t + 1)], bexp).then_inc(bexp_in, 16)
            with sp.Fori(0, B) as b:
                sp.wait_ge(trip_open, b * 2 + 2)
                up(x_in, sp.dma_start(xres[:, :, :], x[bass.ds(b, 1)].rearrange("o (t p) d -> p (o t) d", p=P)), 16)
                sp.wait_ge(neg_ok.sem, neg_ok.at(b, 1))
                up(negrow_in, sp.dma_start(negrow[:, :].bitcast(F32), negT[:, :].bitcast(F32)), 16)
                for c in range(NCH):
                    sp.wait_ge(fin_ok.sem, fin_ok.at(b, c + 1))
                    o = out[bass.ds(b, 1)].rearrange("o (t p) d -> p (o t) d", p=P)
                    up(stored, sp.dma_start(o[:, c * TPC:(c + 1) * TPC, :],
                                            big[:, 0, 2, :].rearrange("p (t d) -> p t d", d=D)[:, c * TPC:(c + 1) * TPC, :]), 16)
            sp.wait_ge(stored.sem, B * stored.per)

        @block.vector
        def _(v):
            n = [0]

            def done(ins):
                ins.then_inc(setup_v, 1)
                n[0] += 1

            done(v.memset(bexp_sb[:, :], 0.0))
            v.wait_ge(loaded, 16 * 7)
            bigf = big[:, :, :, :].rearrange("p a g n -> p (a g n)")
            lwf = wk[:, :]
            done(v.tensor_copy(fw_hi[:, :], bigf[:, 0:NFW]))
            done(v.tensor_copy(lw_hi[:, :], lwf[:, 0:NLW]))
            v.wait_ge(setup_v, 3)
            done(v.tensor_tensor(fw_lo[:, :], bigf[:, 0:NFW], fw_hi[:, :].bitcast(F32), ALU.subtract))
            done(v.tensor_tensor(lw_lo[:, :], lwf[:, 0:NLW], lw_hi[:, :].bitcast(F32), ALU.subtract))
            v.wait_ge(setup_v, 5)
            done(v.tensor_reduce(flags[:, 0:1], fw_lo[:, :].bitcast(F32), AX.X, ALU.max, apply_absolute_value=True))
            done(v.memset(vaug[:, :], 0.0))
            done(v.memset(mbuf[:, :], 0.0))
            v.wait_ge(setup_v, 8)
            done(v.memset(vaug4[:, :, :, HDM:HDM + 1], 1.0))
            done(v.tensor_copy(sel_r[:, :], cst_sb[:, CSEL:CSEL + 4 * P]))
            done(v.tensor_copy(ones_r[:, :], cst_sb[0:1, CO:CO + P]))
            v.wait_ge(setup_a, 1)
            done(v.tensor_scalar(decay[:, KM:2 * KM], decay[:, 0:KM], -1.0, 1.0, ALU.mult, ALU.add))
            v.wait_ge(setup_v, 12)
            done(v.tensor_tensor(decay[:, 2 * KM:3 * KM], decay[:, KM:2 * KM], cols_sb[:, COL["bv"]:COL["bv"] + KM], ALU.mult))
            v.wait_ge(setup_p, 1)
            done(v.tensor_copy(xn[:, 5 * D:6 * D], ps[:, 0, 0:D]))
            v.wait_ge(setup_p, 2)
            done(v.tensor_copy(gh_hi[:, :], ps[:, 1, 0:2 * D]))
            v.wait_ge(setup_v, 15)
            done(v.tensor_tensor(gh_lo[:, :], ps[:, 1, 0:2 * D], gh_hi[:, :].bitcast(F32), ALU.subtract))
            v.wait_ge(setup_p, 3)
            done(v.tensor_scalar(iflag[:, 0:1], ps[:, 2, 0:1], 0.0, None, ALU.is_gt))
            v.wait_ge(setup_v, 17)

            with v.Fori(0, B) as b:
                k = [0]

                def step(ins):
                    k[0] += 1
                    up(chain, ins)

                def own():
                    v.wait_ge(chain.sem, chain.at(b, k[0]))

                def layer_norm_stats(src, n_, eps):
                    for t in range(NT):
                        step(v.bn_stats(bn[:, t, :], src[:, t, :]))
                    own()
                    step(v.tensor_tensor(lnw[:, 0, :], bn[:, :, 1], bn[:, :, 4], ALU.add))
                    step(v.tensor_tensor(lnw[:, 1, :], bn[:, :, 1], bn[:, :, 4], ALU.subtract))
                    step(v.tensor_tensor(lnw[:, 2, :], bn[:, :, 2], bn[:, :, 5], ALU.add))
                    own()
                    step(v.tensor_scalar(mean, lnw[:, 0, :], 0.5, None, ALU.mult))
                    step(v.scalar_tensor_tensor(lnw[:, 3, :], lnw[:, 1, :], 0.25, lnw[:, 1, :], ALU.mult, ALU.mult))
                    step(v.tensor_scalar(lnw[:, 2, :], lnw[:, 2, :], 1.0 / D, eps, ALU.mult, ALU.add))
                    own()
                    up(var_ok, v.tensor_tensor(var, lnw[:, 2, :], lnw[:, 3, :], ALU.add))
                    v.wait_ge(rstd_ok.sem, rstd_ok.at(b, n_))

                def normalise(src, dst):
                    for t in range(NT):
                        ins = v.tensor_scalar(dst[:, t, :], src[:, t, :], mean[:, t:t + 1], rstd[:, t:t + 1],
                                              ALU.subtract, ALU.mult)
                        if t < NT - 1:
                            step(ins)
                    return ins

                def split_rest(lo, hi, bank, c, sig_mm, n_mm, sig_hi, sig_lo):
                    v.wait_ge(sig_mm.sem, sig_mm.at(b, n_mm))
                    v.wait_ge(sig_hi.sem, sig_hi.at(b, n_mm))
                    up(sig_lo, v.tensor_tensor(lo[:, c * CH:(c + 1) * CH], ps[:, bank, :],
                                               hi[:, c * CH:(c + 1) * CH].bitcast(F32), ALU.subtract))

                def split_hidden(n_, buf, m):
                    src = act32[n_ % 3]
                    up(hid_hi, v.tensor_copy(hid[:, buf, 0, m, :], src))
                    v.wait_ge(hid_hi.sem, hid_hi.at(b, n_ + 1))
                    up(hid_lo, v.tensor_tensor(hid[:, buf, 1, m, :], src, hid[:, buf, 0, m, :].bitcast(F32), ALU.subtract))

                v.wait_ge(trip_open, b * 2 + 2)
                v.wait_ge(x_in.sem, x_in.at(b, 16))
                xnv = xn[:, :].rearrange("p (t d) -> p t d", d=D)
                layer_norm_stats(xres, 1, LN_EPS)
                up(ln_ok, normalise(xres, xnv))
                for c in range(NCH):
                    split_rest(xt_lo, xt_hi, c, c, xT_mm, c + 1, x_hi, x_lo)
                for c in range(NCH):
                    split_rest(spl[:, 1], spl[:, 0], 2 + c, c, r_mm, c + 1, r_hi, r_lo)
                for t in range(NT):
                    v.wait_ge(max_mm.sem, max_mm.at(b, t + 1))
                    bank = 6 if t % 2 == 0 else 0
                    up(row_max, v.tensor_reduce(mx[:, t:t + 1], ps[:, bank:bank + 2, :], AX.XY, ALU.max))
                step(v.memset(uaug[:, :, D:D + 1], 1.0))

                def gate_units(c):
                    for m in range(KM):
                        u = c * KM + m
                        v.wait_ge(l1_mm.sem, l1_mm.at(b, 2 * u + 2))
                        v.wait_ge(l1_act.sem, l1_act.at(b, u + 1))
                        n_ = 12 * c + m
                        h_ = act32[n_ % 3]
                        step(v.scalar_tensor_tensor(h_, ps[:, (2, 4)[u % 2] + 1, :], col("w2s", m), h_, ALU.mult, ALU.mult))
                        own()
                        split_hidden(n_, c, m)

                def act_units(first, first_hid, buf):
                    for m in range(KM):
                        v.wait_ge(h_act.sem, h_act.at(b, first + m + 1))
                        split_hidden(first_hid + m, buf, m)

                gate_units(0)
                v.wait_ge(maxT.sem, maxT.at(b, 1))
                up(neg_ok, v.tensor_scalar(negT[:, :], ps[0:NT, 6, 0:P], -1.0, None, ALU.mult))
                for t in range(NT):
                    v.wait_ge(pv_mm.sem, pv_mm.at(b, t + 1))
                    o = ps[:, 4 + t % 2, 0:D + 1]
                    step(v.reciprocal(mrow[:, 0:1], o[:, D:D + 1]))
                    own()
                    up(pv_norm, v.tensor_scalar(s_nat[:, t * D:(t + 1) * D], o[:, 0:D], mrow[:, 0:1], None, ALU.mult))
                    v.wait_ge(pv_norm.sem, pv_norm.at(b, t + 1))
                act_units(0, 4, 1)
                act_units(4, 8, 0)

                def residual(c):
                    v.wait_ge(gnat_mm.sem, gnat_mm.at(b, c + 1))
                    own()
                    sl = slice(c * CH, (c + 1) * CH)
                    step(v.tensor_tensor(s_nat[:, sl], s_nat[:, sl], ps[:, (7, 1)[c], :], ALU.mult))
                    own()
                    xr = xres[:, :, :].rearrange("p t d -> p (t d)")[:, sl]
                    up(res_ok, v.tensor_tensor(xr, xr, s_nat[:, sl], ALU.add))

                gate_units(1)
                residual(0)
                act_units(8, 16, 0)
                act_units(12, 20, 1)
                residual(1)
                v.wait_ge(res_ok.sem, res_ok.at(b, 2))
                layer_norm_stats(xres, 2, LN_EPS)
                up(ln_ok, normalise(xres, xnv))
                for c in range(NCH):
                    split_rest(xt_lo, xt_hi, 6 + c, c, xT_mm, 3 + c, x_hi, x_lo)
                for u in range(NCH * KM):
                    c, m = u // KM, u % KM
                    v.wait_ge(qk_mm.sem, qk_mm.at(b, 2 * u + 2))
                    v.wait_ge(q_copy.sem, q_copy.at(b, u + 1))
                    up(prod_ok, v.scalar_tensor_tensor(wk[:, u * CH:(u + 1) * CH], ps[:, 2 * (u % 3) + 1, :], col("bk", m),
                                                       q1[:, m, c * CH:(c + 1) * CH], ALU.add, ALU.mult))

                def softmax8(src, e_sig_in, e_sig_out, out_sig):
                    w3d = lambda i: sm[:, i, :].rearrange("p (t e) -> p t e", e=E)
                    one = lambda i: sm[:, i, 0:NT]
                    bc = lambda i: sm[:, i, 0:NT].unsqueeze(2).broadcast_to([P, NT, E])
                    step(v.tensor_reduce(one(0), src, AX.X, ALU.max))
                    own()
                    up(e_sig_in, v.tensor_tensor(w3d(1), src, bc(0), ALU.subtract))
                    v.wait_ge(e_sig_out.sem, e_sig_out.at(b, 1))
                    step(v.tensor_reduce(one(3), w3d(2), AX.X, ALU.add))
                    own()
                    step(v.reciprocal(one(4), one(3)))
                    own()
                    ins = v.tensor_tensor(w3d(5), w3d(2), bc(4), ALU.mult)
                    if out_sig is None:
                        step(ins)
                        own()
                    else:
                        up(out_sig, ins)
                        v.wait_ge(out_sig.sem, out_sig.at(b, 1))

                v.wait_ge(hs_mm.sem, hs_mm.at(b, 2))
                step(v.tensor_copy(sm[:, 6, :].rearrange("p (c n) -> p c n", c=2), ps[:, 6:8, 0:TPC * H1]))
                own()
                softmax8(sm[:, 6, :].rearrange("p (t e) -> p t e", e=E), hs_sub, hs_exp, attn_ok)
                for u in range(NCH * KM):
                    c, m = u // KM, u % KM
                    sl = slice(c * CH, (c + 1) * CH)
                    v.wait_ge(bc_mm.sem, bc_mm.at(b, u + 1))
                    up(u1_ok, v.tensor_tensor(v1[:, m, sl], v1[:, m, sl], ps[:, u % 4, :], ALU.mult))
                    v.wait_ge(u1_ok.sem, u1_ok.at(b, u + 1))
                    z = wk[:, m * S + c * CH:m * S + (c + 1) * CH]
                    init = 0.0 if c == 0 else v1[:, m, c * CH - 1:c * CH]
                    step(v.tensor_tensor_scan(v1[:, m, sl], decay[:, m:m + 1].broadcast_to([P, CH]), v1[:, m, sl], init,
                                              ALU.mult, ALU.add))
                    own()
                    step(v.tensor_tensor(z, q1[:, m, sl], v1[:, m, sl], ALU.mult))
                    v.wait_ge(aug_ok.sem, aug_ok.at(b, u + 1))
                    own()
                    up(z_ok, v.tensor_tensor(z, z, xn[:, (u % 2) * CH:(u % 2 + 1) * CH], ALU.add))
                for c in range(NCH):
                    v.wait_ge(o_mm.sem, o_mm.at(b, c + 1))
                    if c == 0:
                        v.wait_ge(z_ok.sem, z_ok.at(b, 8))
                    o3 = xnv[:, c * TPC:(c + 1) * TPC, :]
                    step(v.tensor_tensor(o3, ps[:, 4 + c, :].rearrange("p (t d) -> p t d", d=D),
                                         rows_sb[:, 0:D].unsqueeze(1).broadcast_to([P, TPC, D]), ALU.add))
                own()
                layer_norm_stats(xnv, 3, LN1_EPS)
                step(normalise(xnv, xnv))
                own()
                step(v.tensor_tensor(xnv, xnv, rows_sb[:, D:2 * D].unsqueeze(1).broadcast_to([P, NT, D]), ALU.mult))
                own()
                up(s1_ok, v.tensor_tensor(xnv, xnv, rows_sb[:, 2 * D:3 * D].unsqueeze(1).broadcast_to([P, NT, D]), ALU.add))
                for i in range(4):
                    j, c = i // 2, i % 2
                    v.wait_ge(mq_hi.sem, mq_hi.at(b, i + 1))
                    up(mq_lo, v.scalar_tensor_tensor(spl[:, 2 * j + 1, c * CH:(c + 1) * CH], ps[:, (6, 7, 0, 1)[i], :],
                                                     col(("mbq", "mbk")[j]), spl[:, 2 * j, c * CH:(c + 1) * CH].bitcast(F32),
                                                     ALU.add, ALU.subtract))
                    if c == 1:
                        step(v.tensor_reduce(qk_max[:, j:j + 1], spl[:, 2 * j, :].bitcast(F32), AX.X, ALU.max,
                                             apply_absolute_value=True))
                own()
                step(v.scalar_tensor_tensor(qk_max[:, 2:3], qk_max[:, 0:1], -1.002 / HDM ** 0.5, qk_max[:, 1:2],
                                            ALU.mult, ALU.mult))
                own()
                up(bnd_in, v.tensor_scalar(sm[:, 7, 0:HM], cst_sb[:, CBM:CBM + HM], qk_max[:, 2:3], None, ALU.mult))
                for c in range(NCH):
                    v.wait_ge(mv_mm.sem, mv_mm.at(b, c + 1))
                    up(mv_ok, v.tensor_tensor(
                        vaug4[:, c * TPC:(c + 1) * TPC, :, 0:HDM],
                        ps[:, 2 + c, :].rearrange("p (t h n) -> p t h n", t=TPC, n=HDM),
                        rows_sb[:, 3 * D:4 * D].rearrange("p (h n) -> p h n", n=HDM).unsqueeze(1)
                        .broadcast_to([P, TPC, HM, HDM]), ALU.add))
                v.wait_ge(bnd_mm.sem, bnd_mm.at(b, 1))
                step(v.tensor_reduce(flags[:, 1:2], ps[:, 5, 0:HM], AX.X, ALU.min))
                own()
                step(v.tensor_scalar(flags[:, 2:3], flags[:, 1:2], -SAFE, None, ALU.is_ge))
                step(v.tensor_scalar(iflag[:, 1:2], flags[:, 1:2], -SAFE, None, ALU.is_lt))
                own()
                up(bnd_ok, v.tensor_scalar(bias_m[:, :], ps[:, 5, 0:HM], flags[:, 2:3], None, ALU.mult))
                v.wait_ge(gate_mm.sem, gate_mm.at(b, 1))
                w3d = lambda i: sm[:, i, :].rearrange("p (t e) -> p t e", e=E)
                step(v.tensor_tensor(w3d(6), ps[:, 4, 0:NT * E].rearrange("p (t e) -> p t e", e=E),
                                     rows_sb[:, 4 * D:4 * D + E].unsqueeze(1).broadcast_to([P, NT, E]), ALU.add))
                own()
                softmax8(w3d(6), g_sub, g_exp, None)
                gate, left = w3d(5), sm[:, 8, :]
                for r in range(2):
                    src = gate if r == 0 else w3d(8)
                    step(v.tensor_reduce(sm[:, 0, 0:NT], src, AX.X, ALU.max))
                    own()
                    step(v.tensor_tensor(w3d(1), src, sm[:, 0, 0:NT].unsqueeze(2).broadcast_to([P, NT, E]), ALU.is_ge))
                    own()
                    step(v.tensor_tensor_scan(sm[:, 3, :], cst_sb[:, CMASK:CMASK + NT * E], sm[:, 1, :], 0.0,
                                              ALU.mult, ALU.add))
                    own()
                    step(v.scalar_tensor_tensor(sm[:, 9 + r, :], sm[:, 3, :], 1.0, sm[:, 1, :], ALU.is_equal, ALU.mult))
                    own()
                    if r == 0:
                        step(v.scalar_tensor_tensor(left, sm[:, 9, :], -4.0, sm[:, 5, :], ALU.mult, ALU.add))
                        own()
                step(v.tensor_tensor(sm[:, 9, :], sm[:, 9, :], sm[:, 10, :], ALU.add))
                own()
                up(comb_ok, v.tensor_tensor(sm[:, 11, :], sm[:, 5, :], sm[:, 9, :], ALU.mult))

                need_max = v.value_load(iflag[0:1, 1:2], min_val=0, max_val=1)
                base = {s_: s_.given for s_ in (gen_mx, gen_add)}
                with v.If(need_max > 0):
                    for gt in range(NG * NT):
                        g4, t = gt // NT, gt % NT
                        for g in range(GH):
                            n_ = gt * GH + g
                            v.wait_ge(gen_mm.sem, gen_mm.at(b, n_ + 1))
                            if gt and g == 0:
                                v.wait_ge(gen_T.sem, gen_T.at(b, gt))
                            v.tensor_reduce(mbuf[:, QUAD * g + 3 * HDM:QUAD * g + 3 * HDM + 1],
                                            ps[:, (0 if n_ % 2 == 0 else 2):(2 if n_ % 2 == 0 else 4), :],
                                            AX.XY, ALU.max, negate=True).then_inc(gen_mx.sem, 1)
                        v.wait_ge(gen_T.sem, gen_T.at(b, gt + 1))
                        qs = q_st[:, g4, t * P:(t + 1) * P]
                        v.tensor_tensor(qs, qs.bitcast(F32), ps[:, 6 + gt % 2, 0:P], ALU.add).then_inc(gen_add.sem, 1)
                with v.Else():
                    v.sem_inc(gen_mx.sem, gen_mx.per)
                    v.sem_inc(gen_add.sem, gen_add.per)
                gen_mx.given, gen_add.given = gen_mx.per, gen_add.per

                def load_kz(g4, g):
                    rg = slice(QUAD * g, QUAD * (g + 1))
                    up(kz_ok, v.tensor_copy(kz[rg, g, :], k_st[rg, g4, :].bitcast(F32)))

                v.wait_ge(kz_set.sem, kz_set.at(b, 1))
                v.wait_ge(stk_ok.sem, stk_ok.at(b, 2 * NG))
                for g in range(GH):
                    load_kz(0, g)
                for g4 in range(NG):
                    if g4 < NG - 1:
                        for g in range(GH):
                            v.wait_ge(ms_mm.sem, ms_mm.at(b, (g4 * NT + NT - 1) * GH + g + 1))
                            load_kz(g4 + 1, g)
                    v.wait_ge(mp_mm.sem, mp_mm.at(b, (g4 + 1) * NT * 2))
                    up(oT_ok, v.tensor_copy(wk[:, g4 * S:(g4 + 1) * S].rearrange("p (h n) -> p h n", n=CH), ps[:, 4:6, :]))
                att = big[:, 0, 0, :].rearrange("p (t d) -> p t d", d=D)
                for t in range(NT):
                    v.wait_ge(oN_mm.sem, oN_mm.at(b, t + 1))
                    o4 = ps[:, 6 + t % 2, :].rearrange("p (h n) -> p h n", n=QUAD)
                    step(v.reciprocal(sm[:, 0, 0:HM], o4[:, :, HDM]))
                    own()
                    up(att_ok, v.tensor_tensor(att[:, t, :].rearrange("p (h n) -> p h n", n=HDM), o4[:, :, 0:HDM],
                                               sm[:, 0, 0:HM].unsqueeze(2).broadcast_to([P, HM, HDM]), ALU.mult))
                    v.wait_ge(att_ok.sem, att_ok.at(b, t + 1))
                v.wait_ge(eb_mm.sem, eb_mm.at(b, 1))
                step(v.tensor_tensor(att.rearrange("p (c t) d -> p c (t d)", c=2), att.rearrange("p (c t) d -> p c (t d)", c=2),
                                     ps[:, 4:6, :], ALU.add))
                own()
                fin = big[:, 0, 2, :].rearrange("p (t d) -> p t d", d=D)
                g2 = big[:, 0, 1, :].rearrange("p (t d) -> p t d", d=D)

                def finish(c):
                    tl = slice(c * TPC, (c + 1) * TPC)
                    v.wait_ge(g2_ok.sem, g2_ok.at(b, c + 1))
                    step(v.tensor_tensor(g2[:, tl, :], g2[:, tl, :], xnv[:, tl, :], ALU.mult))
                    own()
                    up(fin_ok, v.tensor_tensor(fin[:, tl, :], g2[:, tl, :], xres[:, tl, :], ALU.add))

                for t in range(NT):
                    v.wait_ge(ex_mm.sem, ex_mm.at(b, t + 1))
                    for e in range(E):
                        ins = v.scalar_tensor_tensor(att[:, t, :], ps[:, 2 * (t % 2) + e // 4, (e % 4) * D:(e % 4 + 1) * D],
                                                     sm[:, 11, t * E + e:t * E + e + 1], att[:, t, :], ALU.mult, ALU.add)
                        if e < E - 1:
                            step(ins)
                            own()
                    up(ex_ok, ins)
                    if t == NT - 2:
                        finish(0)
                finish(1)
                v.wait_ge(fin_ok.sem, fin_ok.at(b, 2))
                v.sem_inc(trip_open, 1)

        @block.gpsimd
        def _(g_):
            g_.memset(st[:, 13 * NT:14 * NT], -0.5).then_inc(half_set, 1)
            g_.wait_ge(half_set, 1)
            with g_.Fori(0, B) as b:
                for n_ in range(3):
                    g_.wait_ge(var_ok.sem, var_ok.at(b, n_ + 1))
                    up(rstd_ok, g_.tensor_tensor(rstd, var, st[:, 13 * NT:14 * NT], ALU.pow))
                g_.wait_ge(stk_mm.sem, stk_mm.at(b, 2 * NG))
                up(kz_open, g_.tensor_tensor(scrap[:, :], st[:, 13 * NT:14 * NT], st[:, 13 * NT:14 * NT], ALU.mult))
                up(kz_set, g_.memset(kz[:, :, :].bitcast(F32), 0.0))

        @block.scalar
        def _(a):
            a.wait_ge(loaded, 16 * 7)
            a.activation(decay[:, 0:KM], cols_sb[:, COL["alpha"]:COL["alpha"] + KM], ACT.Sigmoid).then_inc(setup_a, 1)
            a.wait_ge(setup_v, 17)
            a.sem_inc(trip_open, 2)
            with a.Fori(0, B) as b:
                a.wait_ge(trip_open, b * 2 + 2)

                def split_head(hi, bank, c, sig_mm, n_mm, sig_hi):
                    a.wait_ge(sig_mm.sem, sig_mm.at(b, n_mm))
                    up(sig_hi, a.activation(hi[:, c * CH:(c + 1) * CH], ps[:, bank, :], ACT.Copy))

                for c in range(NCH):
                    split_head(xt_hi, c, c, xT_mm, c + 1, x_hi)
                for c in range(NCH):
                    split_head(spl[:, 0], 2 + c, c, r_mm, c + 1, r_hi)
                for c in range(NCH):
                    a.wait_ge(u_mm.sem, u_mm.at(b, c + 1))
                    up(u_ok, a.activation(uaug[:, c * TPC:(c + 1) * TPC, 0:D],
                                          ps[:, 4 + c, :].rearrange("p (t d) -> p t d", d=D), ACT.Copy))

                def silu_units(c):
                    for m in range(KM):
                        u = c * KM + m
                        a.wait_ge(l1_mm.sem, l1_mm.at(b, 2 * u + 1))
                        n_ = 12 * c + m
                        if n_ >= 3:
                            a.wait_ge(hid_lo.sem, hid_lo.at(b, n_ - 2))
                        up(l1_act, a.activation(act32[n_ % 3], ps[:, (2, 4)[u % 2], :], ACT.Silu, scale=col("w1s", m)))

                def gelu_units(first, first_hid, name, banks):
                    for m in range(KM):
                        n_ = first_hid + m
                        a.wait_ge(h_mm.sem, h_mm.at(b, first + m + 1))
                        a.wait_ge(hid_lo.sem, hid_lo.at(b, n_ - 2))
                        up(h_act, a.activation(act32[n_ % 3], ps[:, banks[m], :], ACT.Gelu, scale=col(name, m)))

                def silu_g(c):
                    a.wait_ge(w3_mm.sem, w3_mm.at(b, c + 1))
                    up(w3_act, a.activation(gT[:, c * CH:(c + 1) * CH], ps[:, 0, :], ACT.Silu, scale=col("w3s")))

                silu_units(0)
                for n_ in range(2 * NT):
                    h, jt = n_ // NT, n_ % NT
                    a.wait_ge(sc_mm.sem, sc_mm.at(b, n_ + 1))
                    up(sc_exp, a.activation(big[:, h, jt // 2, (jt % 2) * CH:(jt % 2 + 1) * CH],
                                            ps[:, (0, 1, 6, 7)[n_ % 4], :], ACT.Exp))
                gelu_units(0, 4, "h1s", (0, 1, 2, 3))
                gelu_units(4, 8, "h2s", (4, 5, 6, 7))
                silu_g(0)
                silu_units(1)
                gelu_units(8, 16, "h1s", (0, 1, 6, 7))
                gelu_units(12, 20, "h2s", (2, 3, 4, 5))
                silu_g(1)
                for c in range(NCH):
                    split_head(xt_hi, 6 + c, c, xT_mm, 3 + c, x_hi)
                for u in range(NCH * KM):
                    c, m = u // KM, u % KM
                    a.wait_ge(qk_mm.sem, qk_mm.at(b, 2 * u + 1))
                    up(q_copy, a.activation(q1[:, m, c * CH:(c + 1) * CH], ps[:, 2 * (u % 3), :], ACT.Identity,
                                            bias=col("bq", m)))
                for u in range(NCH * KM):
                    c, m = u // KM, u % KM
                    a.wait_ge(v_mm.sem, v_mm.at(b, u + 1))
                    up(v_copy, a.activation(v1[:, m, c * CH:(c + 1) * CH], ps[:, u % 6, :], ACT.Identity,
                                            bias=decay[:, 2 * KM + m:2 * KM + m + 1], scale=decay[:, KM + m:KM + m + 1]))
                    if u == 3:
                        a.wait_ge(hs_sub.sem, hs_sub.at(b, 1))
                        up(hs_exp, a.activation(sm[:, 2, :], sm[:, 1, :], ACT.Exp, scale=HD1 ** -0.5))
                for u in range(NCH * KM):
                    c, m = u // KM, u % KM
                    if u >= 2:
                        a.wait_ge(z_ok.sem, z_ok.at(b, u - 1))
                    up(aug_ok, a.activation(xn[:, (u % 2) * CH:(u % 2 + 1) * CH], q1[:, m, c * CH:(c + 1) * CH], ACT.Sigmoid,
                                            scale=col("aug", m)))
                for i in range(4):
                    j, c = i // 2, i % 2
                    a.wait_ge(mq_mm.sem, mq_mm.at(b, i + 1))
                    up(mq_hi, a.activation(spl[:, 2 * j, c * CH:(c + 1) * CH], ps[:, (6, 7, 0, 1)[i], :], ACT.Identity,
                                           bias=col(("mbq", "mbk")[j])))
                for i in range(2 * NG):
                    g4, j = i // 2, i % 2
                    a.wait_ge(stk_mm.sem, stk_mm.at(b, i + 1))
                    dst = (q_st, k_st)[j][:, g4, :].rearrange("p (h n) -> p h n", n=CH)
                    src = ps[:, (6, 0)[i % 2]:(8, 2)[i % 2], :]
                    if j == 0:
                        up(stk_ok, a.activation(dst, src, ACT.Copy))
                    else:
                        up(stk_ok, a.activation(dst, src, ACT.Identity, bias=col("row24")))
                a.wait_ge(g_sub.sem, g_sub.at(b, 1))
                up(g_exp, a.activation(sm[:, 2, :], sm[:, 1, :], ACT.Exp))
                a.wait_ge(bnd_ok.sem, bnd_ok.at(b, 1))
                for u in range(UNITS):
                    g4, jt, g = u // (NT * GH), (u // GH) % NT, u % GH
                    a.wait_ge(ms_mm.sem, ms_mm.at(b, u + 1))
                    if u >= 2 * GH:
                        a.wait_ge(mp_mm.sem, mp_mm.at(b, 2 * (u // GH - 1)))
                    pr = (0, 2, 6)[u % 3]
                    h = g4 * GH + g
                    up(ms_exp, a.activation(prob[:, jt % 2, g, :].rearrange("p (h n) -> p h n", n=CH), ps[:, pr:pr + 2, :],
                                            ACT.Exp, bias=bias_m[:, h:h + 1], scale=HDM ** -0.5))
                a.wait_ge(cT_mm.sem, cT_mm.at(b, 1))
                up(cT_ok, a.activation(ct[:, :], ps[0:NT * E, 3, 0:P], ACT.Copy))
                for c in range(NCH):
                    a.wait_ge(ex_ok.sem, ex_ok.at(b, (c + 1) * TPC))
                    up(g2_ok, a.activation(big[:, 0, 1, c * CH:(c + 1) * CH], big[:, 0, 0, c * CH:(c + 1) * CH], ACT.Silu))
                a.wait_ge(stored.sem, stored.at(b, 32))
                a.sem_inc(trip_open, 1)

        @block.tensor
        def _(t_):
            def mm(out_, lhsT, rhs, start, stop, **kw):
                return t_.matmul(out_, lhsT, rhs, start=start, stop=stop, **kw)

            def split3(out_, l_hi, l_lo, r_hi_, r_lo_, start=True, stop=True):
                mm(out_, l_hi, r_hi_, start, False)
                mm(out_, l_hi, r_lo_, False, False)
                return mm(out_, l_lo, r_hi_, False, stop)

            t_.wait_ge(loaded, 16 * 7)
            waT, wkk, wq, wv, wbT = (xn[:, i * D:(i + 1) * D] for i in range(5))
            mm(ps[:, 0, 0:D], waT, wkk, True, True).then_inc(setup_p, 1)
            mm(ps[:, 1, D:2 * D], wv, wbT, True, True)
            t_.wait_ge(setup_v, 14)
            mm(ps[:, 1, 0:D], wq, xn[:, 5 * D:6 * D], True, True).then_inc(setup_p, 1)
            mm(ps[:, 2, 0:1], ones, flags[:, 0:1], True, True).then_inc(setup_p, 1)
            t_.wait_ge(setup_v, 17)
            t_.wait_ge(bexp_in, 16 * NT)
            mm(ps[:, 3, 0:1], ones, flags[:, 0:1], True, True)
            wide = t_.value_load(iflag[0:1, 0:1], min_val=0, max_val=1)

            with t_.Fori(0, B) as b:
                def xT(c):
                    return xt_hi[:, c * CH:(c + 1) * CH], xt_lo[:, c * CH:(c + 1) * CH]

                def tok(t):
                    return xt_hi[:, t * P:(t + 1) * P], xt_lo[:, t * P:(t + 1) * P]

                def lwp(at, n=P):
                    return lw_hi[:, at:at + n], lw_lo[:, at:at + n]

                def transposes(first_bank, n0):
                    t_.wait_ge(ln_ok.sem, ln_ok.at(b, n0 // 2 + 1))
                    for t in range(NT):
                        ins = t_.transpose(ps[:, first_bank + t // TPC, (t % TPC) * P:(t % TPC + 1) * P],
                                           xn[:, t * D:(t + 1) * D], ident)
                        if t % TPC == TPC - 1:
                            up(xT_mm, ins)

                t_.wait_ge(trip_open, b * 2 + 2)
                transposes(0, 0)
                for c in range(NCH):
                    t_.wait_ge(x_lo.sem, x_lo.at(b, c + 1))
                    up(r_mm, split3(ps[:, 2 + c, :], gh_hi[:, 0:D], gh_lo[:, 0:D], *xT(c)))
                for t in range(NT):
                    ins = split3(ps[:, 4 + t // TPC, (t % TPC) * D:(t % TPC + 1) * D], *tok(t), gh_hi[:, D:2 * D], gh_lo[:, D:2 * D])
                    if t % TPC == TPC - 1:
                        up(u_mm, ins)
                t_.wait_ge(r_hi.sem, r_hi.at(b, 2))
                for t in range(NT):
                    bank = 6 if t % 2 == 0 else 0
                    if t >= 2:
                        t_.wait_ge(row_max.sem, row_max.at(b, t - 1))
                    for c in range(NCH):
                        ins = mm(ps[:, bank + c, :], spl[:, 0, t * P:(t + 1) * P], xT(c)[0], True, True)
                    up(max_mm, ins)

                def l1_units(c, general):
                    for m in range(KM):
                        u = c * KM + m
                        if m >= 2:
                            t_.wait_ge(hid_hi.sem, hid_hi.at(b, 12 * c + m - 1))
                        for i, base in enumerate((FW1, FW2)):
                            bank = ps[:, (2, 4)[u % 2] + i, :]
                            w = slice(base + m * P, base + (m + 1) * P)
                            if general:
                                ins = split3(bank, fw_hi[:, w], fw_lo[:, w], *xT(c))
                            else:
                                mm(bank, fw_hi[:, w], xT(c)[0], True, False)
                                ins = mm(bank, fw_hi[:, w], xT(c)[1], False, True)
                            ins.then_inc(l1_mm.sem, 1)

                def dense(base, width, buf, banks, first_hid, general, signal, mcount):
                    for kk in range(KM):
                        t_.wait_ge(hid_lo.sem, hid_lo.at(b, first_hid + kk + 1))
                        for m in range(mcount):
                            w = slice(base + kk * width + m * P, base + kk * width + (m + 1) * P)
                            o_ = ps[:, banks[m], :]
                            h_hi, h_lo = hid[:, buf, 0, kk, :], hid[:, buf, 1, kk, :]
                            if general:
                                ins = split3(o_, fw_hi[:, w], fw_lo[:, w], h_hi, h_lo, kk == 0, kk == KM - 1)
                            else:
                                mm(o_, fw_hi[:, w], h_hi, kk == 0, False)
                                ins = mm(o_, fw_hi[:, w], h_lo, False, kk == KM - 1)
                            if kk == KM - 1:
                                ins.then_inc(signal.sem, 1)

                t_.wait_ge(u_ok.sem, u_ok.at(b, 2))
                t_.wait_ge(r_lo.sem, r_lo.at(b, 2))
                with t_.If(wide > 0):
                    l1_units(0, True)
                with t_.Else():
                    l1_units(0, False)
                t_.wait_ge(row_max.sem, row_max.at(b, NT))
                up(maxT, t_.transpose(ps[0:NT, 6, 0:P], mx[:, :], ident))
                t_.wait_ge(negrow_in.sem, negrow_in.at(b, 16))
                for n_ in range(2 * NT):
                    h, jt = n_ // NT, n_ % NT
                    if n_ >= 4:
                        t_.wait_ge(sc_exp.sem, sc_exp.at(b, n_ - 3))
                    bank = ps[:, (0, 1, 6, 7)[n_ % 4], :]
                    split3(bank, *tok(jt), spl[:, 0, h * CH:(h + 1) * CH], spl[:, 1, h * CH:(h + 1) * CH], True, False)
                    up(sc_mm, mm(bank, ones_r[:, :], negrow[:, h * CH:(h + 1) * CH], False, True))
                for t in range(NT):
                    if t >= 2:
                        t_.wait_ge(pv_norm.sem, pv_norm.at(b, t - 1))
                    h = t // TPC
                    if t % TPC == 0:
                        t_.wait_ge(sc_exp.sem, sc_exp.at(b, (h + 1) * NT))
                    for jt in range(NT):
                        at = (jt % 2) * CH + (t % TPC) * P
                        ins = mm(ps[:, 4 + t % 2, 0:D + 1], big[:, h, jt // 2, at:at + P], uaug[:, jt, :], jt == 0, jt == NT - 1)
                    up(pv_mm, ins)

                def mlp_rest(general):
                    dense(FH1, HID, 0, (0, 1, 2, 3), 0, general, h_mm, KM)
                    t_.wait_ge(pv_norm.sem, pv_norm.at(b, NT))
                    dense(FH2, HID, 1, (4, 5, 6, 7), 4, general, h_mm, KM)
                    dense(FW3, D, 0, (0,), 8, general, w3_mm, 1)
                    l1_units(1, general)
                    g_transposes(0)
                    t_.wait_ge(res_ok.sem, res_ok.at(b, 1))
                    dense(FH1, HID, 1, (0, 1, 6, 7), 12, general, h_mm, KM)
                    dense(FH2, HID, 0, (2, 3, 4, 5), 16, general, h_mm, KM)
                    dense(FW3, D, 1, (0,), 20, general, w3_mm, 1)
                    g_transposes(1)

                def g_transposes(c):
                    t_.wait_ge(w3_act.sem, w3_act.at(b, c + 1))
                    for i in range(TPC):
                        ins = t_.transpose(ps[:, (7, 1)[c], i * P:(i + 1) * P], gT[:, c * CH + i * P:c * CH + (i + 1) * P], ident)
                    ins.then_inc(gnat_mm.sem, 1)

                with t_.If(wide > 0):
                    mlp_rest(True)
                with t_.Else():
                    mlp_rest(False)
                for s_ in (l1_mm, h_mm, w3_mm, gnat_mm):
                    s_.given = s_.per

                transposes(6, 2)
                for c in range(NCH):
                    t_.wait_ge(x_lo.sem, x_lo.at(b, 3 + c))
                    for m in range(KM):
                        u = c * KM + m
                        if u >= 3:
                            t_.wait_ge(prod_ok.sem, prod_ok.at(b, u - 2))
                        for i, base in enumerate((LQ, LK)):
                            up(qk_mm, split3(ps[:, 2 * (u % 3) + i, :], *lwp(base + m * P), *xT(c)))

                def head_scores(c):
                    t_.wait_ge(prod_ok.sem, prod_ok.at(b, KM * (c + 1)))
                    for i in range(TPC):
                        for m in range(KM):
                            ins = mm(ps[:, 6 + c, i * H1:(i + 1) * H1], wk[:, (c * KM + m) * CH + i * P:(c * KM + m) * CH + (i + 1) * P],
                                     cst_sb[:, CHD + m * H1:CHD + (m + 1) * H1], m == 0, m == KM - 1)
                    up(hs_mm, ins)

                def v_units(c):
                    for m in range(KM):
                        u = c * KM + m
                        if u >= 6:
                            t_.wait_ge(v_copy.sem, v_copy.at(b, u - 5))
                        up(v_mm, split3(ps[:, u % 6, :], *lwp(LV + m * P), *xT(c)))

                head_scores(0)
                t_.wait_ge(prod_ok.sem, prod_ok.at(b, 2 * KM))
                v_units(0)
                head_scores(1)
                v_units(1)
                t_.wait_ge(attn_ok.sem, attn_ok.at(b, 1))
                t_.wait_ge(v_copy.sem, v_copy.at(b, 8))
                attn3 = sm[:, 5, :].rearrange("p (t h) -> p t h", h=H1)
                for u in range(NCH * KM):
                    c, m = u // KM, u % KM
                    if u >= 4:
                        t_.wait_ge(u1_ok.sem, u1_ok.at(b, u - 3))
                    for i in range(TPC):
                        for j in range(P // HD1):
                            w = attn3[:, c * TPC + i, 2 * m + j:2 * m + j + 1].broadcast_to([P, HD1])
                            ins = mm(ps[HD1 * j:HD1 * (j + 1), u % 4, i * P:(i + 1) * P], w, ident, True, True)
                    up(bc_mm, ins)
                for i in range(4):
                    j, c = i // 2, i % 2
                    if j == 1:
                        t_.wait_ge(u1_ok.sem, u1_ok.at(b, 8))
                    up(mq_mm, split3(ps[:, (6, 7, 0, 1)[i], :], *lwp(LM + j * D), *xT(c)))
                for c in range(NCH):
                    t_.wait_ge(z_ok.sem, z_ok.at(b, KM * (c + 1)))
                    for i in range(TPC):
                        for m in range(KM):
                            ins = mm(ps[:, 4 + c, i * D:(i + 1) * D], wk[:, m * S + c * CH + i * P:m * S + c * CH + (i + 1) * P],
                                     wo_sb[:, m * D:(m + 1) * D], m == 0, m == KM - 1)
                    up(o_mm, ins)
                for t in range(NT):
                    ins = split3(ps[:, 2 + t // TPC, (t % TPC) * D:(t % TPC + 1) * D], *tok(t), *lwp(LM + 2 * D, D))
                    if t % TPC == TPC - 1:
                        up(mv_mm, ins)
                t_.wait_ge(s1_ok.sem, s1_ok.at(b, 1))
                for t in range(NT):
                    ins = split3(ps[:, 4, t * E:(t + 1) * E], *tok(t), *lwp(LG, E))
                up(gate_mm, ins)
                t_.wait_ge(bnd_in.sem, bnd_in.at(b, 1))
                up(bnd_mm, mm(ps[:, 5, 0:HM], ones, sm[:, 7, 0:HM], True, True))
                t_.wait_ge(mq_lo.sem, mq_lo.at(b, 4))
                for i in range(2 * NG):
                    g4, j = i // 2, i % 2
                    if i >= 2:
                        t_.wait_ge(stk_ok.sem, stk_ok.at(b, i - 1))
                    rg = slice(QUAD * g4, QUAD * (g4 + 1))
                    for c in range(NCH):
                        bank = ps[:, (6, 0)[i % 2] + c, :]
                        mm(bank, sel_r[rg, 2 * j * P:(2 * j + 1) * P], spl[rg, 2 * j, c * CH:(c + 1) * CH], True, False)
                        ins = mm(bank, sel_r[rg, (2 * j + 1) * P:(2 * j + 2) * P], spl[rg, 2 * j + 1, c * CH:(c + 1) * CH], False, True)
                    up(stk_mm, ins)
                t_.wait_ge(bnd_ok.sem, bnd_ok.at(b, 1))
                t_.wait_ge(stk_ok.sem, stk_ok.at(b, 2 * NG))
                t_.wait_ge(comb_ok.sem, comb_ok.at(b, 1))
                t_.wait_ge(mv_ok.sem, mv_ok.at(b, 2))
                mm(ps[:, 3, 0:1], ones, ones[:, 0:1], True, True)
                need_max = t_.value_load(iflag[0:1, 1:2], min_val=0, max_val=1)
                with t_.If(need_max > 0):
                    for gt in range(NG * NT):
                        g4, t = gt // NT, gt % NT
                        for g in range(GH):
                            n_ = gt * GH + g
                            if n_ >= 2:
                                t_.wait_ge(gen_mx.sem, gen_mx.at(b, n_ - 1))
                            rg = slice(QUAD * g, QUAD * g + 3 * HDM)
                            for c in range(NCH):
                                ins = mm(ps[:, (0 if n_ % 2 == 0 else 2) + c, :], q_st[rg, g4, t * P:(t + 1) * P],
                                         k_st[rg, g4, c * CH:(c + 1) * CH], True, True)
                            ins.then_inc(gen_mm.sem, 1)
                        t_.wait_ge(gen_mx.sem, gen_mx.at(b, (gt + 1) * GH))
                        if gt >= 2:
                            t_.wait_ge(gen_add.sem, gen_add.at(b, gt - 1))
                        t_.transpose(ps[:, 6 + gt % 2, 0:P], mbuf[:, :], ident).then_inc(gen_T.sem, 1)
                with t_.Else():
                    t_.sem_inc(gen_mm.sem, gen_mm.per)
                    t_.sem_inc(gen_T.sem, gen_T.per)
                gen_mm.given, gen_T.given = gen_mm.per, gen_T.per
                t_.wait_ge(gen_add.sem, gen_add.at(b, NG * NT))

                def m_scores(u):
                    g4, jt, g = u // (NT * GH), (u // GH) % NT, u % GH
                    if u >= 3:
                        t_.wait_ge(ms_exp.sem, ms_exp.at(b, u - 2))
                    if jt == 0:
                        t_.wait_ge(kz_ok.sem, kz_ok.at(b, g4 * GH + g + 1))
                    for c in range(NCH):
                        ins = mm(ps[:, (0, 2, 6)[u % 3] + c, :], kz[:, g, jt * P:(jt + 1) * P],
                                 q_st[:, g4, c * CH:(c + 1) * CH], True, True)
                    up(ms_mm, ins)

                def m_values(gj, c):
                    g4, jt = gj // NT, gj % NT
                    if c == 0:
                        t_.wait_ge(ms_exp.sem, ms_exp.at(b, GH * (gj + 1)))
                        if jt == 0 and g4:
                            t_.wait_ge(oT_ok.sem, oT_ok.at(b, g4))
                    for g in range(GH):
                        ins = mm(ps[QUAD * g:QUAD * (g + 1), 4 + c, :], vaug[:, (jt * HM + g4 * GH + g) * (HDM + 1):(jt * HM + g4 * GH + g) * (HDM + 1) + QUAD],
                                 prob[:, jt % 2, g, c * CH:(c + 1) * CH], jt == 0, jt == NT - 1)
                    up(mp_mm, ins)

                for gj in range(NG * NT):
                    for g in range(GH):
                        m_scores(gj * GH + g)
                        if gj and g in (1, 3):
                            m_values(gj - 1, g // 2)
                m_values(NG * NT - 1, 0)
                m_values(NG * NT - 1, 1)

                t_.wait_ge(ms_exp.sem, ms_exp.at(b, UNITS))
                for t in range(NT):
                    if t == 0:
                        t_.wait_ge(oT_ok.sem, oT_ok.at(b, NG))
                    if t >= 2:
                        t_.wait_ge(att_ok.sem, att_ok.at(b, t - 1))
                    for g4 in range(NG):
                        ins = t_.transpose(ps[:, 6 + t % 2, g4 * P:(g4 + 1) * P], wk[:, g4 * S + t * P:g4 * S + (t + 1) * P], ident)
                    up(oN_mm, ins)
                    if t == 0:
                        up(cT_mm, t_.transpose(ps[0:NT * E, 3, 0:P], sm[:, 11, :], ident))
                t_.wait_ge(cT_ok.sem, cT_ok.at(b, 1))
                for c in range(NCH):
                    ins = mm(ps[:, 4 + c, :], ct[:, :], bexp_sb[:, c * CH:(c + 1) * CH], True, True)
                up(eb_mm, ins)
                for t in range(NT):
                    if t >= 2:
                        t_.wait_ge(ex_ok.sem, ex_ok.at(b, t - 1))
                    for c in range(2):
                        ins = split3(ps[:, 2 * (t % 2) + c, :], *tok(t), *lwp(LE + c * CH, CH))
                    up(ex_mm, ins)

        for s_ in [o for o in list(locals().values()) if isinstance(o, Signal)]:
            s_.check()


def kernel(**inputs):
    import numpy as np
    import concourse.bacc as bacc
    from concourse.bass_utils import run_bass_kernel_spmd

    i = {n: np.asarray(a) for n, a in inputs.items()}

    def blocks(wT):
        k_, n_ = wT.shape
        return np.ascontiguousarray(wT.reshape(k_ // P, P, n_).transpose(1, 0, 2)).reshape(P, -1)

    def column(vec):
        return np.ascontiguousarray(vec.reshape(-1, P).T)

    fw = np.concatenate([blocks(i["L0_ffn_" + n].T) for n in ("w1_w", "w2_w", "h1_w", "h2_w", "w3_w")], 1)
    we = np.ascontiguousarray(i["L1_ffn_W_experts"].transpose(1, 0, 2)).reshape(D, E * D)
    lw = np.concatenate([i["L1_attn_Wq"], i["L1_attn_Wk"], i["L1_attn_Wv"], i["L1_ffn_W_qkv"], we, i["L1_ffn_W_gate"]], 1)
    aw = np.concatenate([i["L0_attn_Wa"].T, i["L0_attn_Wk"], i["L0_attn_Wq"], i["L0_attn_Wv"], i["L0_attn_Wb"].T], 1)
    row24 = np.zeros((P, 1), np.float32)
    row24[3 * HDM::QUAD] = 1.0
    b_qkv = i["L1_ffn_b_qkv"]
    cols = np.concatenate(
        [column(i["L0_ffn_" + n]) for n in ("w1_s", "w2_s", "h1_s", "h2_s", "w3_s")]
        + [column(i["L1_attn_" + n]) for n in ("bq", "bk", "bv")]
        + [column(i["L1_attn_aug_param"]), column(i["L1_attn_alpha"])]
        + [column(b_qkv[0:D]), column(b_qkv[D:2 * D]), row24], 1)
    rows = np.concatenate([i["L1_attn_bo"], i["L1_attn_ln_scale"], i["L1_attn_ln_bias"], b_qkv[2 * D:], i["L1_ffn_b_gate"]])
    rows = np.ascontiguousarray(np.broadcast_to(rows[None, :], (P, rows.shape[0])))
    heads1 = np.zeros((P, KM, H1), np.float32)
    for m in range(KM):
        for p in range(P):
            heads1[p, m, (m * P + p) // HD1] = 1.0
    headsm = np.zeros((P, HM), np.float32)
    sel = np.zeros((4, P, P), np.float32)
    for p in range(P):
        headsm[p, p // HDM] = 1.0
        g, d = (p % QUAD) // HDM, p % HDM
        for which, reps in enumerate(((0, 2), (1,), (0, 1), (2,))):
            for r in reps:
                sel[which, p, QUAD * g + HDM * r + d] = 1.0
    mask = np.ones((P, NT, E), np.float32)
    mask[:, :, 0] = 0.0
    cst = np.concatenate([np.eye(P, dtype=np.float32), np.ones((P, P), np.float32), heads1.reshape(P, -1), headsm,
                          sel.transpose(1, 0, 2).reshape(P, -1), mask.reshape(P, -1)], 1)
    arrays = {"in_x": i["L0_attn_x"], "in_fw": fw, "in_lw": lw, "in_aw": aw, "in_wo": blocks(i["L1_attn_Wo"]),
              "in_cst": cst, "in_cols": cols, "in_rows": rows, "in_bexp": i["L1_ffn_b_experts"]}
    arrays = {n: np.ascontiguousarray(a) for n, a in arrays.items()}

    nc = bacc.Bacc("TRN2", target_bir_lowering=False, num_devices=1)
    args = [nc.dram_tensor(n, a.shape, mybir.dt.from_np(a.dtype), kind="ExternalInput").ap() for n, a in arrays.items()]
    args.append(nc.dram_tensor("out_0", (B, S, D), F32, kind="ExternalOutput").ap())
    build_program(nc, *args)
    r = run_bass_kernel_spmd(nc, [arrays], core_ids=[0])
    return r.results[0]["out_0"]
```

```python
from contextlib import ExitStack

import concourse.bass as bass
from concourse import mybir

ALU = mybir.AluOpType
ACT = mybir.ActivationFunctionType
F32 = mybir.dt.float32
F32R = mybir.dt.float32r
I32 = mybir.dt.int32
AX = mybir.AxisListType

P = 128
B, S, D = 4, 1024, 128
NT = S // P
CH = 512
NCH = S // CH
TPC = CH // P
HID = 512
KM = HID // P
H1, HD1 = 8, 64
HM, HDM = 16, 8
GH = 4
NG = HM // GH
E = 8
QUAD = 32
LN_EPS, LN1_EPS = 1e-5, 1e-6
SAFE = 40.0
UNITS = NG * NT * GH
G_EXP_AT = 20
NORM = NT + 6
SETUP = NORM + GH + 17
L1_BANKS = ((2, 4), (4, 6))
H_BANKS = ((0, 1, 2, 3), (0, 1, 2, 3), (4, 5, 6, 7), (1, 2, 3, 4))
W3_BANKS = (0, 5)
MQ_BANKS = (4, 5, 0, 1)
V_BANKS = (4, 5, 0, 1, 2, 3)
STK_BANKS = (6, 4)
ON_BANKS = (6, 7, 2, 3)
EX_BANKS = (0, 2, 6)

_W1, _H1, _H2, _W3 = (0, 1), (2, 3, 4, 5), (6, 7, 8, 9), (10,)
W_BLOCKS = _W1 + _H1 + _W1 + _H2 + _H1 + _W3 + _H2 + _W3
COL = {}
_at = 0
for _name, _n in (("w1s", KM), ("w2s", KM), ("h1s", KM), ("h2s", KM), ("w3s", 1), ("bq", KM), ("bk", KM),
                  ("bv", KM), ("aug", KM), ("alpha", KM), ("mbq", 1), ("mbk", 1), ("row24", 1)):
    COL[_name] = _at
    _at += _n
NCOL = _at
CI, CO, CHD, CBM, CSEL, CMASK = 0, 128, 256, 288, 304, 816
NCST = 816 + NT * E
FW1, FW2, FH1, FH2, FW3 = 0, HID, 2 * HID, 2 * HID + KM * HID, 2 * HID + 2 * KM * HID
NFW = FW3 + KM * D
LQ, LK, LV, LM, LE, LG = 0, HID, 2 * HID, 3 * HID, 3 * HID + 3 * D, 3 * HID + 3 * D + E * D
NLW = LG + E


class Signal:

    def __init__(self, ctx, nc, name, per, start=0):
        self.sem, self.per, self.name, self.given = ctx.enter_context(nc.semaphore(name)), per, name, 0
        self.start = start

    def at(self, b, k):
        return b * self.per + k + self.start

    def check(self):
        assert self.given == self.per, (self.name, self.given, self.per)


def build_program(nc, x, fw, lw, aw, wo, cst, cols, rows, bexp, out):
    with ExitStack() as ctx:
        def sb(name, shape, dt=F32):
            return ctx.enter_context(nc.sbuf_tensor(name, shape, dt))

        def sem(name):
            return ctx.enter_context(nc.semaphore(name))

        def sig(name, per=1, start=0):
            return Signal(ctx, nc, name, per, start)

        fw_sb = sb("fw_sb", [P, NFW], F32R)
        wblk = sb("wblk", [P, 2, HID])
        lw_hi, lw_lo = sb("lw_hi", [P, NLW], F32R), sb("lw_lo", [P, NLW], F32R)
        gh_hi, gh_lo = sb("gh_hi", [P, 2 * D], F32R), sb("gh_lo", [P, 2 * D], F32R)
        wo_sb = sb("wo_sb", [P, KM * D])
        cst_sb = sb("cst_sb", [P, NCST])
        sel_r = sb("sel_r", [P, 4 * P], F32R)
        ones_r = sb("ones_r", [1, P], F32R)
        cols_sb = sb("cols_sb", [P, NCOL])
        rows_sb = sb("rows_sb", [P, 4 * D + E])
        bexp_sb = sb("bexp_sb", [NT * E, NT * D])
        decay = sb("decay", [P, 3 * KM])
        flags = sb("flags", [P, 8])
        iflag = sb("iflag", [P, 2], I32)
        ident, ones = cst_sb[:, CI:CI + P], cst_sb[:, CO:CO + P]

        xres = sb("xres", [P, NT, D])
        xnext = sb("xnext", [P, NT, D])
        xn = sb("xn", [P, NT * D])
        xt_hi, xt_lo = sb("xt_hi", [P, S], F32R), sb("xt_lo", [P, S], F32R)
        spl = sb("spl", [P, 4, S], F32R)
        big = sb("big", [P, 2, 4, S])
        kz = sb("kz", [P, GH, S], F32R)
        hid = sb("hid", [P, 2, 2, KM, CH], F32R)
        wk = sb("wk", [P, 4 * S])
        vaug = sb("vaug", [P, NT * HM * (HDM + 1) + QUAD])
        st = sb("st", [P, NT * 18])
        sm = sb("sm", [P, 12, NT * E])
        mx = sb("mx", [P, NT])
        negT = sb("negT", [NT, P], F32R)
        ct = sb("ct", [NT * E, P])
        bias_m = sb("bias_m", [P, HM])
        qk_max = sb("qk_max", [P, 4])
        mbuf = sb("mbuf", [P, P])
        mrow = sb("mrow", [P, 1])

        bn = st[:, 0:NT * 6].rearrange("p (t k) -> p t k", k=6)
        lnw = st[:, NT * 6:NT * 10].rearrange("p (k t) -> p k t", k=4)
        mean, var, rstd, half, mean1, var1, rstd1, shift1 = (st[:, NT * i:NT * (i + 1)] for i in range(10, 18))
        xn0 = big[:, 1, 2, :].rearrange("p (t d) -> p t d", d=D)
        xnv = xn[:, :].rearrange("p (t d) -> p t d", d=D)
        att, g2, fin, moe = (big[:, 0, i, :].rearrange("p (t d) -> p t d", d=D) for i in range(4))

        def hidden(buf, part, kk):
            if buf < 2:
                return hid[:, buf, part, kk, :]
            return spl[:, 2 * part + kk // 2, (kk % 2) * CH:(kk % 2 + 1) * CH]

        s_nat = wk[:, 0:S]
        act32 = [wk[:, S + i * CH:S + (i + 1) * CH] for i in range(3)]
        uaug = wk[:, S + 3 * CH:S + 3 * CH + NT * (D + 1)].rearrange("p (t n) -> p t n", n=D + 1)
        negrow = spl[0:1, 2, :]
        vaug4 = vaug[:, 0:NT * HM * (HDM + 1)].rearrange("p (t h n) -> p t h n", t=NT, n=HDM + 1)
        q1, v1 = big[:, 0], big[:, 1]
        q_st, k_st = hid[:, 0].rearrange("p a k n -> p (a k n)").rearrange("p (g n) -> p g n", g=NG), \
            hid[:, 1].rearrange("p a k n -> p (a k n)").rearrange("p (g n) -> p g n", g=NG)
        prob = big
        gT = big[:, 0, 0, :]

        ps = ctx.enter_context(nc.psum_tensor("ps", [P, 8, CH], F32))

        wblk_in, wblk_used = sig("wblk_in", 16 * len(W_BLOCKS)), sig("wblk_used", len(W_BLOCKS), 1)
        loaded, bexp_in = sem("loaded"), sem("bexp_in")
        setup_v, setup_a, setup_p = sem("setup_v"), sem("setup_a"), sem("setup_p")

        half_set = sem("half_set")
        x_in = sig("x_in", 16)
        chain = sig("chain", 181, 1)
        xT_mm, x_hi, x_lo = sig("xT_mm", 4), sig("x_hi", 4), sig("x_lo", 4)
        r_mm, r_hi, r_lo = sig("r_mm", 2), sig("r_hi", 2), sig("r_lo", 2)
        u_mm, u_ok = sig("u_mm", 2), sig("u_ok", 2)
        max_mm, row_max = sig("max_mm", NT), sig("row_max", NT)
        maxT, neg_ok, negrow_in = sig("maxT"), sig("neg_ok"), sig("negrow_in", 16)
        l1_mm, l1_act, hid_hi, hid_lo = sig("l1_mm", 16), sig("l1_act", 8), sig("hid_hi", 24), sig("hid_lo", 24)
        sc_mm, sc_exp = sig("sc_mm", 16), sig("sc_exp", 16)
        pv_mm, pv_norm = sig("pv_mm", NT), sig("pv_norm", NT)
        h_mm, h_act = sig("h_mm", 16), sig("h_act", 16)
        w3_mm, w3_act, gnat_mm, res_ok = sig("w3_mm", 2), sig("w3_act", 2), sig("gnat_mm", 2), sig("res_ok", 2)
        ln_ok, var_ok, rstd_ok = sig("ln_ok", 2), sig("var_ok", 3), sig("rstd_ok", 3)
        var1_ok, rstd1_ok, stats1_ok, xn0_ok = sig("var1_ok"), sig("rstd1_ok"), sig("stats1_ok"), sig("xn0_ok")
        qs_ok, gate_in, o_ok, sum_ok = sig("qs_ok", 8), sig("gate_in"), sig("o_ok", 2), sig("sum_ok", 2)
        qk_mm, q_copy, prod_ok = sig("qk_mm", 16), sig("q_copy", 8), sig("prod_ok", 8)
        hs_mm, hs_sub, hs_exp, attn_ok = sig("hs_mm", 2), sig("hs_sub"), sig("hs_exp"), sig("attn_ok")
        v_mm, v_copy, bc_mm, u1_ok = sig("v_mm", 8), sig("v_copy", 8), sig("bc_mm", 8), sig("u1_ok", 8)
        aug_ok, z_ok, o_mm = sig("aug_ok", 8), sig("z_ok", 8), sig("o_mm", 2)
        mq_mm, mq_hi, mq_lo = sig("mq_mm", 4), sig("mq_hi", 4), sig("mq_lo", 4)
        stk_mm, stk_ok = sig("stk_mm", 8), sig("stk_ok", 8)
        mv_mm, mv_ok, gate_mm = sig("mv_mm", 2), sig("mv_ok", 2), sig("gate_mm")
        g_sub, g_exp = sig("g_sub"), sig("g_exp")
        bnd_in, bnd_mm, bnd_ok = sig("bnd_in"), sig("bnd_mm"), sig("bnd_ok")
        kz_ok = sig("kz_ok", HM)
        gen_mm, gen_mx, gen_T, gen_add = (sig("gen_mm", UNITS), sig("gen_mx", UNITS), sig("gen_T", NG * NT),
                                          sig("gen_add", NG * NT))
        ms_mm, ms_exp = sig("ms_mm", UNITS), sig("ms_exp", UNITS)
        mp_mm, oT_ok = sig("mp_mm", NG * NT * 2), sig("oT_ok", NG)
        oN_mm, att_ok = sig("oN_mm", NT), sig("att_ok", NT)
        comb_ok, cT_mm, cT_ok, eb_mm = sig("comb_ok"), sig("cT_mm"), sig("cT_ok"), sig("eb_mm")
        eb_ok = sig("eb_ok")
        ex_mm, ex_ok, g2_ok, fin_ok = sig("ex_mm", NT), sig("ex_ok", NT, 1), sig("g2_ok", 2), sig("fin_ok", 2, 1)
        stored = sig("stored", 32, 1)

        def col(name, k=0):
            return cols_sb[:, COL[name] + k:COL[name] + k + 1]

        def up(signal, ins, n=1):
            signal.given += n
            return ins.then_inc(signal.sem, n)

        def layer_norm_stats(v, step, own, src, tiles, mean_, eps):
            tl = slice(tiles[0], tiles[-1] + 1)
            for t in tiles:
                step(v.bn_stats(bn[:, t, :], src[:, t, :]))
            own()
            step(v.tensor_tensor(lnw[:, 0, tl], bn[:, tl, 1], bn[:, tl, 4], ALU.add))
            step(v.tensor_tensor(lnw[:, 1, tl], bn[:, tl, 1], bn[:, tl, 4], ALU.subtract))
            step(v.tensor_tensor(lnw[:, 2, tl], bn[:, tl, 2], bn[:, tl, 5], ALU.add))
            own()
            step(v.tensor_scalar(mean_[:, tl], lnw[:, 0, tl], 0.5, None, ALU.mult))
            step(v.scalar_tensor_tensor(lnw[:, 3, tl], lnw[:, 1, tl], 0.25, lnw[:, 1, tl], ALU.mult, ALU.mult))
            step(v.tensor_scalar(lnw[:, 2, tl], lnw[:, 2, tl], 1.0 / D, eps, ALU.mult, ALU.add))
            own()

        def var_terms(tiles):
            tl = slice(tiles[0], tiles[-1] + 1)
            return lnw[:, 2, tl], lnw[:, 3, tl]

        block = ctx.enter_context(nc.Block())

        @block.sync
        def _(sp):
            def load_x(i):
                return sp.dma_start(xnext[:, :, :], x[bass.ds(i, 1)].rearrange("o (t p) d -> p (o t) d", p=P))

            load_x(0).then_inc(x_in.sem, 16)
            sp.dma_start(cst_sb[:, :], cst).then_inc(loaded, 16)
            sp.dma_start(cols_sb[:, :], cols).then_inc(loaded, 16)
            sp.dma_start(xn[:, 0:5 * D], aw).then_inc(loaded, 16)
            bigf = big[:, :, :, :].rearrange("p a g n -> p (a g n)")
            sp.dma_start(bigf[:, 0:NFW], fw).then_inc(loaded, 16)
            sp.dma_start(wk[:, 0:NLW], lw).then_inc(loaded, 16)
            sp.dma_start(wo_sb[:, :], wo).then_inc(loaded, 16)
            sp.dma_start(rows_sb[:, :], rows).then_inc(loaded, 16)
            sp.wait_ge(setup_v, 1)
            for t in range(NT):
                sp.dma_start(bexp_sb[E * t:E * (t + 1), D * t:D * (t + 1)], bexp).then_inc(bexp_in, 16)
            sp.wait_ge(setup_v, SETUP)
            wide = sp.value_load(iflag[0:1, 0:1], min_val=0, max_val=1)

            def weight_blocks(b, first, last):
                for n_ in range(first, last):
                    if n_ >= 2:
                        sp.wait_ge(wblk_used.sem, wblk_used.at(b, n_ - 1))
                    else:
                        sp.wait_ge(wblk_used.sem, wblk_used.at(b, 0))
                    at = W_BLOCKS[n_] * HID
                    sp.dma_start(wblk[:, n_ % 2, :], fw[:, at:at + HID]).then_inc(wblk_in.sem, 16)

            with sp.Fori(0, B) as b:
                with sp.If(wide > 0):
                    weight_blocks(b, 0, 2)
                sp.wait_ge(neg_ok.sem, neg_ok.at(b, 1))
                up(negrow_in, sp.dma_start(negrow[:, :].bitcast(F32), negT[:, :].bitcast(F32)), 16)
                with sp.If(wide > 0):
                    weight_blocks(b, 2, len(W_BLOCKS))
                wblk_in.given = wblk_in.per
                sp.wait_ge(res_ok.sem, res_ok.at(b, 2))
                up(x_in, load_x(b + 1), 16)
                for c in range(NCH):
                    sp.wait_ge(fin_ok.sem, fin_ok.at(b, c + 1))
                    o = out[bass.ds(b, 1)].rearrange("o (t p) d -> p (o t) d", p=P)
                    up(stored, sp.dma_start(o[:, c * TPC:(c + 1) * TPC, :], fin[:, c * TPC:(c + 1) * TPC, :]), 16)
            sp.wait_ge(x_in.sem, x_in.at(B, 16))
            sp.wait_ge(stored.sem, stored.at(B, 0))

        @block.vector
        def _(v):
            n = [0]

            def done(ins):
                ins.then_inc(setup_v, 1)
                n[0] += 1

            done(v.memset(bexp_sb[:, :], 0.0))
            v.wait_ge(x_in.sem, 16)
            layer_norm_stats(v, done, lambda: v.wait_ge(setup_v, n[0]), xnext, range(NT), mean1, LN_EPS)
            v.tensor_tensor(var1, *var_terms(range(NT)), ALU.add).then_inc(var1_ok.sem, 1)
            v.wait_ge(rstd1_ok.sem, 1)
            v.scalar_tensor_tensor(shift1, mean1, -1.0, rstd1, ALU.mult, ALU.mult).then_inc(stats1_ok.sem, 1)
            v.wait_ge(loaded, 16 * 7)
            bigf = big[:, :, :, :].rearrange("p a g n -> p (a g n)")
            lwf = wk[:, :]
            done(v.tensor_copy(fw_sb[:, :], bigf[:, 0:NFW]))
            done(v.tensor_copy(lw_hi[:, :], lwf[:, 0:NLW]))
            v.wait_ge(setup_v, NORM + 3)
            done(v.tensor_tensor(bigf[:, 0:NFW], bigf[:, 0:NFW], fw_sb[:, :].bitcast(F32), ALU.subtract))
            done(v.tensor_tensor(lw_lo[:, :], lwf[:, 0:NLW], lw_hi[:, :].bitcast(F32), ALU.subtract))
            v.wait_ge(setup_v, NORM + 5)
            done(v.tensor_reduce(flags[:, 0:1], bigf[:, 0:NFW], AX.X, ALU.max, apply_absolute_value=True))
            done(v.memset(vaug[:, :], 0.0))
            done(v.memset(mbuf[:, :], 0.0))
            v.wait_ge(setup_v, NORM + 8)
            done(v.memset(vaug4[:, :, :, HDM:HDM + 1], 1.0))
            done(v.tensor_copy(sel_r[:, :], cst_sb[:, CSEL:CSEL + 4 * P]))
            v.wait_ge(half_set, 2)
            for g in range(GH):
                done(v.tensor_copy(kz[:, g, :], big[:, 1, 3, :]))
            done(v.tensor_copy(ones_r[:, :], cst_sb[0:1, CO:CO + P]))
            v.wait_ge(setup_a, 1)
            done(v.tensor_scalar(decay[:, KM:2 * KM], decay[:, 0:KM], -1.0, 1.0, ALU.mult, ALU.add))
            v.wait_ge(setup_v, NORM + GH + 12)
            done(v.tensor_tensor(decay[:, 2 * KM:3 * KM], decay[:, KM:2 * KM], cols_sb[:, COL["bv"]:COL["bv"] + KM], ALU.mult))
            v.wait_ge(setup_p, 1)
            done(v.tensor_copy(xn[:, 5 * D:6 * D], ps[:, 0, 0:D]))
            v.wait_ge(setup_p, 2)
            done(v.tensor_copy(gh_hi[:, :], ps[:, 1, 0:2 * D]))
            v.wait_ge(setup_v, NORM + GH + 15)
            done(v.tensor_tensor(gh_lo[:, :], ps[:, 1, 0:2 * D], gh_hi[:, :].bitcast(F32), ALU.subtract))
            v.wait_ge(setup_p, 3)
            done(v.tensor_scalar(iflag[:, 0:1], ps[:, 2, 0:1], 0.0, None, ALU.is_gt))
            v.wait_ge(setup_v, NORM + GH + 17)

            with v.Fori(0, B) as b:
                k = [0]

                def step(ins):
                    k[0] += 1
                    up(chain, ins)

                def own(but=0):
                    v.wait_ge(chain.sem, chain.at(b, k[0] - but))

                def normalise(src, dst, tiles):
                    for t in tiles:
                        ins = v.tensor_scalar(dst[:, t, :], src[:, t, :], mean[:, t:t + 1], rstd[:, t:t + 1],
                                              ALU.subtract, ALU.mult)
                        if t < tiles[-1]:
                            step(ins)
                    return ins

                def split_rest(lo, hi, bank, c, sig_mm, n_mm, sig_hi, sig_lo):
                    v.wait_ge(sig_mm.sem, sig_mm.at(b, n_mm))
                    v.wait_ge(sig_hi.sem, sig_hi.at(b, n_mm))
                    up(sig_lo, v.tensor_tensor(lo[:, c * CH:(c + 1) * CH], ps[:, bank, :],
                                               hi[:, c * CH:(c + 1) * CH].bitcast(F32), ALU.subtract))

                def split_hidden(n_, buf, m):
                    src = act32[n_ % 3]
                    up(hid_hi, v.tensor_copy(hidden(buf, 0, m), src))
                    v.wait_ge(hid_hi.sem, hid_hi.at(b, n_ + 1))
                    up(hid_lo, v.tensor_tensor(hidden(buf, 1, m), src, hidden(buf, 0, m).bitcast(F32), ALU.subtract))

                own()
                v.wait_ge(fin_ok.sem, fin_ok.at(b, 0))
                for c in range(NCH):
                    split_rest(xt_lo, xt_hi, c, c, xT_mm, c + 1, x_hi, x_lo)
                for c in range(NCH):
                    split_rest(spl[:, 1], spl[:, 0], 2 + c, c, r_mm, c + 1, r_hi, r_lo)
                for t in range(NT):
                    v.wait_ge(max_mm.sem, max_mm.at(b, t + 1))
                    bank = 6 if t % 2 == 0 else 0
                    up(row_max, v.tensor_reduce(mx[:, t:t + 1], ps[:, bank:bank + 2, :], AX.XY, ALU.max))
                step(v.memset(uaug[:, :, D:D + 1], 1.0))
                v.wait_ge(maxT.sem, maxT.at(b, 1))
                up(neg_ok, v.tensor_scalar(negT[:, :], ps[0:NT, 6, 0:P], -1.0, None, ALU.mult))

                def gate_units(c):
                    for m in range(KM):
                        u = c * KM + m
                        v.wait_ge(l1_mm.sem, l1_mm.at(b, 2 * u + 2))
                        v.wait_ge(l1_act.sem, l1_act.at(b, u + 1))
                        n_ = 8 * c + m
                        h_ = act32[n_ % 3]
                        step(v.scalar_tensor_tensor(h_, ps[:, L1_BANKS[c][m % 2] + 1, :], col("w2s", m), h_, ALU.mult, ALU.mult))
                        own()
                        split_hidden(n_, 0, m)

                def act_units(first, first_hid, buf):
                    for m in range(KM):
                        v.wait_ge(h_act.sem, h_act.at(b, first + m + 1))
                        split_hidden(first_hid + m, buf, m)

                def residual(c):
                    v.wait_ge(gnat_mm.sem, gnat_mm.at(b, c + 1))
                    own()
                    sl = slice(c * CH, (c + 1) * CH)
                    step(v.tensor_tensor(s_nat[:, sl], s_nat[:, sl], ps[:, 6 + c, :], ALU.mult))
                    own()
                    flat = lambda a_: a_[:, :, :].rearrange("p t d -> p (t d)")[:, sl]
                    up(res_ok, v.tensor_tensor(flat(xres), flat(xnext), s_nat[:, sl], ALU.add))
                    v.wait_ge(res_ok.sem, res_ok.at(b, c + 1))

                gate_units(0)
                for t in range(NT):
                    v.wait_ge(pv_mm.sem, pv_mm.at(b, t + 1))
                    o = ps[:, 4 + t % 2, 0:D + 1]
                    step(v.reciprocal(mrow[:, 0:1], o[:, D:D + 1]))
                    own()
                    up(pv_norm, v.tensor_scalar(s_nat[:, t * D:(t + 1) * D], o[:, 0:D], mrow[:, 0:1], None, ALU.mult))
                    v.wait_ge(pv_norm.sem, pv_norm.at(b, t + 1))
                act_units(0, 4, 1)
                gate_units(1)
                act_units(4, 12, 2)
                act_units(8, 16, 1)

                def block_norm(c):
                    tiles = range(c * TPC, (c + 1) * TPC)
                    layer_norm_stats(v, step, own, xres, tiles, mean, LN_EPS)
                    up(var_ok, v.tensor_tensor(var[:, tiles[0]:tiles[-1] + 1], *var_terms(tiles), ALU.add))
                    v.wait_ge(rstd_ok.sem, rstd_ok.at(b, c + 1))
                    up(ln_ok, normalise(xres, xnv, tiles))

                residual(0)
                block_norm(0)
                act_units(12, 20, 0)
                split_rest(xt_lo, xt_hi, 6, 0, xT_mm, 3, x_hi, x_lo)
                residual(1)
                block_norm(1)

                def products(c):
                    for m in range(KM):
                        u = c * KM + m
                        v.wait_ge(qk_mm.sem, qk_mm.at(b, 2 * u + 2))
                        v.wait_ge(q_copy.sem, q_copy.at(b, u + 1))
                        up(prod_ok, v.scalar_tensor_tensor(wk[:, u * CH:(u + 1) * CH], ps[:, 2 * (u % 3) + 1, :], col("bk", m),
                                                           q1[:, m, c * CH:(c + 1) * CH], ALU.add, ALU.mult))

                products(0)
                split_rest(xt_lo, xt_hi, 7, 1, xT_mm, 4, x_hi, x_lo)
                products(1)

                w3d = lambda i: sm[:, i, :].rearrange("p (t e) -> p t e", e=E)
                over_e = lambda i: sm[:, i, 0:NT].unsqueeze(2).broadcast_to([P, NT, E])

                def softmax8_shift(src, shifted):
                    step(v.tensor_reduce(sm[:, 0, 0:NT], src, AX.X, ALU.max))
                    own()
                    up(shifted, v.tensor_tensor(w3d(1), src, over_e(0), ALU.subtract))

                def softmax8_divide(exp_done):
                    v.wait_ge(exp_done.sem, exp_done.at(b, 1))
                    step(v.tensor_reduce(sm[:, 3, 0:NT], w3d(2), AX.X, ALU.add))
                    own()
                    step(v.reciprocal(sm[:, 4, 0:NT], sm[:, 3, 0:NT]))
                    own()
                    return v.tensor_tensor(w3d(5), w3d(2), over_e(4), ALU.mult)

                v.wait_ge(hs_mm.sem, hs_mm.at(b, 2))
                step(v.tensor_copy(sm[:, 6, :].rearrange("p (c n) -> p c n", c=2), ps[:, 6:8, 0:TPC * H1]))
                own()
                softmax8_shift(w3d(6), hs_sub)
                for i in range(4):
                    j, c = i // 2, i % 2
                    v.wait_ge(mq_hi.sem, mq_hi.at(b, i + 1))
                    up(mq_lo, v.scalar_tensor_tensor(spl[:, 2 * j + 1, c * CH:(c + 1) * CH], ps[:, MQ_BANKS[i], :],
                                                     col(("mbq", "mbk")[j]), spl[:, 2 * j, c * CH:(c + 1) * CH].bitcast(F32),
                                                     ALU.add, ALU.subtract))
                    if c == 1:
                        step(v.tensor_reduce(qk_max[:, j:j + 1], spl[:, 2 * j, :].bitcast(F32), AX.X, ALU.max,
                                             apply_absolute_value=True))
                    if i == 1:
                        up(attn_ok, softmax8_divide(hs_exp))
                own()
                step(v.scalar_tensor_tensor(qk_max[:, 2:3], qk_max[:, 0:1], -1.002 / HDM ** 0.5, qk_max[:, 1:2],
                                            ALU.mult, ALU.mult))
                own()
                up(bnd_in, v.tensor_scalar(sm[:, 7, 0:HM], cst_sb[:, CBM:CBM + HM], qk_max[:, 2:3], None, ALU.mult))
                for c in range(NCH):
                    v.wait_ge(mv_mm.sem, mv_mm.at(b, c + 1))
                    up(mv_ok, v.tensor_tensor(
                        vaug4[:, c * TPC:(c + 1) * TPC, :, 0:HDM],
                        ps[:, 2 + c, :].rearrange("p (t h n) -> p t h n", t=TPC, n=HDM),
                        rows_sb[:, 3 * D:4 * D].rearrange("p (h n) -> p h n", n=HDM).unsqueeze(1)
                        .broadcast_to([P, TPC, HM, HDM]), ALU.add))
                v.wait_ge(gate_mm.sem, gate_mm.at(b, 1))
                up(gate_in, v.tensor_tensor(w3d(6), ps[:, 6, 0:NT * E].rearrange("p (t e) -> p t e", e=E),
                                            rows_sb[:, 4 * D:4 * D + E].unsqueeze(1).broadcast_to([P, NT, E]), ALU.add))
                v.wait_ge(bnd_mm.sem, bnd_mm.at(b, 1))
                step(v.tensor_reduce(flags[:, 1:2], ps[:, 7, 0:HM], AX.X, ALU.min))
                own()
                step(v.tensor_scalar(flags[:, 2:3], flags[:, 1:2], -SAFE, None, ALU.is_ge))
                step(v.tensor_scalar(iflag[:, 1:2], flags[:, 1:2], -SAFE, None, ALU.is_lt))
                own()
                up(bnd_ok, v.tensor_scalar(bias_m[:, :], ps[:, 7, 0:HM], flags[:, 2:3], None, ALU.mult))
                for u in range(NCH * KM):
                    c, m = u // KM, u % KM
                    sl = slice(c * CH, (c + 1) * CH)
                    v.wait_ge(bc_mm.sem, bc_mm.at(b, u + 1))
                    up(u1_ok, v.tensor_tensor(v1[:, m, sl], v1[:, m, sl], ps[:, u % 4, :], ALU.mult))
                    v.wait_ge(u1_ok.sem, u1_ok.at(b, u + 1))
                    z = wk[:, m * S + c * CH:m * S + (c + 1) * CH]
                    init = 0.0 if c == 0 else v1[:, m, c * CH - 1:c * CH]
                    step(v.tensor_tensor_scan(v1[:, m, sl], decay[:, m:m + 1].broadcast_to([P, CH]), v1[:, m, sl], init,
                                              ALU.mult, ALU.add))
                    own()
                    up(qs_ok, v.tensor_tensor(z, q1[:, m, sl], v1[:, m, sl], ALU.mult))

                def load_kz(g4, g):
                    rg = slice(QUAD * g, QUAD * (g + 1))
                    up(kz_ok, v.tensor_copy(kz[rg, g, :], k_st[rg, g4, :].bitcast(F32)))

                v.wait_ge(bnd_ok.sem, bnd_ok.at(b, 1))
                v.wait_ge(stk_ok.sem, stk_ok.at(b, 2 * NG))
                for g in range(GH):
                    load_kz(0, g)
                need_max = v.value_load(iflag[0:1, 1:2], min_val=0, max_val=1)
                with v.If(need_max > 0):
                    for gt in range(NG * NT):
                        g4, t = gt // NT, gt % NT
                        for g in range(GH):
                            n_ = gt * GH + g
                            v.wait_ge(gen_mm.sem, gen_mm.at(b, n_ + 1))
                            if gt and g == 0:
                                v.wait_ge(gen_T.sem, gen_T.at(b, gt))
                            v.tensor_reduce(mbuf[:, QUAD * g + 3 * HDM:QUAD * g + 3 * HDM + 1],
                                            ps[:, (0 if n_ % 2 == 0 else 2):(2 if n_ % 2 == 0 else 4), :],
                                            AX.XY, ALU.max, negate=True).then_inc(gen_mx.sem, 1)
                        v.wait_ge(gen_T.sem, gen_T.at(b, gt + 1))
                        qs = q_st[:, g4, t * P:(t + 1) * P]
                        v.tensor_tensor(qs, qs.bitcast(F32), ps[:, 6 + gt % 2, 0:P], ALU.add).then_inc(gen_add.sem, 1)
                with v.Else():
                    v.sem_inc(gen_mx.sem, gen_mx.per)
                    v.sem_inc(gen_add.sem, gen_add.per)
                gen_mx.given, gen_add.given = gen_mx.per, gen_add.per

                v.wait_ge(z_ok.sem, z_ok.at(b, 8))
                for c in range(NCH):
                    v.wait_ge(o_mm.sem, o_mm.at(b, c + 1))
                    up(o_ok, v.tensor_tensor(xnv[:, c * TPC:(c + 1) * TPC, :], ps[:, 4 + c, :].rearrange("p (t d) -> p t d", d=D),
                                             rows_sb[:, 0:D].unsqueeze(1).broadcast_to([P, TPC, D]), ALU.add))
                v.wait_ge(o_ok.sem, o_ok.at(b, 2))
                every = range(NT)
                layer_norm_stats(v, step, own, xnv, every, mean, LN1_EPS)
                up(var_ok, v.tensor_tensor(var, *var_terms(every), ALU.add))
                softmax8_shift(w3d(6), g_sub)
                step(softmax8_divide(g_exp))
                own()
                gate, left = w3d(5), sm[:, 8, :]
                for r in range(2):
                    src = gate if r == 0 else w3d(8)
                    step(v.tensor_reduce(sm[:, 0, 0:NT], src, AX.X, ALU.max))
                    own()
                    step(v.tensor_tensor(w3d(1), src, over_e(0), ALU.is_ge))
                    own()
                    step(v.tensor_tensor_scan(sm[:, 3, :], cst_sb[:, CMASK:CMASK + NT * E], sm[:, 1, :], 0.0,
                                              ALU.mult, ALU.add))
                    own()
                    step(v.scalar_tensor_tensor(sm[:, 9 + r, :], sm[:, 3, :], 1.0, sm[:, 1, :], ALU.is_equal, ALU.mult))
                    own()
                    if r == 0:
                        step(v.scalar_tensor_tensor(left, sm[:, 9, :], -4.0, sm[:, 5, :], ALU.mult, ALU.add))
                        own()
                step(v.tensor_tensor(sm[:, 9, :], sm[:, 9, :], sm[:, 10, :], ALU.add))
                own()
                up(comb_ok, v.tensor_tensor(sm[:, 11, :], sm[:, 5, :], sm[:, 9, :], ALU.mult))
                v.wait_ge(rstd_ok.sem, rstd_ok.at(b, 3))
                step(normalise(xnv, xnv, every))
                own()
                step(v.tensor_tensor(xnv, xnv, rows_sb[:, D:2 * D].unsqueeze(1).broadcast_to([P, NT, D]), ALU.mult))
                own()
                step(v.tensor_tensor(xnv, xnv, rows_sb[:, 2 * D:3 * D].unsqueeze(1).broadcast_to([P, NT, D]), ALU.add))
                v.wait_ge(x_in.sem, x_in.at(b, 32))
                layer_norm_stats(v, step, own, xnext, every, mean1, LN_EPS)
                up(var1_ok, v.tensor_tensor(var1, *var_terms(every), ALU.add))
                v.wait_ge(rstd1_ok.sem, rstd1_ok.at(b, 2))
                up(stats1_ok, v.scalar_tensor_tensor(shift1, mean1, -1.0, rstd1, ALU.mult, ALU.mult))
                for g4 in range(NG):
                    if g4 < NG - 1:
                        for g in range(GH):
                            v.wait_ge(ms_mm.sem, ms_mm.at(b, ((g4 + 1) * NT - 1) * GH + g + 1))
                            load_kz(g4 + 1, g)
                    v.wait_ge(mp_mm.sem, mp_mm.at(b, (g4 + 1) * NT * 2))
                    up(oT_ok, v.tensor_copy(wk[:, g4 * S:(g4 + 1) * S].rearrange("p (h n) -> p h n", n=CH), ps[:, 4:6, :]))
                own()
                for t in range(NT):
                    v.wait_ge(oN_mm.sem, oN_mm.at(b, t + 1))
                    o4 = ps[:, ON_BANKS[t % 4], :].rearrange("p (h n) -> p h n", n=QUAD)
                    step(v.reciprocal(sm[:, t % 2, 0:HM], o4[:, :, HDM]))
                    own()
                    up(att_ok, v.tensor_tensor(att[:, t, :].rearrange("p (h n) -> p h n", n=HDM), o4[:, :, 0:HDM],
                                               sm[:, t % 2, 0:HM].unsqueeze(2).broadcast_to([P, HM, HDM]), ALU.mult))
                    if t:
                        v.wait_ge(att_ok.sem, att_ok.at(b, t))
                v.wait_ge(eb_ok.sem, eb_ok.at(b, 1))
                v.wait_ge(att_ok.sem, att_ok.at(b, NT))

                def finish_sum(c):
                    tl = slice(c * TPC, (c + 1) * TPC)
                    v.wait_ge(ex_ok.sem, ex_ok.at(b, (c + 1) * TPC))
                    own()
                    up(sum_ok, v.tensor_tensor(att[:, tl, :], att[:, tl, :], moe[:, tl, :], ALU.add))

                def finish(c):
                    tl = slice(c * TPC, (c + 1) * TPC)
                    v.wait_ge(g2_ok.sem, g2_ok.at(b, c + 1))
                    step(v.tensor_tensor(g2[:, tl, :], g2[:, tl, :], xnv[:, tl, :], ALU.mult))
                    own()
                    up(fin_ok, v.tensor_tensor(fin[:, tl, :], g2[:, tl, :], xres[:, tl, :], ALU.add))

                for t in range(NT):
                    v.wait_ge(ex_mm.sem, ex_mm.at(b, t + 1))
                    for e in range(E):
                        acc = (att, moe)[e % 2][:, t, :]
                        if e >= 2:
                            own(1)
                        ins = v.scalar_tensor_tensor(acc, ps[:, EX_BANKS[t % 3] + e // 4, (e % 4) * D:(e % 4 + 1) * D],
                                                     sm[:, 11, t * E + e:t * E + e + 1], acc, ALU.mult, ALU.add)
                        if e < E - 1:
                            step(ins)
                    up(ex_ok, ins)
                    if t == TPC - 1:
                        finish_sum(0)
                    if t == NT - 2:
                        finish(0)
                finish_sum(1)
                finish(1)

        @block.gpsimd
        def _(g_):
            g_.memset(half, -0.5).then_inc(half_set, 1)
            g_.memset(big[:, 1, 3, :], 0.0).then_inc(half_set, 1)
            g_.wait_ge(half_set, 2)
            g_.wait_ge(var1_ok.sem, 1)
            g_.tensor_tensor(rstd1, var1, half, ALU.pow).then_inc(rstd1_ok.sem, 1)
            with g_.Fori(0, B) as b:
                for c in range(NCH):
                    tl = slice(c * TPC, (c + 1) * TPC)
                    g_.wait_ge(var_ok.sem, var_ok.at(b, c + 1))
                    up(rstd_ok, g_.tensor_tensor(rstd[:, tl], var[:, tl], half[:, tl], ALU.pow))
                for u in range(NCH * KM):
                    c, m = u // KM, u % KM
                    z = wk[:, m * S + c * CH:m * S + (c + 1) * CH]
                    g_.wait_ge(qs_ok.sem, qs_ok.at(b, u + 1))
                    g_.wait_ge(aug_ok.sem, aug_ok.at(b, u + 1))
                    up(z_ok, g_.tensor_tensor(z, z, xn[:, (u % 2) * CH:(u % 2 + 1) * CH], ALU.add))

                g_.wait_ge(var_ok.sem, var_ok.at(b, 3))
                up(rstd_ok, g_.tensor_tensor(rstd, var, half, ALU.pow))
                g_.wait_ge(var1_ok.sem, var1_ok.at(b, 2))
                up(rstd1_ok, g_.tensor_tensor(rstd1, var1, half, ALU.pow))

        @block.scalar
        def _(a):
            def normalise_next(signal):
                for t in range(NT):
                    ins = a.activation(xn0[:, t, :], xnext[:, t, :], ACT.Identity, bias=shift1[:, t:t + 1],
                                       scale=rstd1[:, t:t + 1])
                ins.then_inc(signal, 1)

            for s_ in (chain, wblk_used, ex_ok, fin_ok, stored):
                a.sem_inc(s_.sem, s_.start)
            a.wait_ge(loaded, 16 * 7)
            a.activation(decay[:, 0:KM], cols_sb[:, COL["alpha"]:COL["alpha"] + KM], ACT.Sigmoid).then_inc(setup_a, 1)
            a.wait_ge(stats1_ok.sem, 1)
            normalise_next(xn0_ok.sem)
            a.wait_ge(setup_v, SETUP)
            with a.Fori(0, B) as b:
                def split_head(hi, bank, c, sig_mm, n_mm, sig_hi):
                    a.wait_ge(sig_mm.sem, sig_mm.at(b, n_mm))
                    up(sig_hi, a.activation(hi[:, c * CH:(c + 1) * CH], ps[:, bank, :], ACT.Copy))

                for c in range(NCH):
                    split_head(xt_hi, c, c, xT_mm, c + 1, x_hi)
                for c in range(NCH):
                    split_head(spl[:, 0], 2 + c, c, r_mm, c + 1, r_hi)
                for c in range(NCH):
                    a.wait_ge(u_mm.sem, u_mm.at(b, c + 1))
                    up(u_ok, a.activation(uaug[:, c * TPC:(c + 1) * TPC, 0:D],
                                          ps[:, 4 + c, :].rearrange("p (t d) -> p t d", d=D), ACT.Copy))

                def silu_units(c):
                    for m in range(KM):
                        u = c * KM + m
                        a.wait_ge(l1_mm.sem, l1_mm.at(b, 2 * u + 1))
                        n_ = 8 * c + m
                        if n_ >= 3:
                            a.wait_ge(hid_lo.sem, hid_lo.at(b, n_ - 2))
                        up(l1_act, a.activation(act32[n_ % 3], ps[:, L1_BANKS[c][m % 2], :], ACT.Silu, scale=col("w1s", m)))

                def gelu_units(first, first_hid, name, banks):
                    for m in range(KM):
                        n_ = first_hid + m
                        a.wait_ge(h_mm.sem, h_mm.at(b, first + m + 1))
                        a.wait_ge(hid_lo.sem, hid_lo.at(b, n_ - 2))
                        up(h_act, a.activation(act32[n_ % 3], ps[:, banks[m], :], ACT.Gelu, scale=col(name, m)))

                def silu_g(c):
                    a.wait_ge(w3_mm.sem, w3_mm.at(b, c + 1))
                    up(w3_act, a.activation(gT[:, c * CH:(c + 1) * CH], ps[:, W3_BANKS[c], :], ACT.Silu, scale=col("w3s")))

                silu_units(0)
                a.wait_ge(fin_ok.sem, fin_ok.at(b, 0))
                a.wait_ge(stored.sem, stored.at(b, 0))
                for n_ in range(2 * NT):
                    h, jt = n_ // NT, n_ % NT
                    a.wait_ge(sc_mm.sem, sc_mm.at(b, n_ + 1))
                    up(sc_exp, a.activation(big[:, h, jt // 2, (jt % 2) * CH:(jt % 2 + 1) * CH],
                                            ps[:, (0, 1, 6, 7)[n_ % 4], :], ACT.Exp))
                gelu_units(0, 4, "h1s", H_BANKS[0])
                silu_units(1)
                gelu_units(4, 12, "h2s", H_BANKS[1])
                gelu_units(8, 16, "h1s", H_BANKS[2])
                silu_g(0)
                gelu_units(12, 20, "h2s", H_BANKS[3])
                split_head(xt_hi, 6, 0, xT_mm, 3, x_hi)
                silu_g(1)

                def q_units(c):
                    for m in range(KM):
                        u = c * KM + m
                        a.wait_ge(qk_mm.sem, qk_mm.at(b, 2 * u + 1))
                        up(q_copy, a.activation(q1[:, m, c * CH:(c + 1) * CH], ps[:, 2 * (u % 3), :], ACT.Identity,
                                                bias=col("bq", m)))

                a.wait_ge(gnat_mm.sem, gnat_mm.at(b, 2))
                q_units(0)
                split_head(xt_hi, 7, 1, xT_mm, 4, x_hi)
                q_units(1)
                for i in range(4):
                    j, c = i // 2, i % 2
                    a.wait_ge(mq_mm.sem, mq_mm.at(b, i + 1))
                    up(mq_hi, a.activation(spl[:, 2 * j, c * CH:(c + 1) * CH], ps[:, MQ_BANKS[i], :], ACT.Identity,
                                           bias=col(("mbq", "mbk")[j])))
                    if i == 1:
                        a.wait_ge(hs_sub.sem, hs_sub.at(b, 1))
                        up(hs_exp, a.activation(sm[:, 2, :], sm[:, 1, :], ACT.Exp, scale=HD1 ** -0.5))
                for u in range(NCH * KM):
                    c, m = u // KM, u % KM
                    a.wait_ge(v_mm.sem, v_mm.at(b, u + 1))
                    up(v_copy, a.activation(v1[:, m, c * CH:(c + 1) * CH], ps[:, V_BANKS[u % 6], :], ACT.Identity,
                                            bias=decay[:, 2 * KM + m:2 * KM + m + 1], scale=decay[:, KM + m:KM + m + 1]))

                def sigmoid_unit(u):
                    c, m = u // KM, u % KM
                    if u >= 2:
                        a.wait_ge(z_ok.sem, z_ok.at(b, u - 1))
                    up(aug_ok, a.activation(xn[:, (u % 2) * CH:(u % 2 + 1) * CH], q1[:, m, c * CH:(c + 1) * CH], ACT.Sigmoid,
                                            scale=col("aug", m)))

                for i in range(2 * NG):
                    sigmoid_unit(i)
                    g4, j = i // 2, i % 2
                    a.wait_ge(stk_mm.sem, stk_mm.at(b, i + 1))
                    dst = (q_st, k_st)[j][:, g4, :].rearrange("p (h n) -> p h n", n=CH)
                    src = ps[:, STK_BANKS[j]:STK_BANKS[j] + 2, :]
                    if j == 0:
                        up(stk_ok, a.activation(dst, src, ACT.Copy))
                    else:
                        up(stk_ok, a.activation(dst, src, ACT.Identity, bias=col("row24")))
                a.wait_ge(bnd_ok.sem, bnd_ok.at(b, 1))
                for u in range(UNITS):
                    g4, jt, g = u // (NT * GH), (u // GH) % NT, u % GH
                    a.wait_ge(ms_mm.sem, ms_mm.at(b, u + 1))
                    if u == 0:
                        a.wait_ge(qs_ok.sem, qs_ok.at(b, 8))
                    if u >= 2 * GH:
                        a.wait_ge(mp_mm.sem, mp_mm.at(b, 2 * (u // GH - 1)))
                    pr = (0, 2, 6)[u % 3]
                    h = g4 * GH + g
                    up(ms_exp, a.activation(prob[:, jt % 2, g, :].rearrange("p (h n) -> p h n", n=CH), ps[:, pr:pr + 2, :],
                                            ACT.Exp, bias=bias_m[:, h:h + 1], scale=HDM ** -0.5))
                    if u == G_EXP_AT:
                        a.wait_ge(g_sub.sem, g_sub.at(b, 1))
                        up(g_exp, a.activation(sm[:, 2, :], sm[:, 1, :], ACT.Exp))
                a.wait_ge(cT_mm.sem, cT_mm.at(b, 1))
                up(cT_ok, a.activation(ct[:, :], ps[0:NT * E, 4, 0:P], ACT.Copy))
                a.wait_ge(stats1_ok.sem, stats1_ok.at(b, 2))
                a.wait_ge(eb_mm.sem, eb_mm.at(b, 1))
                up(eb_ok, a.activation(big[:, 0, 3, :].rearrange("p (h n) -> p h n", n=CH), ps[:, 4:6, :], ACT.Copy))
                normalise_next(xn0_ok.sem)
                xn0_ok.given += 1
                for c in range(NCH):
                    a.wait_ge(sum_ok.sem, sum_ok.at(b, c + 1))
                    up(g2_ok, a.activation(big[:, 0, 1, c * CH:(c + 1) * CH], big[:, 0, 0, c * CH:(c + 1) * CH], ACT.Silu))

        @block.tensor
        def _(t_):
            def mm(out_, lhsT, rhs, start, stop, **kw):
                return t_.matmul(out_, lhsT, rhs, start=start, stop=stop, **kw)

            def split3(out_, l_hi, l_lo, r_hi_, r_lo_, start=True, stop=True):
                mm(out_, l_hi, r_hi_, start, False)
                mm(out_, l_hi, r_lo_, False, False)
                return mm(out_, l_lo, r_hi_, False, stop)

            def full2(out_, w, r_hi_, r_lo_, start=True, stop=True):
                mm(out_, w, r_hi_.bitcast(F32), start, False)
                return mm(out_, w, r_lo_.bitcast(F32), False, stop)

            t_.wait_ge(loaded, 16 * 7)
            waT, wkk, wq, wv, wbT = (xn[:, i * D:(i + 1) * D] for i in range(5))
            mm(ps[:, 0, 0:D], waT, wkk, True, True).then_inc(setup_p, 1)
            mm(ps[:, 1, D:2 * D], wv, wbT, True, True)
            t_.wait_ge(setup_v, NORM + GH + 14)
            mm(ps[:, 1, 0:D], wq, xn[:, 5 * D:6 * D], True, True).then_inc(setup_p, 1)
            mm(ps[:, 2, 0:1], ones, flags[:, 0:1], True, True).then_inc(setup_p, 1)
            t_.wait_ge(setup_v, NORM + GH + 17)
            t_.wait_ge(bexp_in, 16 * NT)
            mm(ps[:, 3, 0:1], ones, flags[:, 0:1], True, True)
            wide = t_.value_load(iflag[0:1, 0:1], min_val=0, max_val=1)

            with t_.Fori(0, B) as b:
                def xT(c):
                    return xt_hi[:, c * CH:(c + 1) * CH], xt_lo[:, c * CH:(c + 1) * CH]

                def tok(t):
                    return xt_hi[:, t * P:(t + 1) * P], xt_lo[:, t * P:(t + 1) * P]

                def lwp(at, n=P):
                    return lw_hi[:, at:at + n], lw_lo[:, at:at + n]

                def transposes(src, bank, c):
                    for i in range(TPC):
                        ins = t_.transpose(ps[:, bank, i * P:(i + 1) * P], src[:, c * TPC + i, :], ident)
                    ins.then_inc(xT_mm.sem, 1)

                t_.wait_ge(xn0_ok.sem, xn0_ok.at(b, 1))
                t_.wait_ge(ex_ok.sem, ex_ok.at(b, 0))
                for c in range(NCH):
                    transposes(xn0, c, c)
                for c in range(NCH):
                    t_.wait_ge(x_lo.sem, x_lo.at(b, c + 1))
                    up(r_mm, split3(ps[:, 2 + c, :], gh_hi[:, 0:D], gh_lo[:, 0:D], *xT(c)))

                def row_scores(t):
                    bank = 6 if t % 2 == 0 else 0
                    if t >= 2:
                        t_.wait_ge(row_max.sem, row_max.at(b, t - 1))
                    for c in range(NCH):
                        ins = mm(ps[:, bank + c, :], spl[:, 0, t * P:(t + 1) * P], xT(c)[0], True, True)
                    ins.then_inc(max_mm.sem, 1)

                t_.wait_ge(r_hi.sem, r_hi.at(b, 2))
                for t in range(NT):
                    if t in (0, TPC):
                        row_scores(2 * t // TPC)
                        row_scores(2 * t // TPC + 1)
                    ins = split3(ps[:, 4 + t // TPC, (t % TPC) * D:(t % TPC + 1) * D], *tok(t), gh_hi[:, D:2 * D], gh_lo[:, D:2 * D])
                    if t % TPC == TPC - 1:
                        up(u_mm, ins)

                def l1_unit(c, m, general):
                    if m >= 2:
                        t_.wait_ge(hid_hi.sem, hid_hi.at(b, 8 * c + m - 1))
                    if general and m == 0:
                        t_.wait_ge(wblk_in.sem, wblk_in.at(b, 16 * (6 * c + 2)))
                    for i, base in enumerate((FW1, FW2)):
                        bank = ps[:, L1_BANKS[c][m % 2] + i, :]
                        w = slice(base + m * P, base + (m + 1) * P)
                        if general:
                            ins = full2(bank, wblk[:, i, m * P:(m + 1) * P], *xT(c))
                        else:
                            mm(bank, fw_sb[:, w], xT(c)[0], True, False)
                            ins = mm(bank, fw_sb[:, w], xT(c)[1], False, True)
                        ins.then_inc(l1_mm.sem, 1)
                    if general and m == KM - 1:
                        t_.drain().then_inc(wblk_used.sem, 2)

                def dense(base, width, buf, banks, first_hid, general, block, signal, mcount, between=None):
                    for kk in range(KM):
                        t_.wait_ge(hid_lo.sem, hid_lo.at(b, first_hid + kk + 1))
                        if general and (mcount > 1 or kk == 0):
                            t_.wait_ge(wblk_in.sem, wblk_in.at(b, 16 * (block + kk + 1)))
                        for m in range(mcount):
                            w = slice(base + kk * width + m * P, base + kk * width + (m + 1) * P)
                            o_ = ps[:, banks[m], :]
                            h_hi, h_lo = hidden(buf, 0, kk), hidden(buf, 1, kk)
                            if general:
                                at = kk * D if mcount == 1 else m * P
                                ins = full2(o_, wblk[:, (block + kk * (mcount > 1)) % 2, at:at + P], h_hi, h_lo, kk == 0, kk == KM - 1)
                            else:
                                mm(o_, fw_sb[:, w], h_hi, kk == 0, False)
                                ins = mm(o_, fw_sb[:, w], h_lo, False, kk == KM - 1)
                            if kk == KM - 1:
                                ins.then_inc(signal.sem, 1)
                        if general and (mcount > 1 or kk == KM - 1):
                            t_.drain().then_inc(wblk_used.sem, 1)
                        if between and kk == KM - 2:
                            between()

                def first_layer(general):
                    t_.wait_ge(r_lo.sem, r_lo.at(b, 2))
                    l1_unit(0, 0, general)
                    row_scores(4)
                    t_.wait_ge(u_ok.sem, u_ok.at(b, 2))
                    l1_unit(0, 1, general)
                    for t in range(5, NT):
                        row_scores(t)
                    t_.wait_ge(row_max.sem, row_max.at(b, NT))
                    t_.transpose(ps[0:NT, 6, 0:P], mx[:, :], ident).then_inc(maxT.sem, 1)
                    l1_unit(0, 2, general)
                    l1_unit(0, 3, general)

                with t_.If(wide > 0):
                    first_layer(True)
                with t_.Else():
                    first_layer(False)
                t_.wait_ge(neg_ok.sem, neg_ok.at(b, 1))
                t_.wait_ge(negrow_in.sem, negrow_in.at(b, 16))
                for n_ in range(2 * NT):
                    h, jt = n_ // NT, n_ % NT
                    if n_ >= 4:
                        t_.wait_ge(sc_exp.sem, sc_exp.at(b, n_ - 3))
                    bank = ps[:, (0, 1, 6, 7)[n_ % 4], :]
                    split3(bank, *tok(jt), spl[:, 0, h * CH:(h + 1) * CH], spl[:, 1, h * CH:(h + 1) * CH], True, False)
                    up(sc_mm, mm(bank, ones_r[:, :], negrow[:, h * CH:(h + 1) * CH], False, True))
                for t in range(NT):
                    if t >= 2:
                        t_.wait_ge(pv_norm.sem, pv_norm.at(b, t - 1))
                    h = t // TPC
                    if t % TPC == 0:
                        t_.wait_ge(sc_exp.sem, sc_exp.at(b, (h + 1) * NT))
                    if t == 0:
                        t_.wait_ge(hid_hi.sem, hid_hi.at(b, KM))
                    for jt in range(NT):
                        at = (jt % 2) * CH + (t % TPC) * P
                        ins = mm(ps[:, 4 + t % 2, 0:D + 1], big[:, h, jt // 2, at:at + P], uaug[:, jt, :], jt == 0, jt == NT - 1)
                    up(pv_mm, ins)

                def g_transposes(c):
                    t_.wait_ge(w3_act.sem, w3_act.at(b, c + 1))
                    for i in range(TPC):
                        ins = t_.transpose(ps[:, 6 + c, i * P:(i + 1) * P], gT[:, c * CH + i * P:c * CH + (i + 1) * P], ident)
                    ins.then_inc(gnat_mm.sem, 1)

                def mlp_rest(general):
                    dense(FH1, HID, 0, H_BANKS[0], 0, general, 2, h_mm, KM)
                    t_.wait_ge(pv_norm.sem, pv_norm.at(b, NT))
                    for m in range(KM):
                        l1_unit(1, m, general)
                    t_.wait_ge(h_act.sem, h_act.at(b, 4))
                    dense(FH2, HID, 1, H_BANKS[1], 4, general, 8, h_mm, KM)
                    t_.wait_ge(hid_hi.sem, hid_hi.at(b, 12))
                    dense(FH1, HID, 0, H_BANKS[2], 8, general, 12, h_mm, KM)
                    dense(FW3, D, 2, W3_BANKS[0:1], 12, general, 16, w3_mm, 1)
                    dense(FH2, HID, 1, H_BANKS[3], 16, general, 17, h_mm, KM, between=lambda: g_transposes(0))
                    t_.wait_ge(ln_ok.sem, ln_ok.at(b, 1))
                    transposes(xnv, 6, 0)
                    dense(FW3, D, 0, W3_BANKS[1:2], 20, general, 21, w3_mm, 1)

                with t_.If(wide > 0):
                    mlp_rest(True)
                with t_.Else():
                    mlp_rest(False)

                for u in range(NCH * KM):
                    c, m = u // KM, u % KM
                    if u == 2:
                        g_transposes(1)
                    if u == KM:
                        t_.wait_ge(ln_ok.sem, ln_ok.at(b, 2))
                        transposes(xnv, 7, 1)
                    if m == 0:
                        t_.wait_ge(x_lo.sem, x_lo.at(b, 3 + c))
                    if u >= 3:
                        t_.wait_ge(prod_ok.sem, prod_ok.at(b, u - 2))
                    for i, base in enumerate((LQ, LK)):
                        up(qk_mm, split3(ps[:, 2 * (u % 3) + i, :], *lwp(base + m * P), *xT(c)))
                for s_ in (wblk_used, l1_mm, h_mm, w3_mm, gnat_mm, maxT, max_mm, xT_mm):
                    s_.given = s_.per

                def head_scores(c):
                    t_.wait_ge(prod_ok.sem, prod_ok.at(b, KM * (c + 1)))
                    for i in range(TPC):
                        for m in range(KM):
                            ins = mm(ps[:, 6 + c, i * H1:(i + 1) * H1], wk[:, (c * KM + m) * CH + i * P:(c * KM + m) * CH + (i + 1) * P],
                                     cst_sb[:, CHD + m * H1:CHD + (m + 1) * H1], m == 0, m == KM - 1)
                    up(hs_mm, ins)

                head_scores(0)
                head_scores(1)
                for i in range(4):
                    j, c = i // 2, i % 2
                    up(mq_mm, split3(ps[:, MQ_BANKS[i], :], *lwp(LM + j * D), *xT(c)))
                for t in range(NT):
                    ins = split3(ps[:, 2 + t // TPC, (t % TPC) * D:(t % TPC + 1) * D], *tok(t), *lwp(LM + 2 * D, D))
                    if t % TPC == TPC - 1:
                        up(mv_mm, ins)
                for u in range(NCH * KM):
                    c, m = u // KM, u % KM
                    if u == 0:
                        t_.wait_ge(mq_lo.sem, mq_lo.at(b, 2))
                    if u == 2:
                        t_.wait_ge(mq_lo.sem, mq_lo.at(b, 4))
                    if u == 4:
                        t_.wait_ge(mv_ok.sem, mv_ok.at(b, 2))
                    if u >= 6:
                        t_.wait_ge(v_copy.sem, v_copy.at(b, u - 5))
                    up(v_mm, split3(ps[:, V_BANKS[u % 6], :], *lwp(LV + m * P), *xT(c)))
                for t in range(NT):
                    ins = split3(ps[:, 6, t * E:(t + 1) * E], *tok(t), *lwp(LG, E))
                up(gate_mm, ins)
                t_.wait_ge(bnd_in.sem, bnd_in.at(b, 1))
                up(bnd_mm, mm(ps[:, 7, 0:HM], ones, sm[:, 7, 0:HM], True, True))
                attn3 = sm[:, 5, :].rearrange("p (t h) -> p t h", h=H1)

                def spread(u):
                    c, m = u // KM, u % KM
                    if u >= 4:
                        t_.wait_ge(u1_ok.sem, u1_ok.at(b, u - 3))
                    for i in range(TPC):
                        for j in range(P // HD1):
                            w = attn3[:, c * TPC + i, 2 * m + j:2 * m + j + 1].broadcast_to([P, HD1])
                            ins = mm(ps[HD1 * j:HD1 * (j + 1), u % 4, i * P:(i + 1) * P], w, ident, True, True)
                    up(bc_mm, ins)

                def stack(i):
                    g4, j = i // 2, i % 2
                    if i == 0:
                        t_.wait_ge(gate_in.sem, gate_in.at(b, 1))
                        t_.wait_ge(bnd_ok.sem, bnd_ok.at(b, 1))
                    if i == 1:
                        t_.wait_ge(v_copy.sem, v_copy.at(b, 8))
                    if i >= 2:
                        t_.wait_ge(stk_ok.sem, stk_ok.at(b, i - 1))
                    rg = slice(QUAD * g4, QUAD * (g4 + 1))
                    for c in range(NCH):
                        bank = ps[:, STK_BANKS[j] + c, :]
                        mm(bank, sel_r[rg, 2 * j * P:(2 * j + 1) * P], spl[rg, 2 * j, c * CH:(c + 1) * CH], True, False)
                        ins = mm(bank, sel_r[rg, (2 * j + 1) * P:(2 * j + 2) * P], spl[rg, 2 * j + 1, c * CH:(c + 1) * CH], False, True)
                    up(stk_mm, ins)

                t_.wait_ge(attn_ok.sem, attn_ok.at(b, 1))
                t_.wait_ge(v_copy.sem, v_copy.at(b, 6))
                for u in range(3):
                    spread(u)
                for i in range(2 * NG):
                    stack(i)
                    if i + 3 < NCH * KM:
                        spread(i + 3)
                t_.wait_ge(stk_ok.sem, stk_ok.at(b, 2 * NG))
                t_.wait_ge(u1_ok.sem, u1_ok.at(b, 8))
                mm(ps[:, 7, 0:1], ones, ones[:, 0:1], True, True)
                need_max = t_.value_load(iflag[0:1, 1:2], min_val=0, max_val=1)
                with t_.If(need_max > 0):
                    for gt in range(NG * NT):
                        g4, t = gt // NT, gt % NT
                        for g in range(GH):
                            n_ = gt * GH + g
                            if n_ >= 2:
                                t_.wait_ge(gen_mx.sem, gen_mx.at(b, n_ - 1))
                            rg = slice(QUAD * g, QUAD * g + 3 * HDM)
                            for c in range(NCH):
                                ins = mm(ps[:, (0 if n_ % 2 == 0 else 2) + c, :], q_st[rg, g4, t * P:(t + 1) * P],
                                         k_st[rg, g4, c * CH:(c + 1) * CH], True, True)
                            ins.then_inc(gen_mm.sem, 1)
                        t_.wait_ge(gen_mx.sem, gen_mx.at(b, (gt + 1) * GH))
                        if gt >= 2:
                            t_.wait_ge(gen_add.sem, gen_add.at(b, gt - 1))
                        t_.transpose(ps[:, 6 + gt % 2, 0:P], mbuf[:, :], ident).then_inc(gen_T.sem, 1)
                with t_.Else():
                    t_.sem_inc(gen_mm.sem, gen_mm.per)
                    t_.sem_inc(gen_T.sem, gen_T.per)
                gen_mm.given, gen_T.given = gen_mm.per, gen_T.per
                t_.wait_ge(gen_add.sem, gen_add.at(b, NG * NT))

                def m_scores(u):
                    g4, jt, g = u // (NT * GH), (u // GH) % NT, u % GH
                    if u >= 3:
                        t_.wait_ge(ms_exp.sem, ms_exp.at(b, u - 2))
                    if jt == 0:
                        t_.wait_ge(kz_ok.sem, kz_ok.at(b, g4 * GH + g + 1))
                    for c in range(NCH):
                        ins = mm(ps[:, (0, 2, 6)[u % 3] + c, :], kz[:, g, jt * P:(jt + 1) * P],
                                 q_st[:, g4, c * CH:(c + 1) * CH], True, True)
                    up(ms_mm, ins)

                def m_values(gj, c):
                    g4, jt = gj // NT, gj % NT
                    if c == 0:
                        t_.wait_ge(ms_exp.sem, ms_exp.at(b, GH * (gj + 1)))
                        if gj == 0:
                            t_.wait_ge(o_ok.sem, o_ok.at(b, 2))
                        if jt == 0 and g4:
                            t_.wait_ge(oT_ok.sem, oT_ok.at(b, g4))
                    for g in range(GH):
                        ins = mm(ps[QUAD * g:QUAD * (g + 1), 4 + c, :], vaug[:, (jt * HM + g4 * GH + g) * (HDM + 1):(jt * HM + g4 * GH + g) * (HDM + 1) + QUAD],
                                 prob[:, jt % 2, g, c * CH:(c + 1) * CH], jt == 0, jt == NT - 1)
                    up(mp_mm, ins)

                def out_projection(c):
                    t_.wait_ge(z_ok.sem, z_ok.at(b, KM * (c + 1)))
                    for i in range(TPC):
                        for m in range(KM):
                            ins = mm(ps[:, 4 + c, i * D:(i + 1) * D], wk[:, m * S + c * CH + i * P:m * S + c * CH + (i + 1) * P],
                                     wo_sb[:, m * D:(m + 1) * D], m == 0, m == KM - 1)
                    up(o_mm, ins)

                def expert_unit(t):
                    if t == 1:
                        t_.wait_ge(att_ok.sem, att_ok.at(b, NT))
                    if t >= 3:
                        t_.wait_ge(ex_ok.sem, ex_ok.at(b, t - 2))
                    for c in range(2):
                        ins = split3(ps[:, EX_BANKS[t % 3] + c, :], *tok(t), *lwp(LE + c * CH, CH))
                    up(ex_mm, ins)

                def to_natural(t):
                    if t >= 4:
                        t_.wait_ge(att_ok.sem, att_ok.at(b, t - 3))
                    for g4 in range(NG):
                        ins = t_.transpose(ps[:, ON_BANKS[t % 4], g4 * P:(g4 + 1) * P], wk[:, g4 * S + t * P:g4 * S + (t + 1) * P], ident)
                    up(oN_mm, ins)

                for gj in range(NG * NT):
                    for g in range(GH):
                        m_scores(gj * GH + g)
                        if gj * GH + g in (2, 4):
                            out_projection((gj * GH + g) // 2 - 1)
                        if gj and g in (1, 3):
                            m_values(gj - 1, g // 2)
                m_values(NG * NT - 1, 0)
                m_values(NG * NT - 1, 1)

                expert_unit(0)
                t_.wait_ge(oT_ok.sem, oT_ok.at(b, NG))
                t_.wait_ge(comb_ok.sem, comb_ok.at(b, 1))
                for t in range(4):
                    to_natural(t)
                up(cT_mm, t_.transpose(ps[0:NT * E, 4, 0:P], sm[:, 11, :], ident))
                for t in range(4, NT):
                    to_natural(t)
                t_.wait_ge(cT_ok.sem, cT_ok.at(b, 1))
                for c in range(NCH):
                    ins = mm(ps[:, 4 + c, :], ct[:, :], bexp_sb[:, c * CH:(c + 1) * CH], True, True)
                up(eb_mm, ins)
                for t in range(1, NT):
                    expert_unit(t)

        for s_ in [o for o in list(locals().values()) if isinstance(o, Signal)]:
            s_.check()


def kernel(**inputs):
    import numpy as np
    import concourse.bacc as bacc
    from concourse.bass_utils import run_bass_kernel_spmd

    i = {n: np.asarray(a) for n, a in inputs.items()}

    def blocks(wT):
        k_, n_ = wT.shape
        return np.ascontiguousarray(wT.reshape(k_ // P, P, n_).transpose(1, 0, 2)).reshape(P, -1)

    def column(vec):
        return np.ascontiguousarray(vec.reshape(-1, P).T)

    fw = np.concatenate([blocks(i["L0_ffn_" + n].T) for n in ("w1_w", "w2_w", "h1_w", "h2_w", "w3_w")], 1)
    we = np.ascontiguousarray(i["L1_ffn_W_experts"].transpose(1, 0, 2)).reshape(D, E * D)
    lw = np.concatenate([i["L1_attn_Wq"], i["L1_attn_Wk"], i["L1_attn_Wv"], i["L1_ffn_W_qkv"], we, i["L1_ffn_W_gate"]], 1)
    aw = np.concatenate([i["L0_attn_Wa"].T, i["L0_attn_Wk"], i["L0_attn_Wq"], i["L0_attn_Wv"], i["L0_attn_Wb"].T], 1)
    row24 = np.zeros((P, 1), np.float32)
    row24[3 * HDM::QUAD] = 1.0
    b_qkv = i["L1_ffn_b_qkv"]
    cols = np.concatenate(
        [column(i["L0_ffn_" + n]) for n in ("w1_s", "w2_s", "h1_s", "h2_s", "w3_s")]
        + [column(i["L1_attn_" + n]) for n in ("bq", "bk", "bv")]
        + [column(i["L1_attn_aug_param"]), column(i["L1_attn_alpha"])]
        + [column(b_qkv[0:D]), column(b_qkv[D:2 * D]), row24], 1)
    rows = np.concatenate([i["L1_attn_bo"], i["L1_attn_ln_scale"], i["L1_attn_ln_bias"], b_qkv[2 * D:], i["L1_ffn_b_gate"]])
    rows = np.ascontiguousarray(np.broadcast_to(rows[None, :], (P, rows.shape[0])))
    heads1 = np.zeros((P, KM, H1), np.float32)
    for m in range(KM):
        for p in range(P):
            heads1[p, m, (m * P + p) // HD1] = 1.0
    headsm = np.zeros((P, HM), np.float32)
    sel = np.zeros((4, P, P), np.float32)
    for p in range(P):
        headsm[p, p // HDM] = 1.0
        g, d = (p % QUAD) // HDM, p % HDM
        for which, reps in enumerate(((0, 2), (1,), (0, 1), (2,))):
            for r in reps:
                sel[which, p, QUAD * g + HDM * r + d] = 1.0
    mask = np.ones((P, NT, E), np.float32)
    mask[:, :, 0] = 0.0
    cst = np.concatenate([np.eye(P, dtype=np.float32), np.ones((P, P), np.float32), heads1.reshape(P, -1), headsm,
                          sel.transpose(1, 0, 2).reshape(P, -1), mask.reshape(P, -1)], 1)
    x5 = np.concatenate([i["L0_attn_x"], i["L0_attn_x"][0:1]])
    arrays = {"in_x": x5, "in_fw": fw, "in_lw": lw, "in_aw": aw, "in_wo": blocks(i["L1_attn_Wo"]),
              "in_cst": cst, "in_cols": cols, "in_rows": rows, "in_bexp": i["L1_ffn_b_experts"]}
    arrays = {n: np.ascontiguousarray(a) for n, a in arrays.items()}

    nc = bacc.Bacc("TRN2", target_bir_lowering=False, num_devices=1)
    args = [nc.dram_tensor(n, a.shape, mybir.dt.from_np(a.dtype), kind="ExternalInput").ap() for n, a in arrays.items()]
    args.append(nc.dram_tensor("out_0", (B, S, D), F32, kind="ExternalOutput").ap())
    build_program(nc, *args)
    r = run_bass_kernel_spmd(nc, [arrays], core_ids=[0])
    return r.results[0]["out_0"]
```

```python
from contextlib import ExitStack

import concourse.bass as bass
from concourse import mybir

ALU = mybir.AluOpType
ACT = mybir.ActivationFunctionType
F32 = mybir.dt.float32
F32R = mybir.dt.float32r
I32 = mybir.dt.int32
AX = mybir.AxisListType

P = 128
B, S, D = 4, 1024, 128
NT = S // P
CH = 512
NCH = S // CH
TPC = CH // P
HID = 512
KM = HID // P
H1, HD1 = 8, 64
HM, HDM = 16, 8
GH = 4
NG = HM // GH
E = 8
QUAD = 32
LN_EPS, LN1_EPS = 1e-5, 1e-6
SAFE = 40.0
UNITS = NG * NT * GH
EXA = 4
G_EXP_AT = 20
L1_BANKS = ((0, 4), (0, 6))
MAX_BANKS, SC_BANKS = (2, 6), (2, 3, 6, 7)
H_BANKS = ((0, 1, 2, 3), (4, 5, 6, 7))
W3_BANKS, GT_BANKS = (0, 4), (1, 7)
MV_BANKS = (2, 3, 6)
MQ_BANKS = (4, 5, 0, 1)
STK_BANKS = (4, 6)
PV_BANKS = (4, 5, 4, 5, 4, 5, 2, 3)
T_BANKS = (5, 7)
EX_BANKS = (0, 6, 2)

_W1, _H1, _H2, _W3 = (0, 1), (2, 3, 4, 5), (6, 7, 8, 9), (10,)
W_BLOCKS = _W1 + _W1 + _H1 + _H1 + _H2 + _W3 + _H2 + _W3
COL = {}
_at = 0
for _name, _n in (("w1s", KM), ("w2s", KM), ("h1s", KM), ("h2s", KM), ("w3s", 1), ("bq", KM), ("bk", KM),
                  ("bv", KM), ("aug", KM), ("alpha", KM), ("mbq", 1), ("mbk", 1), ("row24", 1)):
    COL[_name] = _at
    _at += _n
NCOL = _at
CI, CO, CHD, CBM, CSEL, CMASK = 0, 128, 256, 288, 304, 816
NCST = 816 + NT * E
FW1, FW2, FH1, FH2, FW3 = 0, HID, 2 * HID, 2 * HID + KM * HID, 2 * HID + 2 * KM * HID
NFW = FW3 + KM * D
FW_PART = 2 * NFW // 3
FW_HALVES = (slice(0, FW_PART), slice(FW_PART, NFW))
LQ, LK, LV, LM, LG, LE = 0, HID, 2 * HID, 3 * HID, 3 * HID + 3 * D, 3 * HID + 3 * D + E
NLW = LE + E * D


class Signal:

    def __init__(self, ctx, nc, name, per, start=0):
        self.sem, self.per, self.name, self.given = ctx.enter_context(nc.semaphore(name)), per, name, 0
        self.start = start

    def at(self, b, k):
        return b * self.per + k + self.start

    def check(self):
        assert self.given == self.per, (self.name, self.given, self.per)


def build_program(nc, x, fw, lw, aw, wo, cst, cols, rows, bexp, out):
    with ExitStack() as ctx:
        def sb(name, shape, dt=F32):
            return ctx.enter_context(nc.sbuf_tensor(name, shape, dt))

        def sem(name):
            return ctx.enter_context(nc.semaphore(name))

        def sig(name, per=1, start=0):
            return Signal(ctx, nc, name, per, start)

        fw_sb = sb("fw_sb", [P, NFW], F32R)
        wblk = sb("wblk", [P, 2, HID])
        lw_hi, lw_lo = sb("lw_hi", [P, NLW], F32R), sb("lw_lo", [P, NLW], F32R)
        gh_hi, gh_lo = sb("gh_hi", [P, 2 * D], F32R), sb("gh_lo", [P, 2 * D], F32R)
        wo_sb = sb("wo_sb", [P, KM * D])
        cst_sb = sb("cst_sb", [P, NCST])
        sel_r = sb("sel_r", [P, 4 * P], F32R)
        ones_r = sb("ones_r", [1, P], F32R)
        cols_sb = sb("cols_sb", [P, NCOL])
        rows_sb = sb("rows_sb", [P, 4 * D + E])
        bexp_sb = sb("bexp_sb", [NT * E, NT * D])
        decay = sb("decay", [P, 3 * KM])
        flags = sb("flags", [P, 8])
        iflag = sb("iflag", [P, 2], I32)
        ident, ones = cst_sb[:, CI:CI + P], cst_sb[:, CO:CO + P]

        xres = sb("xres", [P, NT, D])
        xnext = sb("xnext", [P, NT, D])
        xn = sb("xn", [P, NT * D])
        xt_hi, xt_lo = sb("xt_hi", [P, S], F32R), sb("xt_lo", [P, S], F32R)
        spl = sb("spl", [P, 4, S], F32R)
        big = sb("big", [P, 2, 4, S])
        kz = sb("kz", [P, GH, S], F32R)
        hid = sb("hid", [P, 2, 2, KM, CH], F32R)
        wk = sb("wk", [P, 4 * S])
        vaug = sb("vaug", [P, NT * HM * (HDM + 1) + QUAD])
        st = sb("st", [P, NT * 18])
        sm = sb("sm", [P, 12, NT * E])
        mx = sb("mx", [P, NT])
        negT = sb("negT", [NT, P], F32R)
        ct = sb("ct", [NT * E, P])
        bias_m = sb("bias_m", [P, HM])
        qk_max = sb("qk_max", [P, 4])
        mbuf = sb("mbuf", [P, P])
        mrow = sb("mrow", [P, 1])

        bn = st[:, 0:NT * 6].rearrange("p (t k) -> p t k", k=6)
        lnw = st[:, NT * 6:NT * 10].rearrange("p (k t) -> p k t", k=4)
        mean, var, rstd, half, mean1, var1, rstd1, shift1 = (st[:, NT * i:NT * (i + 1)] for i in range(10, 18))
        xn0 = big[:, 1, 2, :].rearrange("p (t d) -> p t d", d=D)
        xnv = xn[:, :].rearrange("p (t d) -> p t d", d=D)
        g2, fin, moe = (big[:, 0, i, :].rearrange("p (t d) -> p t d", d=D) for i in (1, 2, 3))
        att = wk[:, S:2 * S].rearrange("p (t d) -> p t d", d=D)

        zeros = big[:, 1, 3, :]
        scaled = big[:, 1, 0, 0:2 * EXA * D].rearrange("p (r e d) -> p r e d", r=2, e=EXA)
        moe2 = big[:, 1, 1, :].rearrange("p (t d) -> p t d", d=D)

        def hidden(buf, part, kk):
            if buf < 2:
                return hid[:, buf, part, kk, :]
            return spl[:, 2 * part + kk // 2, (kk % 2) * CH:(kk % 2 + 1) * CH]

        s_nat = wk[:, 0:S]
        act32 = [wk[:, S + i * CH:S + (i + 1) * CH] for i in range(3)]
        uaug = wk[:, S + 3 * CH:S + 3 * CH + NT * (D + 1)].rearrange("p (t n) -> p t n", n=D + 1)
        negrow = spl[0:1, 2, :]
        vaug4 = vaug[:, 0:NT * HM * (HDM + 1)].rearrange("p (t h n) -> p t h n", t=NT, n=HDM + 1)
        prods = [wk[:, (2 + u) * CH % (4 * S):(2 + u) * CH % (4 * S) + CH] for u in range(NCH * KM)]
        q1, v1 = big[:, 0], big[:, 1]
        q_st, k_st = hid[:, 0].rearrange("p a k n -> p (a k n)").rearrange("p (g n) -> p g n", g=NG), \
            hid[:, 1].rearrange("p a k n -> p (a k n)").rearrange("p (g n) -> p g n", g=NG)
        prob = big
        gT = big[:, 0, 0, :]

        ps = ctx.enter_context(nc.psum_tensor("ps", [P, 8, CH], F32))

        wblk_in = [sig("wblk_in%d" % i, 8 * len(W_BLOCKS)) for i in range(2)]
        wblk_used = sig("wblk_used", len(W_BLOCKS), 1)
        small_in, aw_in, lw_in, wo_in, fw_in = sem("small_in"), sem("aw_in"), sem("lw_in"), sem("wo_in"), [sem("fw_in0"), sem("fw_in1")]
        fw_hi_ok, lw_hi_ok, lw_ok, wide_ok, kz_zero, fw_dif = sem("fw_hi_ok"), sem("lw_hi_ok"), sem("lw_ok"), sem("wide_ok"), sem("kz_zero"), sem("fw_dif")
        bexp_in = sem("bexp_in")
        setup_v, setup_a, setup_p = sem("setup_v"), sem("setup_a"), sem("setup_p")

        half_set = sem("half_set")
        x_in = sig("x_in", 16)
        chain = sig("chain", 152, 1)
        xT_mm, x_hi, x_lo = sig("xT_mm", 4, 2), sig("x_hi", 4, 2), sig("x_lo", 4, 2)
        r_mm, r_hi, r_lo = sig("r_mm", 2, 2), sig("r_hi", 2, 2), sig("r_lo", 2, 2)
        u_mm, u_ok = sig("u_mm", 2), sig("u_ok", 2)
        max_mm, row_max = sig("max_mm", NT), sig("row_max", NT)
        maxT, neg_ok, negrow_in = sig("maxT"), sig("neg_ok"), sig("negrow_in", 16)
        l1_mm, l1_act, hid_hi, hid_lo = sig("l1_mm", 16), sig("l1_act", 8), sig("hid_hi", 24), sig("hid_lo", 24)
        sc_mm, sc_exp = sig("sc_mm", 16), sig("sc_exp", 16)
        pv_mm, pv_norm = sig("pv_mm", NT), sig("pv_norm", NT)
        h_mm, h_act = sig("h_mm", 16), sig("h_act", 16)
        w3_mm, w3_act, gnat_mm, res_ok = sig("w3_mm", 2), sig("w3_act", 2), sig("gnat_mm", 2), sig("res_ok", 2)
        ln_ok, var_ok, rstd_ok = sig("ln_ok", 2), sig("var_ok", 3), sig("rstd_ok", 3)
        var1_ok, rstd1_ok, stats1_ok, xn0_ok = sig("var1_ok"), sig("rstd1_ok"), sig("stats1_ok"), sig("xn0_ok")
        sg_ok, half_sum = sig("sg_ok", 2), sig("half_sum")
        xs_ok, xs_sum, pe_ok = sig("xs_ok", NT), sig("xs_sum", NT), sig("pe_ok", NT)
        qs_ok, o_ok, sum_ok = sig("qs_ok", 8), sig("o_ok", 2), [sig("sum_ok0"), sig("sum_ok1")]
        qk_mm, q_copy, prod_ok = sig("qk_mm", 16), sig("q_copy", 8), sig("prod_ok", 8)
        hsT_mm, hsT_in = sig("hsT_mm", 2), sig("hsT_in", 2)
        hs_mm, hs_sub, hs_exp, attn_ok = sig("hs_mm", 2), sig("hs_sub"), sig("hs_exp"), sig("attn_ok")
        v_mm, v_copy, bc_mm, u1_ok = sig("v_mm", 8), sig("v_copy", 8), sig("bc_mm", 8), sig("u1_ok", 8)
        aug_ok, z_ok, o_mm = sig("aug_ok", 8), sig("z_ok", 8), sig("o_mm", 2)
        mq_mm, mq_hi, mq_lo = sig("mq_mm", 4), sig("mq_hi", 4), sig("mq_lo", 4)
        stk_mm, stk_ok = sig("stk_mm", 8), sig("stk_ok", 8)
        mv_mm, mv_ok = sig("mv_mm", 3), sig("mv_ok", 3)
        g_sub, g_exp = sig("g_sub"), sig("g_exp")
        bnd_in, bnd_mm, bnd_ok = sig("bnd_in"), sig("bnd_mm"), sig("bnd_ok")
        kz_ok = sig("kz_ok", HM)
        gen_mm, gen_mx, gen_T, gen_add = (sig("gen_mm", UNITS), sig("gen_mx", UNITS), sig("gen_T", NG * NT),
                                          sig("gen_add", NG * NT))
        ms_mm, ms_exp = sig("ms_mm", UNITS), sig("ms_exp", UNITS)
        mp_mm, oT_ok = sig("mp_mm", NG * NT * 2), sig("oT_ok", 2 * NG)
        oN_mm, att_ok = sig("oN_mm", 2 * NG), sig("att_ok", 2 * NG)
        comb_ok, cT_mm, cT_ok, eb_mm = sig("comb_ok"), sig("cT_mm"), sig("cT_ok"), sig("eb_mm")
        eb_ok = sig("eb_ok")
        ex_mm, ex_ok, g2_ok, fin_ok = sig("ex_mm", NT), sig("ex_ok", NT, 1), sig("g2_ok", 2, 1), sig("fin_ok", 2, 1)
        stored = sig("stored", 32, 1)

        def col(name, k=0):
            return cols_sb[:, COL[name] + k:COL[name] + k + 1]

        def up(signal, ins, n=1):
            signal.given += n
            return ins.then_inc(signal.sem, n)

        def layer_norm_stats(v, step, own, src, tiles, mean_, eps):
            tl = slice(tiles[0], tiles[-1] + 1)
            for t in tiles:
                step(v.bn_stats(bn[:, t, :], src[:, t, :]))
            own()
            step(v.tensor_tensor(lnw[:, 0, tl], bn[:, tl, 1], bn[:, tl, 4], ALU.add))
            step(v.tensor_tensor(lnw[:, 1, tl], bn[:, tl, 1], bn[:, tl, 4], ALU.subtract))
            step(v.tensor_tensor(lnw[:, 2, tl], bn[:, tl, 2], bn[:, tl, 5], ALU.add))
            own()
            step(v.tensor_scalar(mean_[:, tl], lnw[:, 0, tl], 0.5, None, ALU.mult))
            step(v.scalar_tensor_tensor(lnw[:, 3, tl], lnw[:, 1, tl], 0.25, lnw[:, 1, tl], ALU.mult, ALU.mult))
            step(v.tensor_scalar(lnw[:, 2, tl], lnw[:, 2, tl], 1.0 / D, eps, ALU.mult, ALU.add))
            own()

        def var_terms(tiles):
            tl = slice(tiles[0], tiles[-1] + 1)
            return lnw[:, 2, tl], lnw[:, 3, tl]

        marks = {}
        block = ctx.enter_context(nc.Block())

        @block.sync
        def _(sp):
            def load_x(i):
                return sp.dma_start(xnext[:, :, :], x[bass.ds(i, 1)].rearrange("o (t p) d -> p (o t) d", p=P))

            load_x(0).then_inc(x_in.sem, 16)
            sp.dma_start(cst_sb[:, :], cst).then_inc(small_in, 16)
            sp.dma_start(cols_sb[:, :], cols).then_inc(small_in, 16)
            sp.dma_start(rows_sb[:, :], rows).then_inc(small_in, 16)
            sp.dma_start(xn[:, 0:5 * D], aw).then_inc(aw_in, 16)
            bigf = big[:, :, :, :].rearrange("p a g n -> p (a g n)")
            for i in range(2):
                sp.dma_start(bigf[:, FW_HALVES[i]], fw[:, FW_HALVES[i]]).then_inc(fw_in[i], 16)
            sp.dma_start(wk[:, 0:NLW], lw).then_inc(lw_in, 16)
            sp.dma_start(wo_sb[:, :], wo).then_inc(wo_in, 16)
            sp.wait_ge(setup_v, 1)
            for t in range(NT):
                sp.dma_start(bexp_sb[E * t:E * (t + 1), D * t:D * (t + 1)], bexp).then_inc(bexp_in, 16)
            sp.wait_ge(wide_ok, 1)
            wide = sp.value_load(iflag[0:1, 0:1], min_val=0, max_val=1)

            def weight_blocks(b, first, last):
                for n_ in range(first, last):
                    if n_ >= 2:
                        sp.wait_ge(wblk_used.sem, wblk_used.at(b, n_ - 1))
                    else:
                        sp.wait_ge(wblk_used.sem, wblk_used.at(b, 0))
                    at = W_BLOCKS[n_] * HID
                    sp.dma_start(wblk[:, n_ % 2, :], fw[:, at:at + HID]).then_inc(wblk_in[n_ % 2].sem, 16)

            with sp.Fori(0, B) as b:
                with sp.If(wide > 0):
                    weight_blocks(b, 0, 2)
                sp.wait_ge(neg_ok.sem, neg_ok.at(b, 1))
                up(negrow_in, sp.dma_start(negrow[:, :].bitcast(F32), negT[:, :].bitcast(F32)), 16)
                with sp.If(wide > 0):
                    weight_blocks(b, 2, len(W_BLOCKS))
                for s_ in wblk_in:
                    s_.given = s_.per
                sp.wait_ge(res_ok.sem, res_ok.at(b, 2))
                up(x_in, load_x(b + 1), 16)
                for c in range(NCH):
                    sp.wait_ge(fin_ok.sem, fin_ok.at(b, c + 1))
                    o = out[bass.ds(b, 1)].rearrange("o (t p) d -> p (o t) d", p=P)
                    up(stored, sp.dma_start(o[:, c * TPC:(c + 1) * TPC, :], fin[:, c * TPC:(c + 1) * TPC, :]), 16)
            sp.wait_ge(x_in.sem, x_in.at(B, 16))
            sp.wait_ge(stored.sem, stored.at(B, 0))

        @block.vector
        def _(v):
            n = [0]

            def done(ins, mark=None):
                ins.then_inc(setup_v, 1)
                n[0] += 1
                if mark:
                    marks[mark] = n[0]

            def so_far():
                v.wait_ge(setup_v, n[0])

            bigf = big[:, :, :, :].rearrange("p a g n -> p (a g n)")
            done(v.memset(bexp_sb[:, :], 0.0), "bexp frame")
            done(v.memset(vaug[:, :], 0.0))
            done(v.memset(mbuf[:, :], 0.0))
            so_far()
            done(v.memset(vaug4[:, :, :, HDM:HDM + 1], 1.0))
            v.wait_ge(x_in.sem, 16)
            layer_norm_stats(v, done, so_far, xnext, range(NT), mean1, LN_EPS)
            v.tensor_tensor(var1, *var_terms(range(NT)), ALU.add).then_inc(var1_ok.sem, 1)
            v.wait_ge(rstd1_ok.sem, 1)
            v.scalar_tensor_tensor(shift1, mean1, -1.0, rstd1, ALU.mult, ALU.mult).then_inc(stats1_ok.sem, 1)
            v.wait_ge(setup_p, 1)
            done(v.tensor_copy(xn[:, 5 * D:6 * D], ps[:, 0, 0:D]), "Wa Wk")
            v.wait_ge(setup_p, 2)
            done(v.tensor_copy(gh_hi[:, :], ps[:, 1, 0:2 * D]))
            so_far()
            done(v.tensor_tensor(gh_lo[:, :], ps[:, 1, 0:2 * D], gh_hi[:, :].bitcast(F32), ALU.subtract), "G and H")
            for c in range(NCH):
                v.wait_ge(x_hi.sem, c + 1)
                v.tensor_tensor(xt_lo[:, c * CH:(c + 1) * CH], ps[:, 4 + c, :], xt_hi[:, c * CH:(c + 1) * CH].bitcast(F32),
                                ALU.subtract).then_inc(x_lo.sem, 1)
            v.wait_ge(small_in, 48)
            done(v.tensor_copy(sel_r[:, :], cst_sb[:, CSEL:CSEL + 4 * P]))
            done(v.tensor_copy(ones_r[:, :], cst_sb[0:1, CO:CO + P]))
            v.wait_ge(setup_a, 1)
            done(v.tensor_scalar(decay[:, KM:2 * KM], decay[:, 0:KM], -1.0, 1.0, ALU.mult, ALU.add))
            so_far()
            done(v.tensor_tensor(decay[:, 2 * KM:3 * KM], decay[:, KM:2 * KM], cols_sb[:, COL["bv"]:COL["bv"] + KM], ALU.mult))
            for i in range(2):
                h_ = FW_HALVES[i]
                if i == 0:
                    v.wait_ge(fw_hi_ok, 1)
                    done(v.tensor_tensor(bigf[:, h_], bigf[:, h_], fw_sb[:, h_].bitcast(F32), ALU.subtract))
                    so_far()
                else:
                    v.wait_ge(fw_dif, 1)
                done(v.tensor_reduce(flags[:, 4 + i:5 + i], bigf[:, h_], AX.X, ALU.max, apply_absolute_value=True))
            for c in range(NCH):
                v.wait_ge(r_hi.sem, c + 1)
                v.tensor_tensor(spl[:, 1, c * CH:(c + 1) * CH], ps[:, c, :], spl[:, 0, c * CH:(c + 1) * CH].bitcast(F32),
                                ALU.subtract).then_inc(r_lo.sem, 1)
            so_far()
            done(v.tensor_tensor(flags[:, 0:1], flags[:, 4:5], flags[:, 5:6], ALU.max), "flags")
            v.wait_ge(setup_p, 3)
            v.tensor_scalar(iflag[:, 0:1], ps[:, 2, 0:1], 0.0, None, ALU.is_gt).then_inc(wide_ok, 1)
            v.wait_ge(wide_ok, 1)
            v.wait_ge(lw_ok, 1)

            with v.Fori(0, B) as b:
                k = [0]

                def step(ins):
                    k[0] += 1
                    up(chain, ins)

                def own(but=0):
                    v.wait_ge(chain.sem, chain.at(b, k[0] - but))

                def normalise(src, dst, tiles):
                    for t in tiles:
                        ins = v.tensor_scalar(dst[:, t, :], src[:, t, :], mean[:, t:t + 1], rstd[:, t:t + 1],
                                              ALU.subtract, ALU.mult)
                        if t < tiles[-1]:
                            step(ins)
                    return ins

                def split_rest(lo, hi, bank, c, sig_mm, n_mm, sig_hi, sig_lo):
                    v.wait_ge(sig_hi.sem, sig_hi.at(b, n_mm))
                    up(sig_lo, v.tensor_tensor(lo[:, c * CH:(c + 1) * CH], ps[:, bank, :],
                                               hi[:, c * CH:(c + 1) * CH].bitcast(F32), ALU.subtract))

                def split_hidden(n_, buf, m):
                    src = act32[n_ % 3]
                    up(hid_hi, v.tensor_copy(hidden(buf, 0, m), src))
                    v.wait_ge(hid_hi.sem, hid_hi.at(b, n_ + 1))
                    up(hid_lo, v.tensor_tensor(hidden(buf, 1, m), src, hidden(buf, 0, m).bitcast(F32), ALU.subtract))

                own()
                def gate_unit(c, m):
                    n_ = c * KM + m
                    v.wait_ge(l1_mm.sem, l1_mm.at(b, 2 * n_ + 2))
                    v.wait_ge(l1_act.sem, l1_act.at(b, n_ + 1))
                    h_ = act32[n_ % 3]
                    step(v.scalar_tensor_tensor(h_, ps[:, L1_BANKS[c][m % 2] + 1, :], col("w2s", m), h_, ALU.mult, ALU.mult))
                    own()
                    split_hidden(n_, 2 * c, m)

                def row_maximum(t):
                    v.wait_ge(max_mm.sem, max_mm.at(b, t + 1))
                    bank = MAX_BANKS[t % 2]
                    up(row_max, v.tensor_reduce(mx[:, t:t + 1], ps[:, bank:bank + 2, :], AX.XY, ALU.max))

                for t in range(NT):
                    row_maximum(t)
                v.wait_ge(g2_ok.sem, g2_ok.at(b, 0))
                step(v.memset(uaug[:, :, D:D + 1], 1.0))
                v.wait_ge(maxT.sem, maxT.at(b, 1))
                up(neg_ok, v.tensor_scalar(negT[:, :], ps[0:NT, 6, 0:P], -1.0, None, ALU.mult))

                def act_units(first, first_hid, buf):
                    for m in range(KM):
                        v.wait_ge(h_act.sem, h_act.at(b, first + m + 1))
                        split_hidden(first_hid + m, buf, m)

                def residual(c):
                    v.wait_ge(gnat_mm.sem, gnat_mm.at(b, c + 1))
                    own()
                    sl = slice(c * CH, (c + 1) * CH)
                    step(v.tensor_tensor(s_nat[:, sl], s_nat[:, sl], ps[:, GT_BANKS[c], :], ALU.mult))
                    own()
                    if c == 0:
                        v.wait_ge(fin_ok.sem, fin_ok.at(b, 0))
                    flat = lambda a_: a_[:, :, :].rearrange("p t d -> p (t d)")[:, sl]
                    up(res_ok, v.tensor_tensor(flat(xres), flat(xnext), s_nat[:, sl], ALU.add))
                    v.wait_ge(res_ok.sem, res_ok.at(b, c + 1))

                def divide(t):
                    v.wait_ge(pv_mm.sem, pv_mm.at(b, t + 1))
                    o = ps[:, PV_BANKS[t], 0:D + 1]
                    step(v.reciprocal(mrow[:, 0:1], o[:, D:D + 1]))
                    own()
                    up(pv_norm, v.tensor_scalar(s_nat[:, t * D:(t + 1) * D], o[:, 0:D], mrow[:, 0:1], None, ALU.mult))
                    v.wait_ge(pv_norm.sem, pv_norm.at(b, t + 1))

                for m in range(KM):
                    gate_unit(0, m)
                for m in range(KM):
                    divide(m)
                    gate_unit(1, m)
                act_units(0, 8, 1)
                act_units(4, 12, 0)
                act_units(8, 16, 2)

                def block_norm(c):
                    tiles = range(c * TPC, (c + 1) * TPC)
                    layer_norm_stats(v, step, own, xres, tiles, mean, LN_EPS)
                    up(var_ok, v.tensor_tensor(var[:, tiles[0]:tiles[-1] + 1], *var_terms(tiles), ALU.add))
                    v.wait_ge(rstd_ok.sem, rstd_ok.at(b, c + 1))
                    up(ln_ok, normalise(xres, xnv, tiles))

                def product(u):
                    c, m = u // KM, u % KM
                    v.wait_ge(qk_mm.sem, qk_mm.at(b, 2 * u + 2))
                    v.wait_ge(q_copy.sem, q_copy.at(b, u + 1))
                    up(prod_ok, v.scalar_tensor_tensor(prods[u], ps[:, 2 * (u % 3) + 1, :], col("bk", m),
                                                       q1[:, m, c * CH:(c + 1) * CH], ALU.add, ALU.mult))

                divide(4)
                divide(5)
                residual(0)
                block_norm(0)
                act_units(12, 20, 1)
                divide(6)
                divide(7)
                split_rest(xt_lo, xt_hi, T_BANKS[0], 0, xT_mm, 1, x_hi, x_lo)
                product(0)
                residual(1)
                block_norm(1)
                product(1)
                split_rest(xt_lo, xt_hi, T_BANKS[1], 1, xT_mm, 2, x_hi, x_lo)
                for u in range(2, 2 * KM):
                    product(u)

                w3d = lambda i: sm[:, i, :].rearrange("p (t e) -> p t e", e=E)
                over_e = lambda i: sm[:, i, 0:NT].unsqueeze(2).broadcast_to([P, NT, E])

                def softmax8_shift(src, shifted):
                    step(v.tensor_reduce(sm[:, 0, 0:NT], src, AX.X, ALU.max))
                    own()
                    up(shifted, v.tensor_tensor(w3d(1), src, over_e(0), ALU.subtract))

                def softmax8_divide(exp_done):
                    v.wait_ge(exp_done.sem, exp_done.at(b, 1))
                    step(v.tensor_reduce(sm[:, 3, 0:NT], w3d(2), AX.X, ALU.add))
                    own()
                    step(v.reciprocal(sm[:, 4, 0:NT], sm[:, 3, 0:NT]))
                    own()
                    return v.tensor_tensor(w3d(5), w3d(2), over_e(4), ALU.mult)

                v.wait_ge(hs_mm.sem, hs_mm.at(b, 2))
                for c in range(NCH):
                    step(v.tensor_copy(sm[:, 6, c * TPC * H1:(c + 1) * TPC * H1].rearrange("p (t m j) -> p t m j", t=TPC, m=KM),
                                       ps[:, 6 + c, :].rearrange("p (t m q) -> p t m q", t=TPC, m=KM)[:, :, :, 0:P // HD1]))
                own()
                softmax8_shift(w3d(6), hs_sub)
                for i in range(4):
                    j, c = i // 2, i % 2
                    v.wait_ge(mq_hi.sem, mq_hi.at(b, i + 1))
                    up(mq_lo, v.scalar_tensor_tensor(spl[:, 2 * j + 1, c * CH:(c + 1) * CH], ps[:, MQ_BANKS[i], :],
                                                     col(("mbq", "mbk")[j]), spl[:, 2 * j, c * CH:(c + 1) * CH].bitcast(F32),
                                                     ALU.add, ALU.subtract))
                up(attn_ok, softmax8_divide(hs_exp))
                for i in range(3):
                    tl = slice(3 * i, min(3 * i + 3, NT))
                    n_ = tl.stop - tl.start
                    v.wait_ge(mv_mm.sem, mv_mm.at(b, i + 1))
                    src = ps[:, MV_BANKS[i], 0:n_ * (D + E)].rearrange("p (t n) -> p t n", n=D + E)
                    step(v.tensor_tensor(
                        vaug4[:, tl, :, 0:HDM], src[:, :, 0:D].rearrange("p t (h n) -> p t h n", n=HDM),
                        rows_sb[:, 3 * D:4 * D].rearrange("p (h n) -> p h n", n=HDM).unsqueeze(1)
                        .broadcast_to([P, n_, HM, HDM]), ALU.add))
                    up(mv_ok, v.tensor_tensor(w3d(6)[:, tl, :], src[:, :, D:D + E],
                                              rows_sb[:, 4 * D:4 * D + E].unsqueeze(1).broadcast_to([P, n_, E]), ALU.add))
                for j in range(2):
                    step(v.tensor_reduce(qk_max[:, j:j + 1], spl[:, 2 * j, :].bitcast(F32), AX.X, ALU.max,
                                         apply_absolute_value=True))
                own()
                step(v.scalar_tensor_tensor(qk_max[:, 2:3], qk_max[:, 0:1], -1.002 / HDM ** 0.5, qk_max[:, 1:2],
                                            ALU.mult, ALU.mult))
                own()
                up(bnd_in, v.tensor_scalar(sm[:, 7, 0:HM], cst_sb[:, CBM:CBM + HM], qk_max[:, 2:3], None, ALU.mult))
                v.wait_ge(bnd_mm.sem, bnd_mm.at(b, 1))
                step(v.tensor_reduce(flags[:, 1:2], ps[:, 6, 0:HM], AX.X, ALU.min))
                own()
                step(v.tensor_scalar(flags[:, 2:3], flags[:, 1:2], -SAFE, None, ALU.is_ge))
                step(v.tensor_scalar(iflag[:, 1:2], flags[:, 1:2], -SAFE, None, ALU.is_lt))
                own()
                up(bnd_ok, v.tensor_scalar(bias_m[:, :], ps[:, 6, 0:HM], flags[:, 2:3], None, ALU.mult))
                def load_kz(g4, g):
                    rg = slice(QUAD * g, QUAD * (g + 1))
                    up(kz_ok, v.tensor_copy(kz[rg, g, :], k_st[rg, g4, :].bitcast(F32)))

                for u in range(NCH * KM):
                    c, m = u // KM, u % KM
                    sl = slice(c * CH, (c + 1) * CH)
                    v.wait_ge(bc_mm.sem, bc_mm.at(b, u + 1))
                    v.wait_ge(v_copy.sem, v_copy.at(b, u + 1))
                    up(u1_ok, v.tensor_tensor(v1[:, m, sl], v1[:, m, sl], ps[:, 2 + u % 2, :], ALU.mult))
                    v.wait_ge(u1_ok.sem, u1_ok.at(b, u + 1))
                    z = wk[:, m * S + c * CH:m * S + (c + 1) * CH]
                    init = 0.0 if c == 0 else v1[:, m, c * CH - 1:c * CH]
                    step(v.tensor_tensor_scan(v1[:, m, sl], decay[:, m:m + 1].broadcast_to([P, CH]), v1[:, m, sl], init,
                                              ALU.mult, ALU.add))
                    own()
                    up(qs_ok, v.tensor_tensor(z, q1[:, m, sl], v1[:, m, sl], ALU.mult))
                    if u == KM - 1:
                        v.wait_ge(kz_zero, 1)
                        v.wait_ge(stk_ok.sem, stk_ok.at(b, 2))
                        for g in range(GH):
                            load_kz(0, g)

                need_max = v.value_load(iflag[0:1, 1:2], min_val=0, max_val=1)
                with v.If(need_max > 0):
                    for gt in range(NG * NT):
                        g4, t = gt // NT, gt % NT
                        for g in range(GH):
                            n_ = gt * GH + g
                            v.wait_ge(gen_mm.sem, gen_mm.at(b, n_ + 1))
                            if gt and g == 0:
                                v.wait_ge(gen_T.sem, gen_T.at(b, gt))
                            v.tensor_reduce(mbuf[:, QUAD * g + 3 * HDM:QUAD * g + 3 * HDM + 1],
                                            ps[:, (0 if n_ % 2 == 0 else 2):(2 if n_ % 2 == 0 else 4), :],
                                            AX.XY, ALU.max, negate=True).then_inc(gen_mx.sem, 1)
                        v.wait_ge(gen_T.sem, gen_T.at(b, gt + 1))
                        qs = q_st[:, g4, t * P:(t + 1) * P]
                        v.tensor_tensor(qs, qs.bitcast(F32), ps[:, 6 + gt % 2, 0:P], ALU.add).then_inc(gen_add.sem, 1)
                with v.Else():
                    v.sem_inc(gen_mx.sem, gen_mx.per)
                    v.sem_inc(gen_add.sem, gen_add.per)
                gen_mx.given, gen_add.given = gen_mx.per, gen_add.per

                v.wait_ge(z_ok.sem, z_ok.at(b, 8))
                for c in range(NCH):
                    v.wait_ge(o_mm.sem, o_mm.at(b, c + 1))
                    up(o_ok, v.tensor_tensor(xnv[:, c * TPC:(c + 1) * TPC, :], ps[:, 4 + c, :].rearrange("p (t d) -> p t d", d=D),
                                             rows_sb[:, 0:D].unsqueeze(1).broadcast_to([P, TPC, D]), ALU.add))
                v.wait_ge(o_ok.sem, o_ok.at(b, 2))
                every = range(NT)
                layer_norm_stats(v, step, own, xnv, every, mean, LN1_EPS)
                up(var_ok, v.tensor_tensor(var, *var_terms(every), ALU.add))
                softmax8_shift(w3d(6), g_sub)
                step(softmax8_divide(g_exp))
                own()
                gate, left = w3d(5), sm[:, 8, :]
                for r in range(2):
                    src = gate if r == 0 else w3d(8)
                    step(v.tensor_reduce(sm[:, 0, 0:NT], src, AX.X, ALU.max))
                    own()
                    step(v.tensor_tensor(w3d(1), src, over_e(0), ALU.is_ge))
                    own()
                    step(v.tensor_tensor_scan(sm[:, 3, :], cst_sb[:, CMASK:CMASK + NT * E], sm[:, 1, :], 0.0,
                                              ALU.mult, ALU.add))
                    own()
                    step(v.scalar_tensor_tensor(sm[:, 9 + r, :], sm[:, 3, :], 1.0, sm[:, 1, :], ALU.is_equal, ALU.mult))
                    own()
                    if r == 0:
                        step(v.scalar_tensor_tensor(left, sm[:, 9, :], -4.0, sm[:, 5, :], ALU.mult, ALU.add))
                        own()
                step(v.tensor_tensor(sm[:, 9, :], sm[:, 9, :], sm[:, 10, :], ALU.add))
                own()
                up(comb_ok, v.tensor_tensor(sm[:, 11, :], sm[:, 5, :], sm[:, 9, :], ALU.mult))
                v.wait_ge(rstd_ok.sem, rstd_ok.at(b, 3))
                step(normalise(xnv, xnv, every))
                own()
                step(v.tensor_tensor(xnv, xnv, rows_sb[:, D:2 * D].unsqueeze(1).broadcast_to([P, NT, D]), ALU.mult))
                own()
                step(v.tensor_tensor(xnv, xnv, rows_sb[:, 2 * D:3 * D].unsqueeze(1).broadcast_to([P, NT, D]), ALU.add))
                for g4 in range(NG):
                    if g4 < NG - 1:
                        for g in range(GH):
                            v.wait_ge(ms_mm.sem, ms_mm.at(b, ((g4 + 1) * NT - 1) * GH + g + 1))
                            load_kz(g4 + 1, g)
                    for c in range(NCH):
                        v.wait_ge(mp_mm.sem, mp_mm.at(b, (g4 + 1) * NT * 2 - 1 + c))
                        up(oT_ok, v.tensor_copy(wk[:, c * CH:(c + 1) * CH], ps[:, 4 + c, :]))
                    for c in range(NCH):
                        n_ = 2 * g4 + c
                        v.wait_ge(oN_mm.sem, oN_mm.at(b, n_ + 1))
                        oN = ps[:, 4 + c, :].rearrange("p (i n) -> p i n", n=QUAD)
                        rec = sm[:, 0, c * TPC * GH:(c + 1) * TPC * GH]
                        step(v.reciprocal(rec, oN[:, :, HDM]))
                        own()
                        up(att_ok, v.tensor_tensor(
                            att[:, c * TPC:(c + 1) * TPC, g4 * GH * HDM:(g4 + 1) * GH * HDM].rearrange("p t (h n) -> p t h n", n=HDM),
                            oN[:, :, 0:HDM].rearrange("p (t h) n -> p t h n", h=GH),
                            rec.rearrange("p (t h) -> p t h", h=GH).unsqueeze(3).broadcast_to([P, TPC, GH, HDM]), ALU.mult))
                    v.wait_ge(att_ok.sem, att_ok.at(b, 2 * g4 + 2))
                    if g4 == 1:
                        v.wait_ge(x_in.sem, x_in.at(b, 32))
                        layer_norm_stats(v, step, own, xnext, every, mean1, LN_EPS)
                        up(var1_ok, v.tensor_tensor(var1, *var_terms(every), ALU.add))
                        v.wait_ge(rstd1_ok.sem, rstd1_ok.at(b, 2))
                        up(stats1_ok, v.scalar_tensor_tensor(shift1, mean1, -1.0, rstd1, ALU.mult, ALU.mult))
                v.wait_ge(eb_ok.sem, eb_ok.at(b, 1))
                v.wait_ge(att_ok.sem, att_ok.at(b, 2 * NG))

                for t in range(NT):
                    v.wait_ge(ex_mm.sem, ex_mm.at(b, t + 1))
                    for e in range(E - EXA):
                        acc = (att, moe)[e % 2][:, t, :]
                        if e >= 2:
                            own(1)
                        ins = v.scalar_tensor_tensor(acc, ps[:, EX_BANKS[t % 3] + e // 4, (e % 4) * D:(e % 4 + 1) * D],
                                                     sm[:, 11, t * E + e:t * E + e + 1], acc, ALU.mult, ALU.add)
                        if e < E - EXA - 1:
                            step(ins)
                    up(ex_ok, ins)
                    if t == TPC:
                        tl = slice(0, TPC)
                        v.wait_ge(ex_ok.sem, ex_ok.at(b, TPC))
                        v.wait_ge(pe_ok.sem, pe_ok.at(b, TPC))
                        step(v.tensor_tensor(moe[:, tl, :], moe[:, tl, :], moe2[:, tl, :], ALU.add))
                        own()
                        up(sum_ok[0], v.tensor_tensor(att[:, tl, :], att[:, tl, :], moe[:, tl, :], ALU.add))
                    if t == NT - 2:
                        for c in range(NCH):
                            split_rest(xt_lo, xt_hi, 4 + c, c, xT_mm, 3 + c, x_hi, x_lo)
                for c in range(NCH):
                    split_rest(spl[:, 1], spl[:, 0], c, c, r_mm, c + 1, r_hi, r_lo)

        @block.gpsimd
        def _(g_):
            g_.memset(half, -0.5).then_inc(half_set, 1)
            g_.memset(zeros, 0.0).then_inc(half_set, 1)
            g_.wait_ge(half_set, 2)
            g_.wait_ge(var1_ok.sem, 1)
            g_.tensor_tensor(rstd1, var1, half, ALU.pow).then_inc(rstd1_ok.sem, 1)
            bigf, h_ = big[:, :, :, :].rearrange("p a g n -> p (a g n)"), FW_HALVES[1]
            g_.wait_ge(fw_hi_ok, 2)
            g_.tensor_tensor(bigf[:, h_], bigf[:, h_], fw_sb[:, h_].bitcast(F32), ALU.subtract).then_inc(fw_dif, 1)
            g_.wait_ge(lw_hi_ok, 1)
            g_.tensor_tensor(lw_lo[:, :], wk[:, 0:NLW], lw_hi[:, :].bitcast(F32), ALU.subtract).then_inc(lw_ok, 1)
            with g_.Fori(0, B) as b:
                for c in range(NCH):
                    tl = slice(c * TPC, (c + 1) * TPC)
                    g_.wait_ge(var_ok.sem, var_ok.at(b, c + 1))
                    up(rstd_ok, g_.tensor_tensor(rstd[:, tl], var[:, tl], half[:, tl], ALU.pow))
                for u in range(NCH * KM):
                    c, m = u // KM, u % KM
                    z = wk[:, m * S + c * CH:m * S + (c + 1) * CH]
                    g_.wait_ge(qs_ok.sem, qs_ok.at(b, u + 1))
                    g_.wait_ge(aug_ok.sem, aug_ok.at(b, u + 1))
                    up(z_ok, g_.tensor_tensor(z, z, xn[:, (u % 2) * CH:(u % 2 + 1) * CH], ALU.add))

                g_.wait_ge(var_ok.sem, var_ok.at(b, 3))
                up(rstd_ok, g_.tensor_tensor(rstd, var, half, ALU.pow))
                g_.wait_ge(var1_ok.sem, var1_ok.at(b, 2))
                up(rstd1_ok, g_.tensor_tensor(rstd1, var1, half, ALU.pow))
                for t in range(NT):
                    g_.wait_ge(xs_ok.sem, xs_ok.at(b, t + 1))
                    w = scaled[:, t % 2]
                    up(xs_sum, g_.tensor_tensor(w[:, 0:2, :], w[:, 0:2, :], w[:, 2:4, :], ALU.add))
                    g_.wait_ge(xs_sum.sem, xs_sum.at(b, t + 1))
                    up(pe_ok, g_.tensor_tensor(moe2[:, t, :], w[:, 0, :], w[:, 1, :], ALU.add))
                tl = slice(TPC, NT)
                g_.wait_ge(ex_ok.sem, ex_ok.at(b, NT))
                g_.wait_ge(pe_ok.sem, pe_ok.at(b, NT))
                up(half_sum, g_.tensor_tensor(moe[:, tl, :], moe[:, tl, :], moe2[:, tl, :], ALU.add))
                g_.wait_ge(half_sum.sem, half_sum.at(b, 1))
                up(sum_ok[1], g_.tensor_tensor(att[:, tl, :], att[:, tl, :], moe[:, tl, :], ALU.add))
                for c in range(NCH):
                    tl = slice(c * TPC, (c + 1) * TPC)
                    g_.wait_ge(g2_ok.sem, g2_ok.at(b, c + 1))
                    up(sg_ok, g_.tensor_tensor(g2[:, tl, :], g2[:, tl, :], xnv[:, tl, :], ALU.mult))
                    g_.wait_ge(sg_ok.sem, sg_ok.at(b, c + 1))
                    up(fin_ok, g_.tensor_tensor(fin[:, tl, :], g2[:, tl, :], xres[:, tl, :], ALU.add))

        @block.scalar
        def _(a):
            def normalise_next(signal):
                for t in range(NT):
                    ins = a.activation(xn0[:, t, :], xnext[:, t, :], ACT.Identity, bias=shift1[:, t:t + 1],
                                       scale=rstd1[:, t:t + 1])
                ins.then_inc(signal, 1)

            for s_ in (chain, wblk_used, ex_ok, g2_ok, fin_ok, stored):
                a.sem_inc(s_.sem, s_.start)
            a.wait_ge(half_set, 2)
            for g in range(GH):
                ins = a.activation(kz[:, g, :], zeros, ACT.Copy)
            ins.then_inc(kz_zero, 1)
            a.wait_ge(small_in, 48)
            a.activation(decay[:, 0:KM], cols_sb[:, COL["alpha"]:COL["alpha"] + KM], ACT.Sigmoid).then_inc(setup_a, 1)
            a.wait_ge(stats1_ok.sem, 1)
            normalise_next(xn0_ok.sem)
            for c in range(NCH):
                a.wait_ge(xT_mm.sem, c + 1)
                a.activation(xt_hi[:, c * CH:(c + 1) * CH], ps[:, 4 + c, :], ACT.Copy).then_inc(x_hi.sem, 1)
            bigf = big[:, :, :, :].rearrange("p a g n -> p (a g n)")
            for i in range(2):
                a.wait_ge(fw_in[i], 16)
                a.activation(fw_sb[:, FW_HALVES[i]], bigf[:, FW_HALVES[i]], ACT.Copy).then_inc(fw_hi_ok, 1)
            a.wait_ge(lw_in, 16)
            a.activation(lw_hi[:, :], wk[:, 0:NLW], ACT.Copy).then_inc(lw_hi_ok, 1)
            for c in range(NCH):
                a.wait_ge(r_mm.sem, c + 1)
                a.activation(spl[:, 0, c * CH:(c + 1) * CH], ps[:, c, :], ACT.Copy).then_inc(r_hi.sem, 1)
            a.wait_ge(lw_ok, 1)
            a.wait_ge(wide_ok, 1)
            with a.Fori(0, B) as b:
                def split_head(hi, bank, c, sig_mm, n_mm, sig_hi):
                    a.wait_ge(sig_mm.sem, sig_mm.at(b, n_mm))
                    up(sig_hi, a.activation(hi[:, c * CH:(c + 1) * CH], ps[:, bank, :], ACT.Copy))

                a.wait_ge(g2_ok.sem, g2_ok.at(b, 0))
                for c in range(NCH):
                    a.wait_ge(u_mm.sem, u_mm.at(b, c + 1))
                    up(u_ok, a.activation(uaug[:, c * TPC:(c + 1) * TPC, 0:D],
                                          ps[:, 4 + c, :].rearrange("p (t d) -> p t d", d=D), ACT.Copy))

                def silu_units(c):
                    for m in range(KM):
                        u = c * KM + m
                        a.wait_ge(l1_mm.sem, l1_mm.at(b, 2 * u + 1))
                        n_ = u
                        if n_ >= 3:
                            a.wait_ge(hid_lo.sem, hid_lo.at(b, n_ - 2))
                        up(l1_act, a.activation(act32[n_ % 3], ps[:, L1_BANKS[c][m % 2], :], ACT.Silu, scale=col("w1s", m)))

                def gelu_units(first, first_hid, name, banks):
                    for m in range(KM):
                        n_ = first_hid + m
                        a.wait_ge(h_mm.sem, h_mm.at(b, first + m + 1))
                        a.wait_ge(hid_lo.sem, hid_lo.at(b, n_ - 2))
                        up(h_act, a.activation(act32[n_ % 3], ps[:, banks[m], :], ACT.Gelu, scale=col(name, m)))

                def silu_g(c):
                    a.wait_ge(w3_mm.sem, w3_mm.at(b, c + 1))
                    up(w3_act, a.activation(gT[:, c * CH:(c + 1) * CH], ps[:, W3_BANKS[c], :], ACT.Silu, scale=col("w3s")))

                silu_units(0)
                a.wait_ge(fin_ok.sem, fin_ok.at(b, 0))
                a.wait_ge(stored.sem, stored.at(b, 0))
                for n_ in range(2 * NT):
                    h, jt = n_ // NT, n_ % NT
                    a.wait_ge(sc_mm.sem, sc_mm.at(b, n_ + 1))
                    up(sc_exp, a.activation(big[:, h, jt // 2, (jt % 2) * CH:(jt % 2 + 1) * CH],
                                            ps[:, SC_BANKS[n_ % 4], :], ACT.Exp))
                silu_units(1)
                for c in range(NCH):
                    gelu_units(c * KM, 8 + c * KM, "h1s", H_BANKS[c])
                gelu_units(8, 16, "h2s", H_BANKS[0])
                silu_g(0)
                gelu_units(12, 20, "h2s", H_BANKS[1])
                split_head(xt_hi, T_BANKS[0], 0, xT_mm, 1, x_hi)
                silu_g(1)

                def q_units(c):
                    for m in range(KM):
                        u = c * KM + m
                        a.wait_ge(qk_mm.sem, qk_mm.at(b, 2 * u + 1))
                        up(q_copy, a.activation(q1[:, m, c * CH:(c + 1) * CH], ps[:, 2 * (u % 3), :], ACT.Identity,
                                                bias=col("bq", m)))

                a.wait_ge(gnat_mm.sem, gnat_mm.at(b, 1))
                q_units(0)
                a.wait_ge(gnat_mm.sem, gnat_mm.at(b, 2))
                split_head(xt_hi, T_BANKS[1], 1, xT_mm, 2, x_hi)
                q_units(1)
                for c in range(NCH):
                    a.wait_ge(hsT_mm.sem, hsT_mm.at(b, c + 1))
                    up(hsT_in, a.activation(xn[:, c * CH:(c + 1) * CH], ps[:, 6 + c, :], ACT.Copy))
                for i in range(4):
                    j, c = i // 2, i % 2
                    a.wait_ge(mq_mm.sem, mq_mm.at(b, i + 1))
                    up(mq_hi, a.activation(spl[:, 2 * j, c * CH:(c + 1) * CH], ps[:, MQ_BANKS[i], :], ACT.Identity,
                                           bias=col(("mbq", "mbk")[j])))
                    if i == 1:
                        a.wait_ge(hs_sub.sem, hs_sub.at(b, 1))
                        up(hs_exp, a.activation(sm[:, 2, :], sm[:, 1, :], ACT.Exp, scale=HD1 ** -0.5))
                for u in range(NCH * KM):
                    c, m = u // KM, u % KM
                    a.wait_ge(v_mm.sem, v_mm.at(b, u + 1))
                    up(v_copy, a.activation(v1[:, m, c * CH:(c + 1) * CH], ps[:, u % 2, :], ACT.Identity,
                                            bias=decay[:, 2 * KM + m:2 * KM + m + 1], scale=decay[:, KM + m:KM + m + 1]))
                    g4, j = u // 2, u % 2
                    a.wait_ge(stk_mm.sem, stk_mm.at(b, u + 1))
                    dst = (q_st, k_st)[j][:, g4, :].rearrange("p (h n) -> p h n", n=CH)
                    src = ps[:, STK_BANKS[j]:STK_BANKS[j] + 2, :]
                    if j == 0:
                        up(stk_ok, a.activation(dst, src, ACT.Copy))
                    else:
                        up(stk_ok, a.activation(dst, src, ACT.Identity, bias=col("row24")))
                    if u >= 2:
                        a.wait_ge(z_ok.sem, z_ok.at(b, u - 1))
                    up(aug_ok, a.activation(xn[:, (u % 2) * CH:(u % 2 + 1) * CH], q1[:, m, c * CH:(c + 1) * CH], ACT.Sigmoid,
                                            scale=col("aug", m)))
                a.wait_ge(bnd_ok.sem, bnd_ok.at(b, 1))
                for u in range(UNITS):
                    g4, jt, g = u // (NT * GH), (u // GH) % NT, u % GH
                    a.wait_ge(ms_mm.sem, ms_mm.at(b, u + 1))
                    if u == 0:
                        a.wait_ge(qs_ok.sem, qs_ok.at(b, 8))
                    if u >= 2 * GH:
                        a.wait_ge(mp_mm.sem, mp_mm.at(b, 2 * (u // GH - 1)))
                    pr = (0, 2, 6)[u % 3]
                    h = g4 * GH + g
                    up(ms_exp, a.activation(prob[:, jt % 2, g, :].rearrange("p (h n) -> p h n", n=CH), ps[:, pr:pr + 2, :],
                                            ACT.Exp, bias=bias_m[:, h:h + 1], scale=HDM ** -0.5))
                    if u == UNITS - 2:
                        a.wait_ge(cT_mm.sem, cT_mm.at(b, 1))
                        up(cT_ok, a.activation(ct[:, :], ps[0:NT * E, 6, 0:P], ACT.Copy))
                    if u == G_EXP_AT:
                        a.wait_ge(g_sub.sem, g_sub.at(b, 1))
                        up(g_exp, a.activation(sm[:, 2, :], sm[:, 1, :], ACT.Exp))
                a.wait_ge(mp_mm.sem, mp_mm.at(b, NG * NT * 2 - 2))
                a.wait_ge(eb_mm.sem, eb_mm.at(b, 1))
                up(eb_ok, a.activation(big[:, 0, 3, :].rearrange("p (h n) -> p h n", n=CH), ps[:, 6:8, :], ACT.Copy))
                a.wait_ge(stats1_ok.sem, stats1_ok.at(b, 2))
                a.wait_ge(mp_mm.sem, mp_mm.at(b, NG * NT * 2))
                normalise_next(xn0_ok.sem)
                xn0_ok.given += 1
                def silu_out(c):
                    a.wait_ge(sum_ok[c].sem, sum_ok[c].at(b, 1))
                    up(g2_ok, a.activation(big[:, 0, 1, c * CH:(c + 1) * CH], wk[:, S + c * CH:S + (c + 1) * CH], ACT.Silu))

                for t in range(NT):
                    a.wait_ge(ex_mm.sem, ex_mm.at(b, t + 1))
                    if t >= 2:
                        a.wait_ge(pe_ok.sem, pe_ok.at(b, t - 1))
                    for i in range(EXA):
                        e = E - EXA + i
                        ins = a.activation(scaled[:, t % 2, i, :], ps[:, EX_BANKS[t % 3] + e // 4, (e % 4) * D:(e % 4 + 1) * D],
                                           ACT.Copy, scale=sm[:, 11, t * E + e:t * E + e + 1])
                    up(xs_ok, ins)
                for i in range(NCH):
                    split_head(xt_hi, 4 + i, i, xT_mm, 3 + i, x_hi)
                for i in range(NCH):
                    split_head(spl[:, 0], i, i, r_mm, 1 + i, r_hi)
                silu_out(0)
                silu_out(1)

        @block.tensor
        def _(t_):
            def mm(out_, lhsT, rhs, start, stop, **kw):
                return t_.matmul(out_, lhsT, rhs, start=start, stop=stop, **kw)

            def split3(out_, l_hi, l_lo, r_hi_, r_lo_, start=True, stop=True):
                mm(out_, l_hi, r_hi_, start, False)
                mm(out_, l_hi, r_lo_, False, False)
                return mm(out_, l_lo, r_hi_, False, stop)

            def with_high(out_, l_hi, l_lo, r_hi_):
                mm(out_, l_hi, r_hi_, True, False)
                mm(out_, l_lo, r_hi_, False, False)

            def full2(out_, w, r_hi_, r_lo_, start=True, stop=True):
                mm(out_, w, r_hi_.bitcast(F32), start, False)
                return mm(out_, w, r_lo_.bitcast(F32), False, stop)

            def transposes(src, bank, c):
                for i in range(TPC):
                    ins = t_.transpose(ps[:, bank, i * P:(i + 1) * P], src[:, c * TPC + i, :], ident)
                ins.then_inc(xT_mm.sem, 1)

            t_.wait_ge(aw_in, 16)
            waT, wkk, wq, wv, wbT = (xn[:, i * D:(i + 1) * D] for i in range(5))
            mm(ps[:, 0, 0:D], waT, wkk, True, True).then_inc(setup_p, 1)
            mm(ps[:, 1, D:2 * D], wv, wbT, True, True)
            t_.wait_ge(setup_v, marks["Wa Wk"])
            mm(ps[:, 1, 0:D], wq, xn[:, 5 * D:6 * D], True, True).then_inc(setup_p, 1)
            t_.wait_ge(small_in, 48)
            t_.wait_ge(xn0_ok.sem, 1)
            for c in range(NCH):
                transposes(xn0, 4 + c, c)
            t_.wait_ge(setup_v, marks["G and H"])
            for c in range(NCH):
                t_.wait_ge(x_lo.sem, c + 1)
                sl = slice(c * CH, (c + 1) * CH)
                split3(ps[:, c, :], gh_hi[:, 0:D], gh_lo[:, 0:D], xt_hi[:, sl], xt_lo[:, sl]).then_inc(r_mm.sem, 1)
            t_.wait_ge(setup_v, marks["flags"])
            mm(ps[:, 2, 0:1], ones, flags[:, 0:1], True, True).then_inc(setup_p, 1)
            t_.wait_ge(wide_ok, 1)
            mm(ps[:, 3, 0:1], ones, flags[:, 0:1], True, True)
            wide = t_.value_load(iflag[0:1, 0:1], min_val=0, max_val=1)

            with t_.Fori(0, B) as b:
                def xT(c):
                    return xt_hi[:, c * CH:(c + 1) * CH], xt_lo[:, c * CH:(c + 1) * CH]

                def tok(t):
                    return xt_hi[:, t * P:(t + 1) * P], xt_lo[:, t * P:(t + 1) * P]

                def lwp(at, n=P):
                    return lw_hi[:, at:at + n], lw_lo[:, at:at + n]

                t_.wait_ge(ex_ok.sem, ex_ok.at(b, 0))
                def row_scores(t):
                    bank = MAX_BANKS[t % 2]
                    if t >= 2:
                        t_.wait_ge(row_max.sem, row_max.at(b, t - 1))
                    for c in range(NCH):
                        ins = mm(ps[:, bank + c, :], spl[:, 0, t * P:(t + 1) * P], xT(c)[0], True, True)
                    ins.then_inc(max_mm.sem, 1)

                t_.wait_ge(r_hi.sem, r_hi.at(b, 0))
                row_scores(0)
                row_scores(1)
                for t in range(NT):
                    ins = split3(ps[:, 4 + t // TPC, (t % TPC) * D:(t % TPC + 1) * D], *tok(t), gh_hi[:, D:2 * D], gh_lo[:, D:2 * D])
                    if t % TPC == TPC - 1:
                        up(u_mm, ins)
                    if t % 2 == 1:
                        row_scores(2 + t // 2)

                def block_wait(n_):
                    s_ = wblk_in[n_ % 2]
                    t_.wait_ge(s_.sem, s_.at(b, 16 * (n_ // 2 + 1)))

                def l1_unit(c, m, general):
                    if m >= 2:
                        t_.wait_ge(hid_hi.sem, hid_hi.at(b, KM * c + m - 1))
                    if general and m == 0:
                        block_wait(2 * c)
                        block_wait(2 * c + 1)
                    for i, base in enumerate((FW1, FW2)):
                        bank = ps[:, L1_BANKS[c][m % 2] + i, :]
                        w = slice(base + m * P, base + (m + 1) * P)
                        if general:
                            ins = full2(bank, wblk[:, i, m * P:(m + 1) * P], *xT(c))
                        else:
                            mm(bank, fw_sb[:, w], xT(c)[0], True, False)
                            ins = mm(bank, fw_sb[:, w], xT(c)[1], False, True)
                        ins.then_inc(l1_mm.sem, 1)
                    if general and m == KM - 1:
                        t_.drain().then_inc(wblk_used.sem, 2)

                def dense(base, width, buf, banks, first_hid, general, block, signal, mcount, between=None):
                    for kk in range(KM):
                        t_.wait_ge(hid_lo.sem, hid_lo.at(b, first_hid + kk + 1))
                        if general and (mcount > 1 or kk == 0):
                            block_wait(block + kk)
                        for m in range(mcount):
                            w = slice(base + kk * width + m * P, base + kk * width + (m + 1) * P)
                            o_ = ps[:, banks[m], :]
                            h_hi, h_lo = hidden(buf, 0, kk), hidden(buf, 1, kk)
                            if general:
                                at = kk * D if mcount == 1 else m * P
                                ins = full2(o_, wblk[:, (block + kk * (mcount > 1)) % 2, at:at + P], h_hi, h_lo, kk == 0, kk == KM - 1)
                            else:
                                mm(o_, fw_sb[:, w], h_hi, kk == 0, False)
                                ins = mm(o_, fw_sb[:, w], h_lo, False, kk == KM - 1)
                            if kk == KM - 1:
                                ins.then_inc(signal.sem, 1)
                        if general and (mcount > 1 or kk == KM - 1):
                            t_.drain().then_inc(wblk_used.sem, 1)
                        if between and kk == 0:
                            between()

                def score_products(n_):
                    h, jt = n_ // NT, n_ % NT
                    sl = slice(h * CH, (h + 1) * CH)
                    split3(ps[:, SC_BANKS[n_ % 4], :], *tok(jt), spl[:, 0, sl], spl[:, 1, sl], True, False)

                def first_layer(general):
                    t_.wait_ge(r_lo.sem, r_lo.at(b, 0))
                    l1_unit(0, 0, general)
                    row_scores(6)
                    t_.wait_ge(u_ok.sem, u_ok.at(b, 2))
                    l1_unit(0, 1, general)
                    row_scores(7)
                    t_.wait_ge(row_max.sem, row_max.at(b, NT))
                    t_.transpose(ps[0:NT, 6, 0:P], mx[:, :], ident).then_inc(maxT.sem, 1)
                    score_products(0)
                    score_products(1)
                    l1_unit(0, 2, general)
                    l1_unit(0, 3, general)

                with t_.If(wide > 0):
                    first_layer(True)
                with t_.Else():
                    first_layer(False)
                t_.wait_ge(neg_ok.sem, neg_ok.at(b, 1))
                t_.wait_ge(negrow_in.sem, negrow_in.at(b, 16))
                for n_ in range(2 * NT):
                    if n_ >= 4:
                        t_.wait_ge(sc_exp.sem, sc_exp.at(b, n_ - 3))
                    if n_ >= 2:
                        score_products(n_)
                    h = n_ // NT
                    up(sc_mm, mm(ps[:, SC_BANKS[n_ % 4], :], ones_r[:, :], negrow[:, h * CH:(h + 1) * CH], False, True))

                def g_transposes(c):
                    t_.wait_ge(w3_act.sem, w3_act.at(b, c + 1))
                    for i in range(TPC):
                        ins = t_.transpose(ps[:, GT_BANKS[c], i * P:(i + 1) * P], gT[:, c * CH + i * P:c * CH + (i + 1) * P], ident)
                    ins.then_inc(gnat_mm.sem, 1)

                def attend(t):
                    if t >= 2:
                        t_.wait_ge(pv_norm.sem, pv_norm.at(b, t - 1))
                    h = t // TPC
                    if t % TPC == 0:
                        t_.wait_ge(sc_exp.sem, sc_exp.at(b, (h + 1) * NT))
                    for jt in range(NT):
                        at = (jt % 2) * CH + (t % TPC) * P
                        ins = mm(ps[:, PV_BANKS[t], 0:D + 1], big[:, h, jt // 2, at:at + P], uaug[:, jt, :], jt == 0, jt == NT - 1)
                    ins.then_inc(pv_mm.sem, 1)

                def mlp_rest(general):
                    t_.wait_ge(hid_hi.sem, hid_hi.at(b, KM))
                    for m in range(KM):
                        attend(m)
                        if m == 1:
                            t_.wait_ge(sc_exp.sem, sc_exp.at(b, 2 * NT))
                        l1_unit(1, m, general)
                    t_.wait_ge(hid_hi.sem, hid_hi.at(b, 2 * KM - 1))
                    dense(FH1, HID, 0, H_BANKS[0], 0, general, 4, h_mm, KM)
                    t_.wait_ge(pv_norm.sem, pv_norm.at(b, KM))
                    t_.wait_ge(hid_hi.sem, hid_hi.at(b, 2 * KM))
                    dense(FH1, HID, 2, H_BANKS[1], 4, general, 8, h_mm, KM)
                    t_.wait_ge(h_act.sem, h_act.at(b, 4))
                    dense(FH2, HID, 1, H_BANKS[0], 8, general, 12, h_mm, KM)
                    t_.wait_ge(h_act.sem, h_act.at(b, 8))
                    attend(4)
                    attend(5)
                    dense(FW3, D, 2, W3_BANKS[0:1], 16, general, 16, w3_mm, 1)
                    t_.wait_ge(pv_norm.sem, pv_norm.at(b, 6))
                    dense(FH2, HID, 0, H_BANKS[1], 12, general, 17, h_mm, KM, between=lambda: g_transposes(0))
                    attend(6)
                    attend(7)
                    t_.wait_ge(ln_ok.sem, ln_ok.at(b, 1))
                    t_.wait_ge(h_act.sem, h_act.at(b, 14))
                    transposes(xnv, T_BANKS[0], 0)
                    dense(FW3, D, 1, W3_BANKS[1:2], 20, general, 21, w3_mm, 1)

                with t_.If(wide > 0):
                    mlp_rest(True)
                with t_.Else():
                    mlp_rest(False)
                t_.wait_ge(lw_ok, 1)
                for u in range(NCH * KM):
                    c, m = u // KM, u % KM
                    if u == 1:
                        t_.wait_ge(pv_norm.sem, pv_norm.at(b, NT))
                    if u == 2:
                        g_transposes(1)
                    if u == KM:
                        t_.wait_ge(ln_ok.sem, ln_ok.at(b, 2))
                        transposes(xnv, T_BANKS[1], 1)
                    if u >= 3:
                        t_.wait_ge(prod_ok.sem, prod_ok.at(b, u - 2))
                    if m == 0:
                        t_.wait_ge(x_hi.sem, x_hi.at(b, 1 + c))
                    for i, base in enumerate((LQ, LK)):
                        with_high(ps[:, 2 * (u % 3) + i, :], *lwp(base + m * P), xT(c)[0])
                    if m == 0:
                        t_.wait_ge(x_lo.sem, x_lo.at(b, 1 + c))
                    for i, base in enumerate((LQ, LK)):
                        up(qk_mm, mm(ps[:, 2 * (u % 3) + i, :], lwp(base + m * P)[0], xT(c)[1], False, True))
                for s_ in (wblk_used, pv_mm, l1_mm, h_mm, w3_mm, gnat_mm, maxT, max_mm):
                    s_.given = s_.per

                def head_scores(c):
                    for m in range(KM):
                        t_.wait_ge(prod_ok.sem, prod_ok.at(b, KM * c + m + 1))
                        ins = mm(ps[QUAD * m:QUAD * (m + 1), 6 + c, :], cst_sb[:, CHD:CHD + QUAD], prods[c * KM + m], True, True)
                    up(hsT_mm, ins)

                head_scores(0)
                head_scores(1)
                for i in range(4):
                    j, c = i // 2, i % 2
                    up(mq_mm, split3(ps[:, MQ_BANKS[i], :], *lwp(LM + j * D), *xT(c)))
                for c in range(NCH):
                    t_.wait_ge(hsT_in.sem, hsT_in.at(b, c + 1))
                    for i in range(TPC):
                        ins = t_.transpose(ps[:, 6 + c, i * P:(i + 1) * P], xn[:, (c * TPC + i) * P:(c * TPC + i + 1) * P], ident)
                    up(hs_mm, ins)
                for t in range(NT):
                    if t == 6:
                        t_.wait_ge(hs_sub.sem, hs_sub.at(b, 1))
                    at = (t % 3) * (D + E)
                    ins = split3(ps[:, MV_BANKS[t // 3], at:at + D + E], *tok(t), *lwp(LM + 2 * D, D + E))
                    if t in (2, 5, 7):
                        up(mv_mm, ins)
                attn3 = sm[:, 5, :].rearrange("p (t h) -> p t h", h=H1)

                def spread(u):
                    c, m = u // KM, u % KM
                    if u >= 2:
                        t_.wait_ge(u1_ok.sem, u1_ok.at(b, u - 1))
                    for i in range(TPC):
                        for j in range(P // HD1):
                            w = attn3[:, c * TPC + i, 2 * m + j:2 * m + j + 1].broadcast_to([P, HD1])
                            ins = mm(ps[HD1 * j:HD1 * (j + 1), 2 + u % 2, i * P:(i + 1) * P], w, ident, True, True)
                    up(bc_mm, ins)

                def stack(i):
                    g4, j = i // 2, i % 2
                    if i >= 2:
                        t_.wait_ge(stk_ok.sem, stk_ok.at(b, i - 1))
                    rg = slice(QUAD * g4, QUAD * (g4 + 1))
                    for c in range(NCH):
                        bank = ps[:, STK_BANKS[j] + c, :]
                        mm(bank, sel_r[rg, 2 * j * P:(2 * j + 1) * P], spl[rg, 2 * j, c * CH:(c + 1) * CH], True, False)
                        ins = mm(bank, sel_r[rg, (2 * j + 1) * P:(2 * j + 2) * P], spl[rg, 2 * j + 1, c * CH:(c + 1) * CH], False, True)
                    up(stk_mm, ins)

                def out_projection(c):
                    t_.wait_ge(z_ok.sem, z_ok.at(b, KM * (c + 1)))
                    for i in range(TPC):
                        for m in range(KM):
                            ins = mm(ps[:, 4 + c, i * D:(i + 1) * D], wk[:, m * S + c * CH + i * P:m * S + c * CH + (i + 1) * P],
                                     wo_sb[:, m * D:(m + 1) * D], m == 0, m == KM - 1)
                    up(o_mm, ins)

                def v_unit(u):
                    c, m = u // KM, u % KM
                    if u >= 2:
                        t_.wait_ge(v_copy.sem, v_copy.at(b, u - 1))
                    up(v_mm, split3(ps[:, u % 2, :], *lwp(LV + m * P), *xT(c)))

                t_.wait_ge(mq_lo.sem, mq_lo.at(b, 4))
                v_unit(0)
                stack(0)
                t_.wait_ge(attn_ok.sem, attn_ok.at(b, 1))
                t_.wait_ge(mv_ok.sem, mv_ok.at(b, 2))
                spread(0)
                v_unit(1)
                t_.wait_ge(mv_ok.sem, mv_ok.at(b, 3))
                t_.wait_ge(bnd_in.sem, bnd_in.at(b, 1))
                up(bnd_mm, mm(ps[:, 6, 0:HM], ones, sm[:, 7, 0:HM], True, True))
                t_.wait_ge(bnd_ok.sem, bnd_ok.at(b, 1))
                for u in range(1, NCH * KM):
                    stack(u)
                    spread(u)
                    if u + 1 < NCH * KM:
                        v_unit(u + 1)
                t_.wait_ge(stk_ok.sem, stk_ok.at(b, 2 * NG - 1))
                t_.wait_ge(wo_in, 16)
                out_projection(0)
                t_.wait_ge(stk_ok.sem, stk_ok.at(b, 2 * NG))
                t_.wait_ge(u1_ok.sem, u1_ok.at(b, 8))
                mm(ps[:, 6, 0:1], ones, ones[:, 0:1], True, True)
                need_max = t_.value_load(iflag[0:1, 1:2], min_val=0, max_val=1)
                with t_.If(need_max > 0):
                    for gt in range(NG * NT):
                        g4, t = gt // NT, gt % NT
                        for g in range(GH):
                            n_ = gt * GH + g
                            if n_ >= 2:
                                t_.wait_ge(gen_mx.sem, gen_mx.at(b, n_ - 1))
                            rg = slice(QUAD * g, QUAD * g + 3 * HDM)
                            for c in range(NCH):
                                ins = mm(ps[:, (0 if n_ % 2 == 0 else 2) + c, :], q_st[rg, g4, t * P:(t + 1) * P],
                                         k_st[rg, g4, c * CH:(c + 1) * CH], True, True)
                            ins.then_inc(gen_mm.sem, 1)
                        t_.wait_ge(gen_mx.sem, gen_mx.at(b, (gt + 1) * GH))
                        if gt >= 2:
                            t_.wait_ge(gen_add.sem, gen_add.at(b, gt - 1))
                        t_.transpose(ps[:, 6 + gt % 2, 0:P], mbuf[:, :], ident).then_inc(gen_T.sem, 1)
                with t_.Else():
                    t_.sem_inc(gen_mm.sem, gen_mm.per)
                    t_.sem_inc(gen_T.sem, gen_T.per)
                gen_mm.given, gen_T.given = gen_mm.per, gen_T.per
                t_.wait_ge(gen_add.sem, gen_add.at(b, NG * NT))

                def m_scores(u):
                    g4, jt, g = u // (NT * GH), (u // GH) % NT, u % GH
                    if u >= 3:
                        t_.wait_ge(ms_exp.sem, ms_exp.at(b, u - 2))
                    if jt == 0:
                        t_.wait_ge(kz_ok.sem, kz_ok.at(b, g4 * GH + g + 1))
                    for c in range(NCH):
                        ins = mm(ps[:, (0, 2, 6)[u % 3] + c, :], kz[:, g, jt * P:(jt + 1) * P],
                                 q_st[:, g4, c * CH:(c + 1) * CH], True, True)
                    up(ms_mm, ins)

                def m_values(gj, c):
                    g4, jt = gj // NT, gj % NT
                    if c == 0:
                        t_.wait_ge(ms_exp.sem, ms_exp.at(b, GH * (gj + 1)))
                        if gj == 0:
                            t_.wait_ge(o_ok.sem, o_ok.at(b, 2))
                    if jt == 0 and g4:
                        t_.wait_ge(att_ok.sem, att_ok.at(b, 2 * g4 - 1 + c))
                    for g in range(GH):
                        ins = mm(ps[QUAD * g:QUAD * (g + 1), 4 + c, :], vaug[:, (jt * HM + g4 * GH + g) * (HDM + 1):(jt * HM + g4 * GH + g) * (HDM + 1) + QUAD],
                                 prob[:, jt % 2, g, c * CH:(c + 1) * CH], jt == 0, jt == NT - 1)
                    up(mp_mm, ins)

                def expert_unit(t):
                    if t == 1:
                        t_.wait_ge(eb_ok.sem, eb_ok.at(b, 1))
                    if t >= 3:
                        t_.wait_ge(ex_ok.sem, ex_ok.at(b, t - 2))
                        t_.wait_ge(xs_ok.sem, xs_ok.at(b, t - 2))
                    for c in range(2):
                        ins = split3(ps[:, EX_BANKS[t % 3] + c, :], *tok(t), *lwp(LE + c * CH, CH))
                    up(ex_mm, ins)

                def to_natural(g4, c):
                    t_.wait_ge(oT_ok.sem, oT_ok.at(b, 2 * g4 + c + 1))
                    for i in range(TPC):
                        t = c * TPC + i
                        ins = t_.transpose(ps[:, 4 + c, i * P:(i + 1) * P], wk[:, t * P:(t + 1) * P], ident)
                    up(oN_mm, ins)

                for gj in range(NG * NT):
                    for g in range(GH):
                        m_scores(gj * GH + g)
                        if gj * GH + g == 2:
                            out_projection(1)
                        if gj % NT == 1 and gj > 1:
                            if g < 2:
                                to_natural(gj // NT - 1, g)
                            else:
                                m_values(gj - 1, g - 2)
                        elif gj and g in (1, 3):
                            m_values(gj - 1, g // 2)
                t_.wait_ge(comb_ok.sem, comb_ok.at(b, 1))
                t_.wait_ge(ms_exp.sem, ms_exp.at(b, UNITS - 2))
                mm(ps[:, 6, 0:1], ones, ones[:, 0:1], True, True)
                up(cT_mm, t_.transpose(ps[0:NT * E, 6, 0:P], sm[:, 11, :], ident))
                t_.wait_ge(ms_exp.sem, ms_exp.at(b, UNITS - 1))
                expert_unit(0)
                t_.wait_ge(cT_ok.sem, cT_ok.at(b, 1))
                t_.wait_ge(bexp_in, 16 * NT)
                for c in range(NCH):
                    ins = mm(ps[:, 6 + c, :], ct[:, :], bexp_sb[:, c * CH:(c + 1) * CH], True, True)
                up(eb_mm, ins)
                m_values(NG * NT - 1, 0)
                m_values(NG * NT - 1, 1)
                expert_unit(1)
                to_natural(NG - 1, 0)
                to_natural(NG - 1, 1)
                for t in range(2, NT):
                    expert_unit(t)
                t_.wait_ge(xn0_ok.sem, xn0_ok.at(b, 2))
                for c in range(NCH):
                    transposes(xn0, 4 + c, c)
                xT_mm.given = xT_mm.per
                for c in range(NCH):
                    t_.wait_ge(x_hi.sem, x_hi.at(b, 3 + c))
                    if c == 0:
                        t_.wait_ge(ex_ok.sem, ex_ok.at(b, NT - 1))
                        t_.wait_ge(xs_ok.sem, xs_ok.at(b, NT - 1))
                    with_high(ps[:, c, :], gh_hi[:, 0:D], gh_lo[:, 0:D], xT(c)[0])
                for c in range(NCH):
                    t_.wait_ge(x_lo.sem, x_lo.at(b, 3 + c))
                    up(r_mm, mm(ps[:, c, :], gh_hi[:, 0:D], xT(c)[1], False, True))

        for s_ in [o for o in list(locals().values()) if isinstance(o, Signal)]:
            s_.check()


def kernel(**inputs):
    import numpy as np
    import concourse.bacc as bacc
    from concourse.bass_utils import run_bass_kernel_spmd

    i = {n: np.asarray(a) for n, a in inputs.items()}

    def blocks(wT):
        k_, n_ = wT.shape
        return np.ascontiguousarray(wT.reshape(k_ // P, P, n_).transpose(1, 0, 2)).reshape(P, -1)

    def column(vec):
        return np.ascontiguousarray(vec.reshape(-1, P).T)

    fw = np.concatenate([blocks(i["L0_ffn_" + n].T) for n in ("w1_w", "w2_w", "h1_w", "h2_w", "w3_w")], 1)
    we = np.ascontiguousarray(i["L1_ffn_W_experts"].transpose(1, 0, 2)).reshape(D, E * D)
    lw = np.concatenate([i["L1_attn_Wq"], i["L1_attn_Wk"], i["L1_attn_Wv"], i["L1_ffn_W_qkv"], i["L1_ffn_W_gate"], we], 1)
    aw = np.concatenate([i["L0_attn_Wa"].T, i["L0_attn_Wk"], i["L0_attn_Wq"], i["L0_attn_Wv"], i["L0_attn_Wb"].T], 1)
    row24 = np.zeros((P, 1), np.float32)
    row24[3 * HDM::QUAD] = 1.0
    b_qkv = i["L1_ffn_b_qkv"]
    cols = np.concatenate(
        [column(i["L0_ffn_" + n]) for n in ("w1_s", "w2_s", "h1_s", "h2_s", "w3_s")]
        + [column(i["L1_attn_" + n]) for n in ("bq", "bk", "bv")]
        + [column(i["L1_attn_aug_param"]), column(i["L1_attn_alpha"])]
        + [column(b_qkv[0:D]), column(b_qkv[D:2 * D]), row24], 1)
    rows = np.concatenate([i["L1_attn_bo"], i["L1_attn_ln_scale"], i["L1_attn_ln_bias"], b_qkv[2 * D:], i["L1_ffn_b_gate"]])
    rows = np.ascontiguousarray(np.broadcast_to(rows[None, :], (P, rows.shape[0])))
    heads1 = np.zeros((P, QUAD), np.float32)
    for p in range(P):
        heads1[p, p // HD1] = 1.0
    headsm = np.zeros((P, HM), np.float32)
    sel = np.zeros((4, P, P), np.float32)
    for p in range(P):
        headsm[p, p // HDM] = 1.0
        g, d = (p % QUAD) // HDM, p % HDM
        for which, reps in enumerate(((0, 2), (1,), (0, 1), (2,))):
            for r in reps:
                sel[which, p, QUAD * g + HDM * r + d] = 1.0
    mask = np.ones((P, NT, E), np.float32)
    mask[:, :, 0] = 0.0
    cst = np.concatenate([np.eye(P, dtype=np.float32), np.ones((P, P), np.float32), heads1, headsm,
                          sel.transpose(1, 0, 2).reshape(P, -1), mask.reshape(P, -1)], 1)
    x5 = np.concatenate([i["L0_attn_x"], i["L0_attn_x"][0:1]])
    arrays = {"in_x": x5, "in_fw": fw, "in_lw": lw, "in_aw": aw, "in_wo": blocks(i["L1_attn_Wo"]),
              "in_cst": cst, "in_cols": cols, "in_rows": rows, "in_bexp": i["L1_ffn_b_experts"]}
    arrays = {n: np.ascontiguousarray(a) for n, a in arrays.items()}

    nc = bacc.Bacc("TRN2", target_bir_lowering=False, num_devices=1)
    args = [nc.dram_tensor(n, a.shape, mybir.dt.from_np(a.dtype), kind="ExternalInput").ap() for n, a in arrays.items()]
    args.append(nc.dram_tensor("out_0", (B, S, D), F32, kind="ExternalOutput").ap())
    build_program(nc, *args)
    r = run_bass_kernel_spmd(nc, [arrays], core_ids=[0])
    return r.results[0]["out_0"]
```
